# Optimizing a Trainium2 kernel written in Bass

```python
import numpy as np
import jax
import jax.numpy as jnp

def _softmax(x, axis=-1):
    return jax.nn.softmax(x, axis=axis)

def _gelu(x):
    return jax.nn.gelu(x, approximate=True)

def _silu(x):
    return jax.nn.silu(x)

def _sigmoid(x):
    return jax.nn.sigmoid(x)

def _layernorm(x, axis=-1, eps=1e-05):
    m = jnp.mean(x, axis=axis, keepdims=True)
    v = jnp.var(x, axis=axis, keepdims=True)
    return (x - m) / jnp.sqrt(v + eps)

def _scatter_add(tgt, idx, src, axis=0):
    return tgt.at[idx].add(src)

def _segment_sum(src, seg, n):
    return jax.ops.segment_sum(src, seg, n)
kernel_name = 'mk_gnn_ffn_d1_gnn_r8_6213b2'

def setup_inputs(seed: int=0):
    np.random.seed(seed)
    _w = jnp.asarray

    def _rec_inputs():
        import jax
        import jax.numpy as jnp
        _gk = jax.random.key(seed)
        x = -0.0002117 + 1 * jax.random.normal(jax.random.fold_in(_gk, 1), (12500, 256), jnp.float32)
        _s = jax.random.randint(jax.random.fold_in(_gk, 2), (100000,), 0, 12500, jnp.int32)
        _d = jax.random.randint(jax.random.fold_in(_gk, 3), (100000,), 0, 12500, jnp.int32)
        _loop = jnp.arange(12500, dtype=jnp.int32)
        src = jnp.concatenate([_s, _d, _loop])
        dst = jnp.concatenate([_d, _s, _loop])
        _o = jnp.argsort(dst, stable=True)
        src = src[_o]
        dst = dst[_o]
        edge_weight = jax.random.uniform(jax.random.fold_in(_gk, 12), (212500,), jnp.float32, 0.0, 1)
        return (x, src, dst, edge_weight)
    x, src, dst, edge_weight = _rec_inputs()

    def _L0_gnn_setup():
        import jax, jax.numpy as jnp
        import numpy as np
        N_NODES = 12500
        key = jax.random.key(seed)
        k = jax.random.split(key, 7)
        N, E, F_IN, F_OUT = (N_NODES, 400000, 256, 256)
        stdv = 1.0 / np.sqrt(F_OUT)
        return {'x': jax.random.normal(k[0], (N, F_IN), dtype=jnp.float32), 'edge_row': jax.random.randint(k[1], (E,), 0, N, dtype=jnp.int32), 'edge_col': jax.random.randint(k[2], (E,), 0, N, dtype=jnp.int32), 'edge_val': jax.random.uniform(k[3], (E,), dtype=jnp.float32), 'weight': jax.random.uniform(k[4], (F_IN, F_OUT), dtype=jnp.float32, minval=-stdv, maxval=stdv), 'learnable_diag': 0.01 * jax.random.normal(k[5], (F_IN,), dtype=jnp.float32), 'bias': jax.random.uniform(k[6], (F_OUT,), dtype=jnp.float32, minval=-stdv, maxval=stdv)}
    _L0_gnn_all = _L0_gnn_setup()
    _L0_gnn_in = {k: v for k, v in _L0_gnn_all.items() if k in ('weight', 'learnable_diag', 'bias')}
    del _L0_gnn_all

    def _L0_ffn_setup():
        import math
        import jax, jax.numpy as jnp
        import numpy as np
        CAPACITY_FACTOR = 1.25
        key = jax.random.key(seed)
        ks = jax.random.split(key, 5)
        B, L, D, F, E = (8, 1024, 256, 1024, 8)
        h = jax.random.normal(ks[0], (B, L, D), dtype=jnp.float32)
        gate_w = jax.random.normal(ks[1], (D, E), dtype=jnp.float32) * 0.02
        gate_b = jnp.zeros((E,), dtype=jnp.float32)
        w1 = jax.random.normal(ks[2], (E, D, F), dtype=jnp.float32) * (1.0 / math.sqrt(D))
        b1 = jnp.zeros((E, F), dtype=jnp.float32)
        w2 = jax.random.normal(ks[3], (E, F, D), dtype=jnp.float32) * (1.0 / math.sqrt(F))
        b2 = jnp.zeros((E, D), dtype=jnp.float32)
        return {'h': h, 'gate_w': gate_w, 'gate_b': gate_b, 'w1': w1, 'b1': b1, 'w2': w2, 'b2': b2}
    _L0_ffn_all = _L0_ffn_setup()
    _L0_ffn_in = {k: v for k, v in _L0_ffn_all.items() if k in ('gate_w', 'gate_b', 'w1', 'b1', 'w2', 'b2')}
    del _L0_ffn_all
    return {'x': x, 'src': src, 'dst': dst, 'edge_weight': edge_weight, 'L0_gnn_weight': _L0_gnn_in['weight'], 'L0_gnn_learnable_diag': _L0_gnn_in['learnable_diag'], 'L0_gnn_bias': _L0_gnn_in['bias'], 'L0_ffn_gate_w': _L0_ffn_in['gate_w'], 'L0_ffn_gate_b': _L0_ffn_in['gate_b'], 'L0_ffn_w1': _L0_ffn_in['w1'], 'L0_ffn_b1': _L0_ffn_in['b1'], 'L0_ffn_w2': _L0_ffn_in['w2'], 'L0_ffn_b2': _L0_ffn_in['b2']}

def reference(x, src, dst, edge_weight, L0_gnn_weight, L0_gnn_learnable_diag, L0_gnn_bias, L0_ffn_gate_w, L0_ffn_gate_b, L0_ffn_w1, L0_ffn_b1, L0_ffn_w2, L0_ffn_b2):
    import jax
    import jax.numpy as jnp

    def _L0_gnn_ref(x, edge_row, edge_col, edge_val, weight, learnable_diag, bias):
        import jax, jax.numpy as jnp
        import numpy as np
        N_NODES = 12500
        gathered = edge_val[:, None] * x[edge_col]
        e1 = jax.ops.segment_sum(gathered, edge_row, num_segments=N_NODES)
        e2 = e1 * (learnable_diag + 1.0)
        e4 = x - e2
        out = e4 @ weight + bias
        return out

    def _L0_ffn_ref(h, gate_w, gate_b, w1, b1, w2, b2):
        import math
        import jax, jax.numpy as jnp
        import numpy as np
        CAPACITY_FACTOR = 1.25
        B, L, D = h.shape
        E = gate_w.shape[1]
        T = B * L
        C = max(1, math.ceil(CAPACITY_FACTOR * T / E))
        x = h.reshape(T, D)
        logits = x @ gate_w + gate_b
        probs = jax.nn.softmax(logits, axis=-1)
        idx = jnp.argmax(probs, axis=-1)
        prb = jnp.take_along_axis(probs, idx[:, None], axis=1)[:, 0]
        one_hot = jax.nn.one_hot(idx, E, dtype=jnp.float32)
        pos = (jnp.cumsum(one_hot, axis=0) * one_hot).sum(-1).astype(jnp.int32) - 1
        kept = pos < C
        pos_safe = jnp.where(kept, pos, C)
        buf = jnp.zeros((E, C, D), dtype=h.dtype).at[idx, pos_safe].set(x, mode='drop')
        hmid = jax.nn.relu(jnp.einsum('ecd,edf->ecf', buf, w1) + b1[:, None, :])
        ybuf = jnp.einsum('ecf,efd->ecd', hmid, w2) + b2[:, None, :]
        pos_g = jnp.minimum(pos, C - 1)
        y_tok = ybuf[idx, pos_g] * (prb * kept)[:, None]
        y = y_tok.reshape(B, L, D)
        y = jnp.nan_to_num(y, nan=0.0, posinf=10000.0, neginf=-10000.0)
        return y
    x = x + _L0_gnn_ref(_layernorm(x, axis=-1), src, dst, edge_weight, L0_gnn_weight, L0_gnn_learnable_diag, L0_gnn_bias)
    x = x + _L0_ffn_ref(_layernorm(x, axis=-1)[None], L0_ffn_gate_w, L0_ffn_gate_b, L0_ffn_w1, L0_ffn_b1, L0_ffn_w2, L0_ffn_b2)[0]
    return x

_drawn_inputs = setup_inputs


def setup_inputs(seed=0):
    import zlib

    import numpy as np

    out = dict(_drawn_inputs(seed))
    spreads = {'L0_ffn_gate_b': (0.0, 0.1), 'L0_ffn_b1': (0.0, 0.8), 'L0_ffn_b2': (0.0, 0.724)}
    factors = {'L0_gnn_learnable_diag': 5.167}
    for name, (base, spread) in spreads.items():
        noise = np.random.default_rng([zlib.crc32(name.encode()), seed]).standard_normal(out[name].shape)
        drawn = base * np.exp(spread * noise) if base else spread * noise
        out[name] = jnp.asarray(drawn.astype(out[name].dtype))
    for name, factor in factors.items():
        out[name] = (out[name] * factor).astype(out[name].dtype)
    return out
```

```python
from contextlib import ExitStack

import concourse.bass as bass
from concourse import mybir

ALU = mybir.AluOpType
ACT = mybir.ActivationFunctionType
AX_X = mybir.AxisListType.X
F32 = mybir.dt.float32
BF16 = mybir.dt.bfloat16
I32 = mybir.dt.int32
U32 = mybir.dt.uint32

P = 128
EPS = 1e-5
COPIES = 4
GC = 4
BC = 8
TG = 7
HUGE = 3.4028234663852886e38


def gnn_moe_layer(nc, x, src, dst, edge_weight, gnn_w, gnn_diag, gnn_bias, gate_w, gate_b,
                  w1, b1, w2, b2, out):
    N, D = x.shape
    E = src.shape[0]
    NX, _, F = w1.shape
    C = max(1, -(-5 * N // (4 * NX)))
    KD = D // P
    KF = F // P

    EQ = -(-E // (P * P))
    EP = EQ * P
    NCH = P * EQ
    NGR = NCH // GC
    NB = NCH // BC
    assert NCH % (2 * BC) == 0
    EFULL = E // EP
    EREST = E - EFULL * EP
    assert 96 <= EFULL == P - 1 and EREST > 0

    NT = -(-N // P)
    NREST = N - (NT - 1) * P
    NG = NT // TG
    assert NG * TG == NT and NG % 2 == 0
    PAD_NODE = N
    DUMP = N + 1
    AR = (NT + 1) * P
    ZR = 11
    assert AR // P % ZR == 0 and DUMP + P <= AR

    TB = 4
    XT = -(-C // P)
    XB = -(-XT // TB)
    assert XT == XB * TB
    BDUMP = NX * C
    BR = P * ZR * (-(-(NX * C + max(TB, 2 * TG) * P) // (P * ZR)))

    acc_dram = nc.dram_tensor("acc_dram", (COPIES, AR, D), F32)
    acc_flat = acc_dram[:, :, :].rearrange("k r d -> (k r) d")
    xs_dram = nc.dram_tensor("xs_dram", (NT * P, D), F32)
    x1_dram = nc.dram_tensor("x1_dram", (NT * P, D), F32)
    buf_dram = nc.dram_tensor("buf_dram", (BR, D), F32)
    y_dram = nc.dram_tensor("y_dram", (NX * C, D), F32)

    with ExitStack() as ctx:
        def sb(name, shape, dt=F32):
            return ctx.enter_context(nc.sbuf_tensor(name, shape, dt))

        def sem(name):
            return ctx.enter_context(nc.semaphore(name))

        ident = sb("ident", [P, P])
        identb = sb("identb", [P, P], BF16)
        earlier = sb("earlier", [P, P])
        upto = sb("upto", [P, P], BF16)
        onesb = sb("onesb", [P, P], BF16)
        onesf = sb("onesf", [P, P])
        row0 = sb("row0", [P, P])
        iota_i = sb("iota_i", [P, P], I32)
        iota_f = sb("iota_f", [P, P])
        part_i = sb("part_i", [P, 1], I32)
        acc_dump = sb("acc_dump", [P, 1])
        acc_dump4 = sb("acc_dump4", [P, COPIES])
        buf_dump = sb("buf_dump", [P, 2 * TG])
        falling = sb("falling", [P, NX])
        valid = sb("valid", [P, NT])
        eps_t = sb("eps_t", [P, 1])
        zeros = sb("zeros", [P, ZR * D])
        neg_diag = sb("neg_diag", [P, D])
        bias_t = sb("bias_t", [P, D])
        gateb_t = sb("gateb_t", [P, NX])
        w_sb = sb("w_sb", [P, KD, D])
        gate_sb = sb("gate_sb", [P, KD, NX])
        b1_rows = sb("b1_rows", [NX * KF, P])
        b1_t = sb("b1_t", [P, NX * KF])
        b2_t = sb("b2_t", [P, NX, D])
        gather_row = sb("gather_row", [P, NT], I32)
        y_scale = sb("y_scale", [P, NT])

        NCP = NCH + GC
        ecols = sb("ecols", [P, NCP, 3])
        esplit = sb("esplit", [P, NCP, 2], BF16)
        dcols = sb("dcols", [P, NCP], I32)
        base_f = sb("base_f", [P, NB])
        base_i = sb("base_i", [P, NB], I32)
        spread = sb("spread", [P, 4])
        flag_i = sb("flag_i", [P, 1], I32)

        big = sb("big", [P, 26000])

        def region():
            at = [0]

            def take(shape, dt=F32):
                n = 1
                for s in shape:
                    n *= s
                n = n * (2 if dt == BF16 else 4) // 4
                v = big[:, at[0]:at[0] + n]
                at[0] += n
                assert at[0] <= 26000
                if dt != F32:
                    v = v.bitcast(dt)
                if len(shape) == 1:
                    return v
                names = "abcd"[:len(shape)]
                return v.rearrange(f"p ({' '.join(names)}) -> p {' '.join(names)}",
                                   **dict(zip(names[1:], shape[1:])))
            return take

        r = region()
        e_src_i, e_dst_i, e_w = r([EP], I32), r([EP], I32), r([EP])
        e_src, e_dst = r([EP]), r([EP])
        src_i, src_part = r([NCH], I32), r([NCH], I32)
        ln_x, ln_n, ln_s = r([2, TG, D]), r([2, TG, D]), r([2, TG, D])
        ln_stat, ln_mv, ln_std, ln_rstd = r([2, TG, 6]), r([2, TG, 2]), r([2, TG]), r([2, TG])
        r = region()
        stage_e, stage_s, stage_d = r([2, GC, 3]), r([2, GC, 2], BF16), r([GC], I32)
        same_w, is_node, g_sb = r([2, GC, P]), r([2, GC, P]), r([2, GC, P])
        rows, window = r([2, GC, D]), r([2, D])
        picked, sooner, offs, idx_f = r([2, GC, P]), r([2, GC]), r([2, GC]), r([2, GC])
        idx_a = r([2, GC], I32)
        gathered = r([GC, D])
        r = region()
        a_in, half, e4 = r([TG, COPIES, D]), r([TG, 2, D]), r([TG, D])
        x_in, x1 = r([2, TG, D]), r([2, TG, D])
        hn = r([2, TG, D])
        e4t, hnt = r([2, KD, P]), r([2, KD, P])
        st3, mv3, std3, rstd3 = r([TG, 6]), r([TG, 2]), r([TG]), r([TG])
        lg, pr, oh, t56 = r([TG, NX]), r([TG, NX]), r([TG, NX]), r([TG, NX])
        ohb = r([TG, NX], BF16)
        seen, seenb, new8 = r([NX]), r([NX], BF16), r([NX])
        c7 = [r([TG]) for _ in range(12)]
        scat_i = r([2, TG + 1], I32)
        r = region()
        w1_sb, w2_sb = r([2, KD, F]), r([2, KF, D])
        tok, tokT = r([2, TB, D]), r([2, KD, TB * P])
        hid, y_sb = r([2, KF, TB * P]), r([2, TB, D])
        r = region()
        yg, x1b = r([2, TG, D]), r([2, TG, D])
        yp, yn = r([2, TG, D]), r([2, TG, D])
        over, big4, neg4 = r([TG, D], U32), r([TG * D]), r([TG * D])
        gidx = r([2, TG + 1], I32)

        ps = ctx.enter_context(nc.psum_tensor("ps", [P, 8 * 512], F32))

        def bank(n, lo=0, hi=512):
            return ps[:, n * 512 + lo:n * 512 + hi]

        edges_in, consts_in, late_in, const_made = sem("edges_in"), sem("consts_in"), sem("late_in"), sem("const_made")
        pool_step = sem("pool_step")
        e_float, e_turned, e_col = sem("e_float"), sem("e_turned"), sem("e_col")
        prep, base_bc, base_out, flag_sum, flag_ok = sem("prep"), sem("base_bc"), sem("base_out"), sem("flag_sum"), sem("flag_ok")
        b1_turned, b1_ok = sem("b1_turned"), sem("b1_ok")
        zeros_ok, acc_zero, buf_zero = sem("zeros_ok"), sem("acc_zero"), sem("buf_zero")
        ln_in = [sem(f"ln_in{i}") for i in range(2)]
        ln_step, ln_sq, ln_xn, ln_xs = sem("ln_step"), sem("ln_sq"), sem("ln_xn"), sem("ln_xs")
        ln_mean = sem("ln_mean")
        ln_out = [sem(f"ln_out{i}") for i in range(2)]
        staged, bc_made, oh_made, g_made, g_copied = sem("staged"), sem("bc_made"), sem("oh_made"), sem("g_made"), sem("g_copied")
        r_made, r_copied, idx_step, idx_made = sem("r_made"), sem("r_copied"), sem("idx_step"), sem("idx_made")
        win_in = [sem(f"win_in{i}") for i in range(2)]
        acc_add = [sem(f"acc_add{i}") for i in range(COPIES)]
        gen_add = [sem(f"gen_add{i}") for i in range(COPIES)]
        gen_in = [sem(f"gen_in{i}") for i in range(GC)]
        gen_staged, gen_bc, gen_same, gen_idx, gen_step, gen_r, gen_rc = (
            sem(n) for n in ("gen_staged", "gen_bc", "gen_same", "gen_idx", "gen_step", "gen_r", "gen_rc"))
        scattered = sem("scattered")
        a_got = [sem(f"a_got{i}") for i in range(TG)]
        x_got = [sem(f"x_got{i}") for i in range(2)]
        half_made, e4_made, e4_turned, e4_copied, w_made = sem("half_made"), sem("e4_made"), sem("e4_turned"), sem("e4_copied"), sem("w_made")
        xb_made, x1_made, stat_made, mv_made, std_made, rstd_made = (
            sem(n) for n in ("xb_made", "x1_made", "stat_made", "mv_made", "std_made", "rstd_made"))
        h_made, h_turned, h_copied, lg_made = sem("h_made"), sem("h_turned"), sem("h_copied"), sem("lg_made")
        x1_out = [sem(f"x1_out{i}") for i in range(2)]
        route, exp_made, rank_made, slot_made = sem("route"), sem("exp_made"), sem("rank_made"), sem("slot_made")
        h_out = [sem(f"h_out{i}") for i in range(2)]
        wts_in = [sem(f"wts_in{i}") for i in range(2)]
        tok_in = [sem(f"tok_in{i}") for i in range(2)]
        tok_turned, tok_copied, m1_made, hid_made, m2_made, y_made = (
            sem(n) for n in ("tok_turned", "tok_copied", "m1_made", "hid_made", "m2_made", "y_made"))
        y_out = [sem(f"y_out{i}") for i in range(2)]
        gidx_made = sem("gidx_made")
        yg_in = [sem(f"yg_in{i}") for i in range(2)]
        x1_in = [sem(f"x1_in{i}") for i in range(2)]
        lim_made, fin_step, o_made = sem("lim_made"), sem("fin_step"), sem("o_made")
        o_out = [sem(f"o_out{i}") for i in range(2)]

        NR = 21
        N_CONST = 13
        NP_FIN = 7

        pool_passed, act_passed, dve_passed = sem("pool_passed"), sem("act_passed"), sem("dve_passed")

        block = ctx.enter_context(nc.Block())

        @block.sync
        def _(sp):
            def edge_load(dst_t, src_d):
                v = src_d[0:EFULL * EP].rearrange("(q n) -> q n", n=EP)
                cut = EFULL // 16 * 16
                sp.dma_start(dst_t[0:cut, :], v[0:cut, :]).then_inc(edges_in, 16)
                sp.dma_start(dst_t[cut:EFULL, :], v[cut:EFULL, :]).then_inc(edges_in, 16)
                sp.dma_start(dst_t[EFULL:P, 0:EREST], src_d[EFULL * EP:E].rearrange("(q n) -> q n", q=1)).then_inc(edges_in, 16)

            sp.wait_ge(e_float, 3)
            edge_load(e_src_i, src)
            edge_load(e_dst_i, dst)
            edge_load(e_w, edge_weight)
            sp.dma_start(neg_diag[:, :], gnn_diag.rearrange("(q n) -> q n", q=1).to_broadcast([P, D])).then_inc(consts_in, 16)
            sp.dma_start(b1_rows[:, :], b1.rearrange("e (m p) -> (e m) p", p=P)).then_inc(consts_in, 16)

            def ln_load(j, slot, tail):
                if tail:
                    sp.dma_start(ln_x[:, slot, 0:TG - 1, :], x[(NT - TG) * P:(NT - 1) * P, :].rearrange("(t p) d -> p t d", p=P)).then_inc(ln_in[slot], 16)
                    sp.dma_start(ln_x[0:NREST, slot, TG - 1, :], x[(NT - 1) * P:N, :]).then_inc(ln_in[slot], 16)
                else:
                    a = TG - 1
                    sp.dma_start(ln_x[:, slot, 0:a, :], x[bass.ds(j * (TG * P), a * P), :].rearrange("(t p) d -> p t d", p=P)).then_inc(ln_in[slot], 16)
                    sp.dma_start(ln_x[:, slot, a, :], x[bass.ds(j * (TG * P) + a * P, P), :]).then_inc(ln_in[slot], 16)

            def ln_store(j, slot):
                sp.wait_ge(ln_xn, j + 1)
                sp.dma_start(acc_dram[0, bass.ds(j * (TG * P), TG * P), :].rearrange("(t p) d -> p t d", p=P), ln_n[:, slot, :, :]).then_inc(ln_out[slot], 16)
                sp.wait_ge(ln_xs, j + 1)
                sp.dma_start(xs_dram[bass.ds(j * (TG * P), TG * P), :].rearrange("(t p) d -> p t d", p=P), ln_s[:, slot, :, :]).then_inc(ln_out[slot], 16)

            ln_load(0, 0, False)
            ln_load(1, 1, False)

            def ln_pair(i, tail):
                for h in range(2):
                    sp.wait_ge(ln_xn, 2 * i + h + 1)
                    ln_load(2 * i + h + 2, h, tail and h == 1)
                    ln_store(2 * i + h, h)

            with sp.Fori(0, NG // 2 - 2) as i:
                ln_pair(i, False)
            ln_pair(NG // 2 - 2, True)
            ln_store(NG - 2, 0)
            ln_store(NG - 1, 1)
            sp.dma_start(bias_t[:, :], gnn_bias.rearrange("(q n) -> q n", q=1).to_broadcast([P, D])).then_inc(late_in, 16)
            sp.dma_start(gateb_t[:, :], gate_b.rearrange("(q n) -> q n", q=1).to_broadcast([P, NX])).then_inc(late_in, 16)
            sp.dma_start(w_sb[:, :, :], gnn_w.rearrange("(k p) n -> p k n", p=P)).then_inc(late_in, 16)
            sp.dma_start(gate_sb[:, :, :], gate_w.rearrange("(k p) n -> p k n", p=P)).then_inc(late_in, 16)
            sp.dma_start(b2_t[:, :, :], b2.rearrange("(q e) n -> q e n", q=1).to_broadcast([P, NX, D])).then_inc(late_in, 16)
            for s in range(2):
                sp.wait_ge(ln_out[s], 32 * (NG // 2))

            sp.wait_ge(flag_ok, 1)
            flag = sp.value_load(flag_i[0:1, 0:1], min_val=0, max_val=P)
            with sp.If(flag == 0):
                def window_load(b, slot, first):
                    if not first:
                        sp.wait_ge(r_made, 4 * (b - 1))
                    base = sp.value_load(base_i[0:1, bass.ds(b, 1)], min_val=0, max_val=N - P)
                    sp.dma_start(window[:, slot, :], xs_dram[bass.ds(base, P), :]).then_inc(win_in[slot], 16)

                for h in range(2):
                    window_load(h, h, True)
                with sp.Fori(1, NB // 2) as i:
                    for h in range(2):
                        window_load(2 * i + h, h, False)

            sp.wait_ge(scattered, 1)
            def node_load(j, h, first, tail):
                if not first:
                    sp.wait_ge(x1_made, TG * (j - 1))
                if tail:
                    sp.dma_start(x_in[:, h, 0:TG - 1, :], x[(NT - TG) * P:(NT - 1) * P, :].rearrange("(t p) d -> p t d", p=P)).then_inc(x_got[h], 16)
                    sp.dma_start(x_in[0:NREST, h, TG - 1, :], x[(NT - 1) * P:N, :]).then_inc(x_got[h], 16)
                else:
                    a = TG - 1
                    sp.dma_start(x_in[:, h, 0:a, :], x[bass.ds(j * (TG * P), a * P), :].rearrange("(t p) d -> p t d", p=P)).then_inc(x_got[h], 16)
                    sp.dma_start(x_in[:, h, a, :], x[bass.ds(j * (TG * P) + a * P, P), :]).then_inc(x_got[h], 16)
                for t in range(TG):
                    if not (first and h == 0):
                        sp.wait_ge(half_made, TG * (j - 1) + t + 1)
                    sp.dma_start(a_in[:, t, :, :], acc_dram[:, bass.ds(j * (TG * P) + t * P, P), :].rearrange("k p d -> p k d")).then_inc(a_got[t], 16)

            def x1_store(j, h):
                sp.wait_ge(x1_made, TG * (j + 1))
                sp.dma_start(x1_dram[bass.ds(j * (TG * P), TG * P), :].rearrange("(t p) d -> p t d", p=P), x1[:, h, :, :]).then_inc(x1_out[h], 16)

            node_load(0, 0, True, False)
            node_load(1, 1, True, False)

            def node_pair(i, tail):
                for h in range(2):
                    x1_store(2 * i + h, h)
                    node_load(2 * i + h + 2, h, False, tail and h == 1)

            with sp.Fori(0, NG // 2 - 2) as i:
                node_pair(i, False)
            node_pair(NG // 2 - 2, True)
            x1_store(NG - 2, 0)
            x1_store(NG - 1, 1)
            for s in range(2):
                sp.wait_ge(x1_out[s], 16 * (NG // 2))
                sp.wait_ge(h_out[s], 16 * TG * (NG // 2))

            def weights_load(e, s, first):
                if not first:
                    sp.wait_ge(m2_made, 2 * XB * (e - 1))
                sp.dma_start(w1_sb[:, s, :, :], w1[bass.ds(e, 1), :, :].rearrange("e (k p) n -> p (e k) n", p=P)).then_inc(wts_in[s], 16)
                sp.dma_start(w2_sb[:, s, :, :], w2[bass.ds(e, 1), :, :].rearrange("e (k p) n -> p (e k) n", p=P)).then_inc(wts_in[s], 16)

            def tokens_load(e, b, first):
                s = b % 2
                if not (first and b < 2):
                    sp.wait_ge(tok_turned, e * XB + b - 1)
                sp.dma_start(tok[:, s, :, :], buf_dram[bass.ds(e * C + b * (TB * P), TB * P), :].rearrange("(t p) d -> p t d", p=P)).then_inc(tok_in[s], 16)

            def expert_pair(e0, first):
                for s in range(2):
                    weights_load(e0 + s, s, first)
                    for b in range(XB):
                        tokens_load(e0 + s, b, first and s == 0)

            expert_pair(0, True)
            with sp.Fori(1, NX // 2) as i:
                expert_pair(2 * i, False)
            tokens_load(NX, 0, False)

            for s in range(2):
                sp.wait_ge(y_out[s], 16 * TB * (NX * XB // 2))
            sp.wait_ge(tok_copied, NX * XB + 1)
            def x1_load(j, h, first):
                if not first:
                    sp.wait_ge(o_made, j - 1)
                sp.dma_start(x1b[:, h, :, :], x1_dram[bass.ds(j * (TG * P), TG * P), :].rearrange("(t p) d -> p t d", p=P)).then_inc(x1_in[h], 16)

            def out_store(j, h, tail):
                sp.wait_ge(o_made, j + 1)
                if tail:
                    sp.dma_start(out[(NT - TG) * P:(NT - 1) * P, :].rearrange("(t p) d -> p t d", p=P), yp[:, h, 0:TG - 1, :]).then_inc(o_out[h], 16)
                    sp.dma_start(out[(NT - 1) * P:N, :], yp[0:NREST, h, TG - 1, :]).then_inc(o_out[h], 16)
                else:
                    a = TG - 1
                    sp.dma_start(out[bass.ds(j * (TG * P), a * P), :].rearrange("(t p) d -> p t d", p=P), yp[:, h, 0:a, :]).then_inc(o_out[h], 16)
                    sp.dma_start(out[bass.ds(j * (TG * P) + a * P, P), :], yp[:, h, a, :]).then_inc(o_out[h], 16)

            x1_load(0, 0, True)
            x1_load(1, 1, True)
            with sp.Fori(0, NG // 2 - 1) as i:
                for h in range(2):
                    out_store(2 * i + h, h, False)
                    x1_load(2 * i + h + 2, h, False)
            out_store(NG - 2, 0, False)
            out_store(NG - 1, 1, True)
            for s in range(2):
                sp.wait_ge(o_out[s], 32 * (NG // 2))

        @block.gpsimd
        def _(pool):
            pool.memset(ident[:, :], 0.0).then_inc(pool_step, 1)
            pool.memset(identb[:, :], 0.0).then_inc(pool_step, 1)
            pool.memset(earlier[:, :], 1.0).then_inc(pool_step, 1)
            pool.memset(upto[:, :], 1.0).then_inc(pool_step, 1)
            pool.memset(row0[:, :], 0.0).then_inc(pool_step, 1)
            pool.memset(valid[:, :], 1.0).then_inc(pool_step, 1)
            pool.memset(onesb[:, :], 1.0).then_inc(const_made, 1)
            pool.memset(onesf[:, :], 1.0).then_inc(const_made, 1)
            pool.memset(eps_t[:, :], EPS).then_inc(const_made, 1)
            pool.iota(iota_i[:, :], pattern=[[1, P]], base=0, channel_multiplier=0).then_inc(const_made, 1)
            pool.iota(part_i[:, :], pattern=[[0, 1]], base=0, channel_multiplier=1).then_inc(const_made, 1)
            for e in range(NX):
                last = pool.memset(falling[:, e:e + 1], float(NX - e))
            last.then_inc(const_made, 1)
            pool.wait_ge(pool_step, 6)
            for t in (ident, identb):
                pool.affine_select(out=t[:, :], in_=t[:, :], compare_op=ALU.not_equal, fill=1.0, base=0,
                                   pattern=[[1, P]], channel_multiplier=-1).then_inc(const_made, 1)
            pool.affine_select(out=earlier[:, :], in_=earlier[:, :], compare_op=ALU.is_gt, fill=0.0, base=0,
                               pattern=[[-1, P]], channel_multiplier=1).then_inc(const_made, 1)
            pool.affine_select(out=upto[:, :], in_=upto[:, :], compare_op=ALU.is_ge, fill=0.0, base=0,
                               pattern=[[1, P]], channel_multiplier=-1).then_inc(const_made, 1)
            pool.memset(row0[0:1, :], 1.0).then_inc(const_made, 1)
            pool.affine_select(out=valid[:, NT - 1:NT], in_=valid[:, NT - 1:NT], compare_op=ALU.is_ge, fill=0.0,
                               base=NREST - 1, pattern=[[0, 1]], channel_multiplier=-1).then_inc(const_made, 1)
            pool.memset(ecols[:, NCH:NCP, :], 0.0).then_inc(const_made, 1)

            def ln_scale(j, h, stored):
                pool.wait_ge(ln_xn, j + 1)
                if stored is not None:
                    pool.wait_ge(ln_out[h], stored)
                pool.tensor_tensor(ln_s[:, h, :, :], ln_n[:, h, :, :],
                                   neg_diag[:, :].unsqueeze(1).to_broadcast([P, TG, D]), ALU.mult).then_inc(ln_xs, 1)

            pool.wait_ge(prep, 4)
            for h in range(2):
                ln_scale(h, h, None)
            with pool.Fori(1, NG // 2) as i:
                for h in range(2):
                    ln_scale(2 * i + h, h, 32 * i)

            pool.wait_ge(acc_zero, 16 * ((COPIES - 1) * (AR // P // ZR) + (AR // P - NT)))
            for s in range(2):
                pool.wait_ge(ln_out[s], 32 * (NG // 2))
            pool.wait_ge(flag_ok, 1)
            flag = pool.value_load(flag_i[0:1, 0:1], min_val=0, max_val=P)
            with pool.If(flag == 0):
                def scatter_group(s, par, first):
                    pool.wait_ge(idx_made, s + 1)
                    for c in range(GC):
                        if c % 2 == 0:
                            pool.wait_ge(r_copied, 2 * s + c // 2 + 1)
                        if not first:
                            pool.wait_ge(acc_add[c], 16 * s)
                        pool.sem_inc(pool_passed, 1)
                        pool.indirect_dma_start(
                            out=acc_flat, out_offset=bass.IndirectOffsetOnAxis(ap=idx_a[:, par, c:c + 1], axis=0),
                            in_=rows[:, par, c, :], in_offset=None, compute_op=ALU.add).then_inc(acc_add[c], 16)

                for g in range(4):
                    scatter_group(g, g % 2, g == 0)
                with pool.Fori(1, NGR // 4) as i:
                    for g in range(4):
                        scatter_group(4 * i + g, g % 2, False)
                for c in range(COPIES):
                    pool.wait_ge(acc_add[c], 16 * NGR)
            with pool.Else():
                def general_group(s, first):
                    pool.wait_ge(gen_staged, s + 1)
                    if not first:
                        pool.wait_ge(gen_r, s)
                    pool.sem_inc(pool_passed, 1)
                    for c in range(GC):
                        pool.indirect_dma_start(
                            out=gathered[:, c, :], out_offset=None, in_=xs_dram[:, :],
                            in_offset=bass.IndirectOffsetOnAxis(ap=stage_d[:, c:c + 1], axis=0)).then_inc(gen_in[c], 16)
                    pool.wait_ge(gen_idx, s + 1)
                    pool.wait_ge(gen_rc, s + 1)
                    pool.sem_inc(pool_passed, 1)
                    for c in range(GC):
                        pool.indirect_dma_start(
                            out=acc_flat, out_offset=bass.IndirectOffsetOnAxis(ap=idx_a[:, 0, c:c + 1], axis=0),
                            in_=rows[:, 0, c, :], in_offset=None, compute_op=ALU.add).then_inc(gen_add[c], 16)
                    for c in range(COPIES):
                        pool.wait_ge(gen_add[c], 16 * (s + 1))
                general_group(0, True)
                with pool.Fori(1, NGR) as s:
                    general_group(s, False)
            pool.sem_inc(scattered, 1)

            pool.wait_ge(late_in, 16 * 5)

            def add_bias(j, h):
                pool.wait_ge(x_got[h], 32 * (j // 2 + 1))
                pool.tensor_tensor(x_in[:, h, :, :], x_in[:, h, :, :],
                                   bias_t[:, :].unsqueeze(1).to_broadcast([P, TG, D]), ALU.add).then_inc(xb_made, 1)

            def send_tokens(j, h):
                pool.wait_ge(slot_made, j + 1)
                pool.wait_ge(buf_zero, 16 * (BR // P // ZR))
                pool.sem_inc(pool_passed, 1)
                for t in range(TG):
                    pool.indirect_dma_start(
                        out=buf_dram[:, :], out_offset=bass.IndirectOffsetOnAxis(ap=scat_i[:, h, t:t + 1], axis=0),
                        in_=hn[:, h, t, :], in_offset=None).then_inc(h_out[h], 16)

            add_bias(0, 0)
            with pool.Fori(0, NG // 2 - 1) as i:
                pool.wait_ge(x_got[1], 32 * (i + 1))
                pool.tensor_tensor(x_in[:, 1, :, :], x_in[:, 1, :, :],
                                   bias_t[:, :].unsqueeze(1).to_broadcast([P, TG, D]), ALU.add).then_inc(xb_made, 1)
                send_tokens(2 * i, 0)
                pool.wait_ge(x_got[0], 32 * (i + 2))
                pool.tensor_tensor(x_in[:, 0, :, :], x_in[:, 0, :, :],
                                   bias_t[:, :].unsqueeze(1).to_broadcast([P, TG, D]), ALU.add).then_inc(xb_made, 1)
                send_tokens(2 * i + 1, 1)
            add_bias(NG - 1, 1)
            send_tokens(NG - 2, 0)
            send_tokens(NG - 1, 1)

            def y_store(e, b):
                s = b % 2
                pool.wait_ge(y_made, 2 * (e * XB + b + 1))
                for t in range(TB):
                    n = min(P, C - (b * TB + t) * P)
                    pool.dma_start(y_dram[bass.ds(e * C + (b * TB + t) * P, n), :], y_sb[0:n, s, t, :]).then_inc(y_out[s], 16)

            with pool.Fori(0, NX) as e:
                for b in range(XB):
                    y_store(e, b)

            for s in range(2):
                pool.wait_ge(y_out[s], 16 * TB * (NX * XB // 2))
            pool.wait_ge(tok_copied, NX * XB + 1)

            def gather_y(j, h, first):
                if not first:
                    pool.wait_ge(fin_step, NP_FIN * (j - 2) + 2)
                pool.tensor_copy(gidx[:, h, 0:TG], gather_row[:, bass.ds(j * TG, TG)]).then_inc(gidx_made, 1)
                pool.wait_ge(gidx_made, j + 1)
                pool.sem_inc(pool_passed, 1)
                for t in range(TG):
                    pool.indirect_dma_start(
                        out=yg[:, h, t, :], out_offset=None, in_=y_dram[:, :],
                        in_offset=bass.IndirectOffsetOnAxis(ap=gidx[:, h, t:t + 1], axis=0)).then_inc(yg_in[h], 16)

            for h in range(2):
                gather_y(h, h, True)
            with pool.Fori(1, NG // 2) as i:
                for h in range(2):
                    gather_y(2 * i + h, h, False)

        @block.scalar
        def _(act):
            act.wait_ge(zeros_ok, 1)
            nz = AR // P // ZR
            for k in range(1, COPIES):
                v = acc_dram[k, :, :].rearrange("(p n) d -> p (n d)", p=P)
                for z in range(nz):
                    act.dma_start(v[:, z * ZR * D:(z + 1) * ZR * D], zeros[:, :]).then_inc(acc_zero, 16)
            for z in range(0, AR - NT * P, P):
                act.dma_start(acc_dram[0, NT * P + z:NT * P + z + P, :], zeros[:, 0:D]).then_inc(acc_zero, 16)

            for k in range(EQ):
                for a in range(3):
                    n = 3 * k + a
                    act.wait_ge(e_turned, n + 1)
                    q = bank(n % 4, 0, P)
                    act.copy(ecols[:, k:NCH:EQ, a], q).then_inc(e_col, 1)
            act.wait_ge(b1_turned, 1)
            act.copy(b1_t[:, :], bank(4, 0, NX * KF)).then_inc(b1_ok, 1)

            bv = buf_dram[:, :].rearrange("(p n) d -> p (n d)", p=P)
            for z in range(BR // P // ZR):
                act.dma_start(bv[:, z * ZR * D:(z + 1) * ZR * D], zeros[:, :]).then_inc(buf_zero, 16)

            act.wait_ge(const_made, N_CONST)
            with act.Fori(0, NG // 2) as i:
                for h in range(2):
                    act.wait_ge(ln_mean, 2 * i + h + 1)
                    act.activation(ln_std[:, h, :], ln_mv[:, h, :, 1], ACT.Sqrt, bias=eps_t[:, 0:1]).then_inc(ln_sq, 1)

            act.wait_ge(flag_ok, 1)
            flag = act.value_load(flag_i[0:1, 0:1], min_val=0, max_val=P)
            act.wait_ge(ln_out[0], 32 * (NG // 2))
            act.wait_ge(ln_out[1], 32 * (NG // 2))
            with act.If(flag == 0):
                def stage(s, par):
                    act.copy(stage_s[:, par, :, :], esplit[:, bass.ds(s * GC, GC), :])
                    act.copy(stage_e[:, par, :, :], ecols[:, bass.ds(s * GC, GC), :]).then_inc(staged, 1)

                def copy_group(s, par, g, peeled):
                    if not (peeled and g == 0):
                        act.wait_ge(idx_made, s)
                    stage(s + 1, 1 - par)
                    for c in range(2):
                        act.wait_ge(g_made, 2 * s + c + 1)
                        if not (peeled and g < 2):
                            act.wait_ge(r_made, 2 * (s - 1))
                        act.copy(g_sb[:, par, 2 * c:2 * c + 2, :], bank(2 + c, 0, 2 * P).rearrange("p (a b) -> p a b", b=P)).then_inc(g_copied, 1)
                    for c in range(2):
                        act.wait_ge(r_made, 2 * s + c + 1)
                        if not (peeled and g < 2):
                            for k in (2 * c, 2 * c + 1):
                                act.wait_ge(acc_add[k], 16 * (s - 1))
                        act.copy(rows[:, par, 2 * c:2 * c + 2, :], bank(4 + 2 * par + c).rearrange("p (a b) -> p a b", b=D)).then_inc(r_copied, 1)

                stage(0, 0)
                for g in range(4):
                    copy_group(g, g % 2, g, True)
                with act.Fori(1, NGR // 4) as i:
                    for g in range(4):
                        copy_group(4 * i + g, g % 2, g, False)
            with act.Else():
                def general_copy(s, first):
                    if not first:
                        act.wait_ge(gen_idx, s)
                        act.wait_ge(gen_r, s)
                    act.copy(stage_s[:, 0, :, :], esplit[:, bass.ds(s * GC, GC), :])
                    act.copy(stage_e[:, 0, :, :], ecols[:, bass.ds(s * GC, GC), :])
                    act.copy(stage_d[:, :], dcols[:, bass.ds(s * GC, GC)]).then_inc(gen_staged, 1)
                    act.wait_ge(gen_r, s + 1)
                    if not first:
                        for c in range(COPIES):
                            act.wait_ge(gen_add[c], 16 * s)
                    for c in range(2):
                        last = act.copy(rows[:, 0, 2 * c:2 * c + 2, :], bank(4 + c).rearrange("p (a b) -> p a b", b=D))
                    last.then_inc(gen_rc, 1)
                general_copy(0, True)
                with act.Fori(1, NGR) as s:
                    general_copy(s, False)

            act.wait_ge(scattered, 1)

            def copy_e4(j, peeled):
                for t in range(TG):
                    act.wait_ge(e4_turned, TG * j + t + 1)
                    if not (peeled and t < 2):
                        act.wait_ge(w_made, TG * j + t - 1)
                    act.copy(e4t[:, t % 2, :, :], bank(4 + t % 2, 0, D).rearrange("p (a b) -> p a b", b=P)).then_inc(e4_copied, 1)

            def copy_h(j, peeled):
                for t in range(TG):
                    act.wait_ge(h_turned, TG * j + t + 1)
                    if not (peeled and t < 2):
                        act.wait_ge(lg_made, TG * j + t - 1)
                    act.copy(hnt[:, t % 2, :, :], bank(5 - t % 2, 0, D).rearrange("p (a b) -> p a b", b=P)).then_inc(h_copied, 1)

            def node_group(j, first, last):
                act.wait_ge(mv_made, j + 1)
                act.activation(std3[:, :], mv3[:, :, 1], ACT.Sqrt, bias=eps_t[:, 0:1]).then_inc(std_made, 1)
                copy_h(j, first)
                if not last:
                    copy_e4(j + 1, False)
                act.wait_ge(route, NR * j + 3)
                act.activation(pr[:, :, :], t56[:, :, :], ACT.Exp).then_inc(exp_made, 1)

            copy_e4(0, True)
            node_group(0, True, False)
            with act.Fori(1, NG - 1) as j:
                node_group(j, False, False)
            node_group(NG - 1, False, True)

            for s in range(2):
                act.wait_ge(h_out[s], 16 * TG * (NG // 2))

            def turn_copy(n, s, first):
                act.wait_ge(tok_turned, n + 1)
                if not first:
                    act.wait_ge(m1_made, KF * (n - 1))
                for k in range(KD):
                    last = act.copy(tokT[:, s, k, :], bank(k))
                last.then_inc(tok_copied, 1)

            def expert_block(e, b, first):
                n = e * XB + b
                s = b % 2
                cols = min(TB * P, C - b * TB * P)
                for m in range(KF):
                    act.wait_ge(m1_made, KF * n + m + 1)
                    if m == 0 and not (first and b < 2):
                        act.wait_ge(m2_made, 2 * (n - 1))
                    act.sem_inc(act_passed, 1)
                    act.activation(hid[:, s, m, 0:cols], bank(2 + m % 4, 0, cols), ACT.Relu, bias=b1_t[:, bass.ds(e * KF + m, 1)]).then_inc(hid_made, 1)
                turn_copy(n + 1, 1 - s, first and b == 0)

            turn_copy(0, 0, True)
            for b in range(XB):
                expert_block(0, b, True)
            with act.Fori(1, NX) as e:
                for b in range(XB):
                    expert_block(e, b, False)

        @block.tensor
        def _(pe):
            pe.wait_ge(const_made, N_CONST)
            pe.wait_ge(e_float, 5)
            pe.wait_ge(edges_in, 16 * 9)
            for k in range(EQ):
                for a, t in enumerate((e_src, e_w, e_dst)):
                    n = 3 * k + a
                    if n >= 4:
                        pe.wait_ge(e_col, n - 3)
                    pe.transpose(bank(n % 4, 0, P), t[:, k * P:(k + 1) * P], ident[:, :]).then_inc(e_turned, 1)
            pe.wait_ge(consts_in, 32)
            pe.transpose(bank(4, 0, NX * KF), b1_rows[:, :], ident[0:NX * KF, 0:NX * KF]).then_inc(b1_turned, 1)
            pe.wait_ge(e_col, 3 * EQ)
            pe.matmul(bank(0, 0, NB), row0[:, :], ecols[:, 0:NCH:BC, 2], start=True, stop=True).then_inc(base_bc, 1)
            pe.wait_ge(prep, 11)
            pe.matmul(bank(1, 0, 1), onesf[:, :], spread[:, 3:4], start=True, stop=True).then_inc(flag_sum, 1)

            pe.wait_ge(flag_ok, 1)
            flag = pe.value_load(flag_i[0:1, 0:1], min_val=0, max_val=P)
            with pe.If(flag == 0):
                def broadcast_src(par, sem_, b0):
                    for c in range(GC):
                        for k in range(2):
                            mm = pe.matmul(bank(b0 + par, c * P, (c + 1) * P), stage_s[:, par, c, k:k + 1].to_broadcast([P, P]),
                                           identb[:, :], start=(k == 0), stop=(k == 1))
                    mm.then_inc(sem_, 1)

                def product_group(s, par, g, fills, peeled):
                    for c in range(GC):
                        pe.wait_ge(oh_made, GC * s + c + 1)
                        if c % 2 == 0 and not (peeled and g == 0):
                            pe.wait_ge(g_copied, 2 * (s - 1) + c // 2 + 1)
                        mm = pe.matmul(bank(2 + c // 2, (c % 2) * P, (c % 2 + 1) * P), is_node[:, par, c, :], same_w[:, par, c, :], start=True, stop=True)
                        if c % 2:
                            mm.then_inc(g_made, 1)
                    pe.wait_ge(staged, s + 2)
                    if not (peeled and g == 0):
                        pe.wait_ge(idx_made, s)
                    broadcast_src(1 - par, bc_made, 0)
                    if g % 2 == 0:
                        pe.wait_ge(win_in[g // 2], 16 * fills)
                    for c in range(GC):
                        if c % 2 == 0:
                            pe.wait_ge(g_copied, 2 * s + c // 2 + 1)
                            if not (peeled and g < 2):
                                pe.wait_ge(r_copied, 2 * (s - 2) + c // 2 + 1)
                        mm = pe.matmul(bank(4 + 2 * par + c // 2, (c % 2) * D, (c % 2 + 1) * D), g_sb[:, par, c, :], window[:, g // 2, :], start=True, stop=True)
                        if c % 2:
                            mm.then_inc(r_made, 1)

                pe.wait_ge(staged, 1)
                broadcast_src(0, bc_made, 0)
                for g in range(4):
                    product_group(g, g % 2, g, 1, True)
                with pe.Fori(1, NGR // 4) as i:
                    for g in range(4):
                        product_group(4 * i + g, g % 2, g, i + 1, False)
            with pe.Else():
                def general_products(s, first):
                    pe.wait_ge(gen_staged, s + 1)
                    if not first:
                        pe.wait_ge(gen_idx, s)
                    for c in range(GC):
                        for k in range(2):
                            mm = pe.matmul(bank(0, c * P, (c + 1) * P), stage_s[:, 0, c, k:k + 1].to_broadcast([P, P]),
                                           identb[:, :], start=(k == 0), stop=(k == 1))
                    mm.then_inc(gen_bc, 1)
                    pe.wait_ge(gen_same, s + 1)
                    if not first:
                        pe.wait_ge(gen_rc, s)
                    for c in range(GC):
                        pe.wait_ge(gen_in[c], 16 * (s + 1))
                        mm = pe.matmul(bank(4 + c // 2, (c % 2) * D, (c % 2 + 1) * D), same_w[:, 0, c, :], gathered[:, c, :], start=True, stop=True)
                    mm.then_inc(gen_r, 1)
                general_products(0, True)
                with pe.Fori(1, NGR) as s:
                    general_products(s, False)

            pe.wait_ge(late_in, 16 * 5)

            def o_bank(t):
                return bank(t // 2, (t % 2) * D, (t % 2 + 1) * D)

            def turn_and_multiply(j, peeled):
                for t in range(TG + 1):
                    if t < TG:
                        pe.wait_ge(e4_made, TG * j + t + 1)
                        if t >= 2:
                            pe.wait_ge(e4_copied, TG * j + t - 1)
                        elif not peeled:
                            pe.wait_ge(h_copied, TG * (j - 1) + TG - 1 + t)
                        for k in range(KD):
                            mm = pe.transpose(bank(4 + t % 2, k * P, (k + 1) * P), e4[:, t, k * P:(k + 1) * P], ident[:, :])
                        mm.then_inc(e4_turned, 1)
                    if t >= 1:
                        u = t - 1
                        pe.wait_ge(e4_copied, TG * j + u + 1)
                        if u == 0 and not peeled:
                            pe.wait_ge(x1_made, TG * j)
                        for k in range(KD):
                            mm = pe.matmul(o_bank(u), e4t[:, u % 2, k, :], w_sb[:, k, :], start=(k == 0), stop=(k == KD - 1))
                        mm.then_inc(w_made, 1)

            def turn_and_gate(j, h, first):
                for t in range(TG + 1):
                    if t < TG:
                        pe.wait_ge(h_made, TG * j + t + 1)
                        if t >= 2:
                            pe.wait_ge(h_copied, TG * j + t - 1)
                        else:
                            pe.wait_ge(e4_copied, TG * j + TG - 1 + t)
                        for k in range(KD):
                            mm = pe.transpose(bank(5 - t % 2, k * P, (k + 1) * P), hn[:, h, t, k * P:(k + 1) * P], ident[:, :])
                        mm.then_inc(h_turned, 1)
                    if t >= 1:
                        u = t - 1
                        pe.wait_ge(h_copied, TG * j + u + 1)
                        if u == 0 and not first:
                            pe.wait_ge(route, NR * (j - 1) + 1)
                        for k in range(KD):
                            mm = pe.matmul(bank(6, u * NX, (u + 1) * NX), hnt[:, u % 2, k, :], gate_sb[:, k, :], start=(k == 0), stop=(k == KD - 1))
                        mm.then_inc(lg_made, 1)

            def rank_products(j, first):
                pe.wait_ge(route, NR * j + 12)
                if not first:
                    pe.wait_ge(route, NR * j)
                r_out = bank(7, 0, TG * NX)
                pe.matmul(r_out, onesb[:, :], seenb.unsqueeze(1).to_broadcast([P, TG, NX]), start=True, stop=True)
                for t in range(TG - 1):
                    pe.matmul(bank(7, (t + 1) * NX, TG * NX).rearrange("p (a b) -> p a b", b=NX), onesb[:, :],
                              ohb[:, t:t + 1, :].to_broadcast([P, TG - 1 - t, NX]), start=False, stop=True, skip_group_check=True)
                pe.matmul(r_out, upto[:, :], ohb[:, :, :].rearrange("p a b -> p (a b)"),
                          start=False, stop=True, skip_group_check=True).then_inc(rank_made, 1)

            turn_and_multiply(0, True)
            turn_and_gate(0, 0, True)
            turn_and_multiply(1, False)
            rank_products(0, True)
            with pe.Fori(0, NG // 2 - 1) as i:
                for h in (1, 0):
                    j = 2 * i + 2 - h
                    turn_and_gate(j, h, False)
                    turn_and_multiply(j + 1, False)
                    rank_products(j, False)
            turn_and_gate(NG - 1, 1, False)
            rank_products(NG - 1, False)

            def turn_tokens(n, s, first):
                if not first:
                    pe.wait_ge(tok_copied, n)
                for k in range(KD):
                    for t in range(TB):
                        mm = pe.transpose(bank(k, t * P, (t + 1) * P), tok[:, s, t, k * P:(k + 1) * P], ident[:, :])
                mm.then_inc(tok_turned, 1)

            def expert_products(e, s_e, b, first):
                n = e * XB + b
                s = b % 2
                cols = min(TB * P, C - b * TB * P)
                pe.wait_ge(tok_copied, n + 1)
                for m in range(KF):
                    if not (first and b == 0 and m < 4):
                        pe.wait_ge(hid_made, KF * n + m - 3)
                    for k in range(KD):
                        mm = pe.matmul(bank(2 + m % 4, 0, cols), w1_sb[:, s_e, k, m * P:(m + 1) * P], tokT[:, s, k, 0:cols],
                                       start=(k == 0), stop=(k == KD - 1))
                    mm.then_inc(m1_made, 1)

            def expert_out(e, s_e, b, first):
                n = e * XB + b
                s = b % 2
                cols = min(TB * P, C - b * TB * P)
                pe.wait_ge(hid_made, KF * (n + 1))
                for t in range(TB):
                    w = min(P, cols - t * P)
                    if t % 2 == 0 and not (first and b == 0):
                        pe.wait_ge(y_made, 2 * n - 1 + t // 2)
                    for m in range(KF):
                        mm = pe.matmul(bank(6 + t // 2, (t % 2) * D, (t % 2 + 1) * D)[0:w, :], hid[:, s, m, t * P:t * P + w], w2_sb[:, s_e, m, :],
                                       start=(m == 0), stop=(m == KF - 1))
                    if t % 2:
                        mm.then_inc(m2_made, 1)

            pe.wait_ge(tok_in[0], 16)
            turn_tokens(0, 0, True)

            def expert(e, s_e, wts, toks, first):
                pe.wait_ge(wts_in[s_e], wts)
                for b in range(XB):
                    expert_products(e, s_e, b, first)
                    pe.wait_ge(tok_in[(b + 1) % 2], 16 * (toks + (b + 1) // 2 + 1))
                    turn_tokens(e * XB + b + 1, (b + 1) % 2, False)
                    expert_out(e, s_e, b, first)

            expert(0, 0, 32, 0, True)
            expert(1, 1, 32, XB // 2, False)
            with pe.Fori(1, NX // 2) as i:
                for s_e in range(2):
                    expert(2 * i + s_e, s_e, 32 * (i + 1), (2 * i + s_e) * (XB // 2), False)

        @block.vector
        def _(dve):
            dve.memset(e_src_i[96:P, :], PAD_NODE).then_inc(e_float, 1)
            dve.memset(e_dst_i[96:P, :], N - 1).then_inc(e_float, 1)
            dve.memset(e_w[96:P, :], 0.0).then_inc(e_float, 1)
            dve.memset(zeros[:, :], 0.0).then_inc(zeros_ok, 1)
            dve.memset(esplit[:, NCH:NCP, :], 0.0)
            dve.wait_ge(edges_in, 16 * 9)
            dve.tensor_copy(e_src, e_src_i).then_inc(e_float, 1)
            dve.tensor_copy(e_dst, e_dst_i).then_inc(e_float, 1)
            dve.wait_ge(const_made, N_CONST)
            dve.tensor_copy(iota_f[:, :], iota_i[:, :]).then_inc(prep, 1)
            dve.tensor_scalar(acc_dump[:, :], part_i[:, :], float(DUMP), None, ALU.add).then_inc(prep, 1)
            for n in range(2 * TG):
                last = dve.tensor_scalar(buf_dump[:, n:n + 1], part_i[:, :], float(BDUMP + n * P), None, ALU.add)
            last.then_inc(prep, 1)
            for c in range(COPIES):
                dve.tensor_scalar(acc_dump4[:, c:c + 1], part_i[:, :], float(DUMP + c * AR), None, ALU.add)
            dve.wait_ge(consts_in, 32)
            dve.tensor_scalar(neg_diag[:, :], neg_diag[:, :], -1.0, -1.0, ALU.mult, ALU.add).then_inc(prep, 1)
            dve.wait_ge(e_col, 3 * EQ)
            dve.tensor_copy(src_i, ecols[:, 0:NCH, 0]).then_inc(prep, 1)
            dve.tensor_copy(dcols[:, 0:NCH], ecols[:, 0:NCH, 2])
            dve.memset(dcols[:, NCH:NCP], 0)
            dve.wait_ge(prep, 5)
            dve.tensor_scalar(src_part, src_i, ~127, None, ALU.bitwise_and).then_inc(prep, 1)
            dve.tensor_scalar(src_i, src_i, 127, None, ALU.bitwise_and).then_inc(prep, 1)
            dve.wait_ge(prep, 7)
            dve.tensor_copy(esplit[:, 0:NCH, 0], src_part)
            dve.tensor_copy(esplit[:, 0:NCH, 1], src_i)
            dve.wait_ge(base_bc, 1)
            dve.tensor_scalar(base_f[:, :], bank(0, 0, NB), float(N - P), None, ALU.min).then_inc(prep, 1)
            dve.wait_ge(prep, 8)
            dve.tensor_copy(base_i[:, :], base_f[:, :])
            rel = ecols[:, 0:NCH, 2].rearrange("p (b c) -> p b c", c=BC)
            dve.tensor_tensor(rel, rel, base_f[:, :].unsqueeze(2).to_broadcast([P, NB, BC]), ALU.subtract).then_inc(prep, 1)
            dve.wait_ge(prep, 9)
            dve.tensor_reduce(spread[:, 0:1], ecols[:, 0:NCH, 2], AX_X, ALU.max)
            dve.tensor_reduce(spread[:, 1:2], ecols[:, 0:NCH, 2], AX_X, ALU.min).then_inc(prep, 1)
            dve.wait_ge(prep, 10)
            dve.tensor_scalar(spread[:, 2:3], spread[:, 0:1], float(P - 1), None, ALU.is_gt).then_inc(base_out, 1)
            dve.wait_ge(base_out, 1)
            dve.scalar_tensor_tensor(out=spread[:, 3:4], in0=spread[:, 1:2], scalar=0.0, in1=spread[:, 2:3], op0=ALU.is_lt, op1=ALU.max).then_inc(prep, 1)
            dve.wait_ge(flag_sum, 1)
            dve.tensor_copy(flag_i[:, :], bank(1, 0, 1)).then_inc(flag_ok, 1)

            def ln_group(j, h, peeled):
                dve.wait_ge(ln_in[h], 32 * (j // 2 + 1) if peeled else 32 * (lni[0] + 1))
                for t in range(TG):
                    last = dve.bn_stats(ln_stat[:, h, t, :], ln_x[:, h, t, :])
                last.then_inc(ln_step, 1)
                dve.wait_ge(ln_step, 2 * j + 1)
                dve.sem_inc(dve_passed, 1)
                for t in range(TG):
                    last = dve.bn_aggr(ln_mv[:, h, t, :], ln_stat[:, h, t, :])
                last.then_inc(ln_mean, 1)
                dve.wait_ge(ln_sq, j + 1)
                dve.reciprocal(ln_rstd[:, h, :], ln_std[:, h, :]).then_inc(ln_step, 1)
                dve.wait_ge(ln_step, 2 * j + 2)
                if not peeled:
                    dve.wait_ge(ln_out[h], 32 * lni[0])
                for t in range(TG):
                    last = dve.tensor_scalar(ln_n[:, h, t, :], ln_x[:, h, t, :], ln_mv[:, h, t, 0:1], ln_rstd[:, h, t:t + 1], ALU.subtract, ALU.mult)
                last.then_inc(ln_xn, 1)

            lni = [None]
            for h in range(2):
                ln_group(h, h, True)
            with dve.Fori(1, NG // 2) as i:
                lni[0] = i
                for h in range(2):
                    ln_group(2 * i + h, h, False)

            flag = dve.value_load(flag_i[0:1, 0:1], min_val=0, max_val=P)
            dve.wait_ge(ln_out[0], 32 * (NG // 2))
            dve.wait_ge(ln_out[1], 32 * (NG // 2))
            with dve.If(flag == 0):
                def match_group(s, par, g, peeled):
                    dve.wait_ge(bc_made, s + 1)
                    if not (peeled and g < 2):
                        dve.wait_ge(g_made, 2 * (s - 1))
                    for c in range(GC):
                        srcs = bank(par, c * P, (c + 1) * P)
                        dve.tensor_scalar(same_w[:, par, c, :], srcs, stage_e[:, par, c, 0:1], stage_e[:, par, c, 1:2], ALU.is_equal, ALU.mult)
                        dve.tensor_scalar(is_node[:, par, c, :], iota_f[:, :], stage_e[:, par, c, 2:3], None, ALU.is_equal).then_inc(oh_made, 1)
                    for c in range(GC):
                        last = dve.scalar_tensor_tensor(out=picked[:, par, c, :], in0=bank(par, c * P, (c + 1) * P), scalar=stage_e[:, par, c, 0:1],
                                                        in1=earlier[:, :], op0=ALU.is_equal, op1=ALU.mult, accum_out=sooner[:, par, c:c + 1])
                    dve.tensor_scalar(offs[:, par, :], stage_e[:, par, :, 0], acc_dump[:, 0:1], None, ALU.subtract).then_inc(idx_step, 1)
                    dve.wait_ge(idx_step, 2 * s + 1)
                    dve.scalar_tensor_tensor(out=idx_f[:, par, :], in0=sooner[:, par, :], scalar=0.0, in1=offs[:, par, :], op0=ALU.is_equal, op1=ALU.mult).then_inc(idx_step, 1)
                    dve.wait_ge(idx_step, 2 * s + 2)
                    if not (peeled and g < 2):
                        for c in range(COPIES):
                            dve.wait_ge(acc_add[c], 16 * (s - 1))
                    dve.tensor_tensor(idx_a[:, par, :], idx_f[:, par, :], acc_dump4[:, :], ALU.add).then_inc(idx_made, 1)

                for g in range(4):
                    match_group(g, g % 2, g, True)
                with dve.Fori(1, NGR // 4) as i:
                    for g in range(4):
                        match_group(4 * i + g, g % 2, g, False)
            with dve.Else():
                def general_match(s, first):
                    dve.wait_ge(gen_bc, s + 1)
                    if not first:
                        dve.wait_ge(gen_r, s)
                        for c in range(COPIES):
                            dve.wait_ge(gen_add[c], 16 * s)
                    for c in range(GC):
                        last = dve.tensor_scalar(same_w[:, 0, c, :], bank(0, c * P, (c + 1) * P), stage_e[:, 0, c, 0:1], stage_e[:, 0, c, 1:2], ALU.is_equal, ALU.mult)
                    last.then_inc(gen_same, 1)
                    for c in range(GC):
                        dve.scalar_tensor_tensor(out=picked[:, 0, c, :], in0=bank(0, c * P, (c + 1) * P), scalar=stage_e[:, 0, c, 0:1],
                                                 in1=earlier[:, :], op0=ALU.is_equal, op1=ALU.mult, accum_out=sooner[:, 0, c:c + 1])
                    dve.tensor_scalar(offs[:, 0, :], stage_e[:, 0, :, 0], acc_dump[:, 0:1], None, ALU.subtract).then_inc(gen_step, 1)
                    dve.wait_ge(gen_step, 2 * s + 1)
                    dve.scalar_tensor_tensor(out=idx_f[:, 0, :], in0=sooner[:, 0, :], scalar=0.0, in1=offs[:, 0, :], op0=ALU.is_equal, op1=ALU.mult).then_inc(gen_step, 1)
                    dve.wait_ge(gen_step, 2 * s + 2)
                    dve.tensor_tensor(idx_a[:, 0, :], idx_f[:, 0, :], acc_dump4[:, :], ALU.add).then_inc(gen_idx, 1)
                general_match(0, True)
                with dve.Fori(1, NGR) as s:
                    general_match(s, False)

            dve.wait_ge(scattered, 1)
            dve.wait_ge(late_in, 16 * 5)
            dve.memset(seen, 0.0)
            dve.memset(seenb, 0.0)

            def sum_copies(j, jn):
                def first_half(t):
                    dve.wait_ge(a_got[t], 16 * jn)
                    dve.tensor_tensor(half[:, t, :, :], a_in[:, t, 0:2, :], a_in[:, t, 2:4, :], ALU.add).then_inc(half_made, 1)
                first_half(0)
                for t in range(TG):
                    if t + 1 < TG:
                        first_half(t + 1)
                    dve.wait_ge(half_made, TG * j + t + 1)
                    dve.tensor_tensor(e4[:, t, :], half[:, t, 0, :], half[:, t, 1, :], ALU.add).then_inc(e4_made, 1)

            def node_group(j, h, first, last_group):
                dve.wait_ge(xb_made, j + 1)
                if not first:
                    dve.wait_ge(x1_out[h], first_fill[0])
                for t in range(TG + 1):
                    if t < TG:
                        dve.wait_ge(w_made, TG * j + min(TG, t - t % 2 + 2))
                        dve.tensor_tensor(x1[:, h, t, :], bank(t // 2, (t % 2) * D, (t % 2 + 1) * D), x_in[:, h, t, :], ALU.add).then_inc(x1_made, 1)
                    if t >= 1:
                        dve.wait_ge(x1_made, TG * j + t)
                        last = dve.bn_stats(st3[:, t - 1, :], x1[:, h, t - 1, :])
                last.then_inc(stat_made, 1)
                dve.wait_ge(stat_made, j + 1)
                dve.sem_inc(dve_passed, 1)
                for t in range(TG):
                    last = dve.bn_aggr(mv3[:, t, :], st3[:, t, :])
                last.then_inc(mv_made, 1)
                dve.wait_ge(std_made, j + 1)
                dve.reciprocal(rstd3[:, :], std3[:, :]).then_inc(rstd_made, 1)
                dve.wait_ge(rstd_made, j + 1)
                if not first:
                    dve.wait_ge(h_out[h], h_fill[0])
                for t in range(TG):
                    dve.tensor_scalar(hn[:, h, t, :], x1[:, h, t, :], mv3[:, t, 0:1], rstd3[:, t:t + 1], ALU.subtract, ALU.mult).then_inc(h_made, 1)
                if not last_group:
                    sum_copies(j + 1, j + 2)
                r0 = NR * j
                mx, sm, rc, prb, top, pos, kept, base, rowf, tmp, k2, sidx = c7
                dve.wait_ge(lg_made, TG * (j + 1))

                def step(ins, n):
                    ins.then_inc(route, 1)
                    dve.wait_ge(route, r0 + n)

                def wide(v):
                    return v.unsqueeze(2).to_broadcast([P, TG, NX])

                def rows8(v):
                    return v.unsqueeze(1).to_broadcast([P, TG, NX])
                vb = valid[:, bass.ds(j * TG, TG)]
                step(dve.tensor_tensor(lg[:, :, :], bank(6, 0, TG * NX).rearrange("p (a b) -> p a b", b=NX), rows8(gateb_t[:, :]), ALU.add), 1)
                step(dve.tensor_reduce(mx, lg[:, :, :], AX_X, ALU.max), 2)
                step(dve.tensor_tensor(t56[:, :, :], lg[:, :, :], wide(mx), ALU.subtract), 3)
                dve.wait_ge(exp_made, j + 1)
                step(dve.tensor_reduce(sm, pr[:, :, :], AX_X, ALU.add), 4)
                step(dve.reciprocal(rc, sm), 5)
                step(dve.tensor_tensor(pr[:, :, :], pr[:, :, :], wide(rc), ALU.mult), 6)
                step(dve.tensor_reduce(prb, pr[:, :, :], AX_X, ALU.max), 7)
                step(dve.tensor_tensor(t56[:, :, :], pr[:, :, :], wide(prb), ALU.is_equal), 8)
                step(dve.tensor_tensor(t56[:, :, :], t56[:, :, :], rows8(falling[:, :]), ALU.mult), 9)
                step(dve.tensor_reduce(top, t56[:, :, :], AX_X, ALU.max), 10)
                step(dve.tensor_tensor(oh[:, :, :], wide(top), rows8(falling[:, :]), ALU.is_equal), 11)
                step(dve.tensor_tensor(ohb[:, :, :], oh[:, :, :], vb.unsqueeze(2).to_broadcast([P, TG, NX]), ALU.mult), 12)
                dve.wait_ge(rank_made, j + 1)
                step(dve.tensor_tensor(t56[:, :, :], bank(7, 0, TG * NX).rearrange("p (a b) -> p a b", b=NX), ohb[:, :, :], ALU.mult), 13)
                step(dve.tensor_reduce(pos, t56[:, :, :], AX_X, ALU.add), 14)
                step(dve.tensor_reduce(new8[:, :], ohb[:, :, :].rearrange("p a b -> p b a"), AX_X, ALU.add), 15)
                dve.tensor_scalar(base, top, -float(C), float(NX * C - 1), ALU.mult, ALU.add)
                dve.tensor_scalar(tmp, pos, float(C), None, ALU.is_le)
                step(dve.tensor_scalar(rowf, pos, float(C), None, ALU.min), 16)
                dve.scalar_tensor_tensor(out=kept, in0=pos, scalar=0.0, in1=tmp, op0=ALU.is_gt, op1=ALU.mult)
                step(dve.tensor_tensor(rowf, rowf, base, ALU.add), 17)
                dve.tensor_tensor(y_scale[:, bass.ds(j * TG, TG)], prb, kept, ALU.mult)
                dve.tensor_scalar(gather_row[:, bass.ds(j * TG, TG)], rowf, 0.0, None, ALU.max)
                step(dve.tensor_tensor(k2, rowf, buf_dump[:, h * TG:(h + 1) * TG], ALU.subtract), 18)
                step(dve.tensor_tensor(sidx, k2, kept, ALU.mult), 19)
                dve.tensor_tensor(scat_i[:, h, 0:TG], sidx, buf_dump[:, h * TG:(h + 1) * TG], ALU.add).then_inc(slot_made, 1)
                step(dve.tensor_tensor(seen, seen, new8, ALU.add), 20)
                step(dve.tensor_copy(seenb, seen), 21)

            first_fill, h_fill = [None], [None]
            sum_copies(0, 1)
            node_group(0, 0, True, False)
            node_group(1, 1, True, False)
            with dve.Fori(1, NG // 2 - 1) as i:
                for h in range(2):
                    first_fill[0], h_fill[0] = 16 * i, 16 * TG * i
                    node_group(2 * i + h, h, False, False)
            for h in range(2):
                first_fill[0], h_fill[0] = 16 * (NG // 2 - 1), 16 * TG * (NG // 2 - 1)
                node_group(NG - 2 + h, h, False, h == 1)

            def expert_sum(e, b, first):
                n = e * XB + b
                s = b % 2
                if not (first and b < 2):
                    dve.wait_ge(y_out[s], yfill(e, b))
                for t in range(0, TB, 2):
                    dve.wait_ge(m2_made, 2 * n + t // 2 + 1)
                    full = min(2, max(0, (C - (b * TB + t) * P) // P))
                    ins = None
                    if full == 2:
                        ins = dve.tensor_tensor(y_sb[:, s, t:t + 2, :], bank(6 + t // 2).rearrange("p (a b) -> p a b", b=D),
                                                b2_t[:, bass.ds(e, 1), :].to_broadcast([P, 2, D]), ALU.add)
                    else:
                        for u in range(2):
                            w = min(P, C - (b * TB + t + u) * P)
                            ins = dve.tensor_tensor(y_sb[0:w, s, t + u, :], bank(6 + t // 2, u * D, (u + 1) * D)[0:w, :],
                                                    b2_t[0:w, bass.ds(e, 1), :].rearrange("p a d -> p (a d)"), ALU.add)
                    ins.then_inc(y_made, 1)

            def yfill(e, b):
                return 16 * TB * (e * (XB // 2) + b // 2)

            for b in range(XB):
                expert_sum(0, b, True)
            with dve.Fori(1, NX) as e:
                for b in range(XB):
                    expert_sum(e, b, False)

            dve.wait_ge(tok_copied, NX * XB + 1)
            dve.wait_ge(m2_made, 2 * NX * XB)
            dve.memset(big4, 10000.0).then_inc(lim_made, 1)
            dve.memset(neg4, -10000.0).then_inc(lim_made, 1)
            dve.wait_ge(lim_made, 2)

            def finish(j, h, first):
                f0 = NP_FIN * j
                dve.wait_ge(yg_in[h], yg_fill[0])
                for t in range(TG):
                    sc = y_scale[:, bass.ds(j * TG + t, 1)]
                    if not first and t == 0:
                        dve.wait_ge(o_out[h], o_fill[0])
                    dve.tensor_scalar(yp[:, h, t, :], yg[:, h, t, :], sc, 0.0, ALU.mult, ALU.max)
                    last = dve.tensor_scalar(yn[:, h, t, :], yg[:, h, t, :], sc, 0.0, ALU.mult, ALU.min)
                last.then_inc(fin_step, 2)
                dve.wait_ge(fin_step, f0 + 2)
                flat_p = yp[:, h, :, :].rearrange("p a b -> p (a b)")
                flat_n = yn[:, h, :, :].rearrange("p a b -> p (a b)")
                flat_m = over[:, :, :].rearrange("p a b -> p (a b)")
                dve.tensor_scalar(flat_m, flat_p, HUGE, None, ALU.is_gt).then_inc(fin_step, 1)
                dve.wait_ge(fin_step, f0 + 3)
                dve.sem_inc(dve_passed, 1)
                dve.copy_predicated(flat_p, flat_m, big4).then_inc(fin_step, 1)
                dve.wait_ge(fin_step, f0 + 4)
                dve.tensor_scalar(flat_m, flat_n, -HUGE, None, ALU.is_lt).then_inc(fin_step, 1)
                dve.wait_ge(fin_step, f0 + 5)
                dve.sem_inc(dve_passed, 1)
                dve.copy_predicated(flat_n, flat_m, neg4).then_inc(fin_step, 1)
                dve.wait_ge(fin_step, f0 + 6)
                dve.tensor_tensor(flat_p, flat_p, flat_n, ALU.add).then_inc(fin_step, 1)
                dve.wait_ge(fin_step, f0 + 7)
                dve.wait_ge(x1_in[h], x1_fill[0])
                dve.tensor_tensor(flat_p, flat_p, x1b[:, h, :, :].rearrange("p a b -> p (a b)"), ALU.add).then_inc(o_made, 1)

            yg_fill, o_fill, x1_fill = [None], [None], [None]
            for h in range(2):
                yg_fill[0], x1_fill[0] = 16 * TG, 16
                finish(h, h, True)
            with dve.Fori(1, NG // 2) as i:
                for h in range(2):
                    yg_fill[0], o_fill[0], x1_fill[0] = 16 * TG * (i + 1), 32 * i, 16 * (i + 1)
                    finish(2 * i + h, h, False)


_INS = ['x', 'src', 'dst', 'edge_weight', 'L0_gnn_weight', 'L0_gnn_learnable_diag', 'L0_gnn_bias',
        'L0_ffn_gate_w', 'L0_ffn_gate_b', 'L0_ffn_w1', 'L0_ffn_b1', 'L0_ffn_w2', 'L0_ffn_b2']
_OUTS = [((12500, 256), 'float32')]


def kernel(**inputs):
    import numpy as _np
    import concourse.bacc as _bacc
    from concourse import mybir as _mybir
    from concourse.bass_utils import run_bass_kernel_spmd as _run

    nc = _bacc.Bacc("TRN2", target_bir_lowering=False, num_devices=1)
    arrays, args = {}, []
    for name in _INS:
        a = _np.ascontiguousarray(inputs[name])
        arrays[f"in_{name}_dram"] = a
        args.append(nc.dram_tensor(f"in_{name}_dram", a.shape, _mybir.dt.from_np(a.dtype), kind="ExternalInput").ap())
    for i, (shape, dtype) in enumerate(_OUTS):
        dt = _mybir.dt.from_np(_np.dtype(dtype))
        args.append(nc.dram_tensor(f"out_{i}_dram", shape, dt, kind="ExternalOutput").ap())
    gnn_moe_layer(nc, *args)
    r = _run(nc, [arrays], core_ids=[0])
    got = tuple(r.results[0][f"out_{i}_dram"] for i in range(len(_OUTS)))
    return got[0]
```

```python
from contextlib import ExitStack

import concourse.bass as bass
from concourse import mybir

ALU = mybir.AluOpType
ACT = mybir.ActivationFunctionType
AX_X = mybir.AxisListType.X
F32 = mybir.dt.float32
BF16 = mybir.dt.bfloat16
F32R = mybir.dt.float32r
I32 = mybir.dt.int32
U32 = mybir.dt.uint32

P = 128
EPS = 1e-5
COPIES = 4
GC = 4
BC = 8
TG = 7
HUGE = 3.4028234663852886e38


def gnn_moe_layer(nc, x, src, dst, edge_weight, gnn_w, gnn_diag, gnn_bias, gate_w, gate_b,
                  w1, b1, w2, b2, out):
    N, D = x.shape
    E = src.shape[0]
    NX, _, F = w1.shape
    C = max(1, -(-5 * N // (4 * NX)))
    KD = D // P
    KF = F // P

    EQ = -(-E // (P * P))
    EP = EQ * P
    NCH = P * EQ
    NGR = NCH // GC
    NB = NCH // BC
    assert NCH % (2 * BC) == 0
    EFULL = E // EP
    EREST = E - EFULL * EP
    assert 96 <= EFULL == P - 1 and EREST > 0

    NT = -(-N // P)
    NREST = N - (NT - 1) * P
    NG = NT // TG
    assert NG * TG == NT and NG % 2 == 0
    PAD_NODE = N
    DUMP = N + 1
    AR = (NT + 1) * P
    ZR = 11
    assert AR // P % ZR == 0 and DUMP + P <= AR

    TB = 4
    XT = -(-C // P)
    XB = -(-XT // TB)
    assert XT == XB * TB and XB == 4 and NX % 2 == 0 and KD == 2
    BDUMP = NX * C
    ZB = 2
    BZ = -(-(NX * C + max(TB, 2 * TG) * P) // (P * ZB))
    BR = BZ * P * ZB
    assert BZ < NB // 2

    acc_dram = nc.dram_tensor("acc_dram", (COPIES, AR, D), F32)
    acc_flat = acc_dram[:, :, :].rearrange("k r d -> (k r) d")
    xs_dram = nc.dram_tensor("xs_dram", (NT * P, D), F32)
    x1_dram = nc.dram_tensor("x1_dram", (NT * P, D), F32)
    buf_dram = nc.dram_tensor("buf_dram", (BR, D), F32)
    y_dram = nc.dram_tensor("y_dram", (NX * C, D), F32)

    with ExitStack() as ctx:
        def sb(name, shape, dt=F32):
            return ctx.enter_context(nc.sbuf_tensor(name, shape, dt))

        def sem(name):
            return ctx.enter_context(nc.semaphore(name))

        ident = sb("ident", [P, P])
        identb = sb("identb", [P, P], BF16)
        earlier = sb("earlier", [P, P])
        upto = sb("upto", [P, P], BF16)
        onesb = sb("onesb", [P, P], BF16)
        onesf = sb("onesf", [P, P])
        row0 = sb("row0", [P, P])
        iota_i = sb("iota_i", [P, P], I32)
        iota_f = sb("iota_f", [P, P])
        part_i = sb("part_i", [P, 1], I32)
        acc_dump = sb("acc_dump", [P, 1])
        acc_dump4 = sb("acc_dump4", [P, COPIES])
        buf_dump = sb("buf_dump", [P, 2 * TG])
        falling = sb("falling", [P, NX])
        valid = sb("valid", [P, NT])
        eps_t = sb("eps_t", [P, 1])
        zeros = sb("zeros", [P, ZR * D])
        neg_diag = sb("neg_diag", [P, D])
        bias_t = sb("bias_t", [P, D])
        gateb_t = sb("gateb_t", [P, NX])
        w_sb = sb("w_sb", [P, KD, D])
        gate_sb = sb("gate_sb", [P, KD, NX])
        b1_rows = sb("b1_rows", [NX * KF, P])
        b1_t = sb("b1_t", [P, NX * KF])
        b2_t = sb("b2_t", [P, NX, D])
        gather_row = sb("gather_row", [P, NT], I32)
        y_scale = sb("y_scale", [P, NT])

        zero_sum = sb("zero_sum", [P, 1])
        zero_part = sb("zero_part", [P, 1])
        y_zero = sb("y_zero", [P, D])
        fine_i = sb("fine_i", [P, 1], I32)

        base_f = sb("base_f", [P, NB])
        base_i = sb("base_i", [P, NB], I32)
        spread = sb("spread", [P, 4])
        flag_i = sb("flag_i", [P, 1], I32)

        REGION = 37000
        region_at = -(-nc.sbuf_base // 32) * 32
        big = sb("big", [P, REGION])
        assert region_at + 4 * REGION <= nc.sbuf_base

        def region(start=0):
            at = [start]

            def take(shape, dt=F32, name=None):
                n = 1
                for s in shape:
                    n *= s
                n = n * (2 if dt == BF16 else 4) // 4
                at[0] += n
                assert at[0] <= REGION
                if dt == F32R:
                    at_byte = region_at + 4 * (at[0] - n)
                    return nc.alloc_sbuf_tensor_at(name, [P] + shape, F32R, offset=at_byte)
                v = big[:, at[0] - n:at[0]]
                if dt != F32:
                    v = v.bitcast(dt)
                if len(shape) == 1:
                    return v
                names = "abcd"[:len(shape)]
                return v.rearrange(f"p ({' '.join(names)}) -> p {' '.join(names)}",
                                   **dict(zip(names[1:], shape[1:])))
            return take

        NCP = NCH + GC
        r = region()
        ecols = r([NCP, 3])
        esplit = r([NCP, 2], BF16)
        dcols = r([NCP], I32)
        cols_end = NCP * 5
        r = region(cols_end)
        e_src_i, e_dst_i, e_w = r([EP], I32), r([EP], I32), r([EP])
        e_src, e_dst = r([EP]), r([EP])
        src_i, src_part = r([NCH], I32), r([NCH], I32)
        ln_x, ln_n, ln_s = r([2, TG, D]), r([2, TG, D]), r([2, TG, D])
        ln_stat, ln_mv, ln_std, ln_rstd = r([2, TG, 6]), r([2, TG, 2]), r([2, TG]), r([2, TG])
        r = region(cols_end)
        stage_e, stage_s, stage_d = r([2, GC, 3]), r([2, GC, 2], BF16), r([GC], I32)
        same_w, is_node, g_sb = r([2, GC, P]), r([2, GC, P]), r([2, GC, P])
        rows, window = r([2, GC, D]), r([2, D])
        picked, sooner, offs, idx_f = r([2, GC, P]), r([2, GC]), r([2, GC]), r([2, GC])
        idx_a = r([2, GC], I32)
        gathered = r([GC, D])
        r = region()
        a_in, half, e4 = r([TG, COPIES, D]), r([TG, 2, D]), r([TG, D])
        x_in, x1 = r([2, TG, D]), r([2, TG, D])
        hn = r([2, TG, D])
        e4t, hnt = r([2, KD, P]), r([2, KD, P])
        st3, mv3, std3, rstd3 = r([TG, 6]), r([TG, 2]), r([TG]), r([TG])
        lg, pr, oh, t56 = r([TG, NX]), r([TG, NX]), r([TG, NX]), r([TG, NX])
        ohb = r([TG, NX], BF16)
        seen, seenb, new8 = r([NX]), r([NX], BF16), r([NX])
        c7 = [r([TG]) for _ in range(12)]
        scat_i = r([2, TG + 1], I32)
        r = region()
        w1_in_sb, w2_in_sb = r([KD, F]), r([KF, D])
        w1_hi, w1_lo = r([2, KD, F], F32R, "w1_hi"), r([2, KD, F], F32R, "w1_lo")
        w2_hi, w2_lo = r([2, KF, D], F32R, "w2_hi"), r([2, KF, D], F32R, "w2_lo")
        tok, tokT = r([2, TB, D]), r([KD, TB * P])
        tok_hi, tok_lo = r([KD, TB * P], F32R, "tok_hi"), r([KD, TB * P], F32R, "tok_lo")
        hid = r([2, TB * P])
        hid_hi, hid_lo = r([KF, TB * P], F32R, "hid_hi"), r([KF, TB * P], F32R, "hid_lo")
        y_sb = r([2, TB, D])
        r = region()
        yg, x1b = r([2, TG, D]), r([2, TG, D])
        yp, yn = r([2, TG, D]), r([2, TG, D])
        over, big4, neg4 = r([TG, D], U32), r([TG * D]), r([TG * D])
        gidx = r([2, TG + 1], I32)

        ps = ctx.enter_context(nc.psum_tensor("ps", [P, 8 * 512], F32))

        def bank(n, lo=0, hi=512):
            return ps[:, n * 512 + lo:n * 512 + hi]

        edges_in, consts_in, late_in, const_made = sem("edges_in"), sem("consts_in"), sem("late_in"), sem("const_made")
        pool_step = sem("pool_step")
        e_float, e_turned, e_col = sem("e_float"), sem("e_turned"), sem("e_col")
        prep, base_bc, base_out, flag_sum, flag_ok = sem("prep"), sem("base_bc"), sem("base_out"), sem("flag_sum"), sem("flag_ok")
        b1_turned, b1_ok = sem("b1_turned"), sem("b1_ok")
        zeros_ok, acc_zero, buf_zero = sem("zeros_ok"), sem("acc_zero"), sem("buf_zero")
        ln_in = [sem(f"ln_in{i}") for i in range(2)]
        ln_step, ln_sq, ln_xn, ln_xs = sem("ln_step"), sem("ln_sq"), sem("ln_xn"), sem("ln_xs")
        ln_mean = sem("ln_mean")
        ln_out = [sem(f"ln_out{i}") for i in range(2)]
        staged, bc_made, oh_made, g_made, g_copied = sem("staged"), sem("bc_made"), sem("oh_made"), sem("g_made"), sem("g_copied")
        r_made, r_copied, idx_step, idx_made = sem("r_made"), sem("r_copied"), sem("idx_step"), sem("idx_made")
        win_in = [sem(f"win_in{i}") for i in range(2)]
        acc_add = [sem(f"acc_add{i}") for i in range(COPIES)]
        gen_add = [sem(f"gen_add{i}") for i in range(COPIES)]
        gen_in = [sem(f"gen_in{i}") for i in range(GC)]
        gen_staged, gen_bc, gen_same, gen_idx, gen_step, gen_r, gen_rc = (
            sem(n) for n in ("gen_staged", "gen_bc", "gen_same", "gen_idx", "gen_step", "gen_r", "gen_rc"))
        scattered = sem("scattered")
        a_got = [sem(f"a_got{i}") for i in range(TG)]
        x_got = [sem(f"x_got{i}") for i in range(2)]
        half_made, e4_made, e4_turned, e4_copied, w_made = sem("half_made"), sem("e4_made"), sem("e4_turned"), sem("e4_copied"), sem("w_made")
        xb_made, x1_made, stat_made, mv_made, std_made, rstd_made = (
            sem(n) for n in ("xb_made", "x1_made", "stat_made", "mv_made", "std_made", "rstd_made"))
        h_made, h_turned, h_copied, lg_made = sem("h_made"), sem("h_turned"), sem("h_copied"), sem("lg_made")
        x1_out = [sem(f"x1_out{i}") for i in range(2)]
        route, exp_made, rank_made, slot_made = sem("route"), sem("exp_made"), sem("rank_made"), sem("slot_made")
        h_out = [sem(f"h_out{i}") for i in range(2)]
        w1_in, w2_in, w_hi_made, w_split = sem("w1_in"), sem("w2_in"), sem("w_hi_made"), sem("w_split")
        tok_hi_made, tok_split, hid_hi_made, hid_split = (
            sem(n) for n in ("tok_hi_made", "tok_split", "hid_hi_made", "hid_split"))
        tok_in = [sem(f"tok_in{i}") for i in range(2)]
        tok_turned, tok_copied, m1_made, hid_made, m2_made, y_made = (
            sem(n) for n in ("tok_turned", "tok_copied", "m1_made", "hid_made", "m2_made", "y_made"))
        y_out = [sem(f"y_out{i}") for i in range(2)]
        gidx_made, check_step, fine_sum = sem("gidx_made"), sem("check_step"), sem("fine_sum")
        yg_in = [sem(f"yg_in{i}") for i in range(2)]
        x1_in = [sem(f"x1_in{i}") for i in range(2)]
        lim_made, fin_step, o_made = sem("lim_made"), sem("fin_step"), sem("o_made")
        o_out = [sem(f"o_out{i}") for i in range(2)]

        NR = 21
        N_CONST = 13
        NP_FIN = 6

        pool_passed, act_passed, dve_passed = sem("pool_passed"), sem("act_passed"), sem("dve_passed")

        block = ctx.enter_context(nc.Block())

        @block.sync
        def _(sp):
            def edge_load(dst_t, src_d):
                v = src_d[0:EFULL * EP].rearrange("(q n) -> q n", n=EP)
                cut = EFULL // 16 * 16
                sp.dma_start(dst_t[0:cut, :], v[0:cut, :]).then_inc(edges_in, 16)
                sp.dma_start(dst_t[cut:EFULL, :], v[cut:EFULL, :]).then_inc(edges_in, 16)
                sp.dma_start(dst_t[EFULL:P, 0:EREST], src_d[EFULL * EP:E].rearrange("(q n) -> q n", q=1)).then_inc(edges_in, 16)

            sp.wait_ge(e_float, 3)
            edge_load(e_src_i, src)
            edge_load(e_dst_i, dst)
            edge_load(e_w, edge_weight)
            sp.dma_start(neg_diag[:, :], gnn_diag.rearrange("(q n) -> q n", q=1).to_broadcast([P, D])).then_inc(consts_in, 16)
            sp.dma_start(b1_rows[:, :], b1.rearrange("e (m p) -> (e m) p", p=P)).then_inc(consts_in, 16)

            def ln_load(j, slot, tail):
                if tail:
                    sp.dma_start(ln_x[:, slot, 0:TG - 1, :], x[(NT - TG) * P:(NT - 1) * P, :].rearrange("(t p) d -> p t d", p=P)).then_inc(ln_in[slot], 16)
                    sp.dma_start(ln_x[0:NREST, slot, TG - 1, :], x[(NT - 1) * P:N, :]).then_inc(ln_in[slot], 16)
                else:
                    a = TG - 1
                    sp.dma_start(ln_x[:, slot, 0:a, :], x[bass.ds(j * (TG * P), a * P), :].rearrange("(t p) d -> p t d", p=P)).then_inc(ln_in[slot], 16)
                    sp.dma_start(ln_x[:, slot, a, :], x[bass.ds(j * (TG * P) + a * P, P), :]).then_inc(ln_in[slot], 16)

            def ln_store(j, slot):
                sp.wait_ge(ln_xn, j + 1)
                sp.dma_start(acc_dram[0, bass.ds(j * (TG * P), TG * P), :].rearrange("(t p) d -> p t d", p=P), ln_n[:, slot, :, :]).then_inc(ln_out[slot], 16)
                sp.wait_ge(ln_xs, j + 1)
                sp.dma_start(xs_dram[bass.ds(j * (TG * P), TG * P), :].rearrange("(t p) d -> p t d", p=P), ln_s[:, slot, :, :]).then_inc(ln_out[slot], 16)

            ln_load(0, 0, False)
            ln_load(1, 1, False)

            def ln_pair(i, tail):
                for h in range(2):
                    sp.wait_ge(ln_xn, 2 * i + h + 1)
                    ln_load(2 * i + h + 2, h, tail and h == 1)
                    ln_store(2 * i + h, h)

            with sp.Fori(0, NG // 2 - 2) as i:
                ln_pair(i, False)
            ln_pair(NG // 2 - 2, True)
            ln_store(NG - 2, 0)
            ln_store(NG - 1, 1)
            sp.dma_start(bias_t[:, :], gnn_bias.rearrange("(q n) -> q n", q=1).to_broadcast([P, D])).then_inc(late_in, 16)
            sp.dma_start(gateb_t[:, :], gate_b.rearrange("(q n) -> q n", q=1).to_broadcast([P, NX])).then_inc(late_in, 16)
            sp.dma_start(w_sb[:, :, :], gnn_w.rearrange("(k p) n -> p k n", p=P)).then_inc(late_in, 16)
            sp.dma_start(gate_sb[:, :, :], gate_w.rearrange("(k p) n -> p k n", p=P)).then_inc(late_in, 16)
            sp.dma_start(b2_t[:, :, :], b2.rearrange("(q e) n -> q e n", q=1).to_broadcast([P, NX, D])).then_inc(late_in, 16)
            for s in range(2):
                sp.wait_ge(ln_out[s], 32 * (NG // 2))

            sp.wait_ge(flag_ok, 1)
            flag = sp.value_load(flag_i[0:1, 0:1], min_val=0, max_val=P)
            buf_rows = buf_dram[:, :].rearrange("(z p n) d -> z p (n d)", p=P, n=ZB)
            with sp.If(flag == 0):
                def window_load(b, slot, first):
                    if not first:
                        sp.wait_ge(r_made, 4 * (b - 1))
                    base = sp.value_load(base_i[0:1, bass.ds(b, 1)], min_val=0, max_val=N - P)
                    sp.dma_start(window[:, slot, :], xs_dram[bass.ds(base, P), :]).then_inc(win_in[slot], 16)

                for h in range(2):
                    window_load(h, h, True)
                with sp.Fori(1, 1 + BZ) as i:
                    sp.dma_start(buf_rows[bass.ds(i - 1, 1), :, :].rearrange("z p n -> p (z n)"), zeros[:, 0:ZB * D]).then_inc(buf_zero, 16)
                    for h in range(2):
                        window_load(2 * i + h, h, False)
                with sp.Fori(1 + BZ, NB // 2) as i:
                    for h in range(2):
                        window_load(2 * i + h, h, False)
            with sp.Else():
                with sp.Fori(0, BZ) as z:
                    sp.dma_start(buf_rows[bass.ds(z, 1), :, :].rearrange("z p n -> p (z n)"), zeros[:, 0:ZB * D]).then_inc(buf_zero, 16)

            sp.wait_ge(scattered, 1)
            def node_load(j, h, first, tail):
                if not first:
                    sp.wait_ge(x1_made, TG * (j - 1))
                if tail:
                    sp.dma_start(x_in[:, h, 0:TG - 1, :], x[(NT - TG) * P:(NT - 1) * P, :].rearrange("(t p) d -> p t d", p=P)).then_inc(x_got[h], 16)
                    sp.dma_start(x_in[0:NREST, h, TG - 1, :], x[(NT - 1) * P:N, :]).then_inc(x_got[h], 16)
                else:
                    a = TG - 1
                    sp.dma_start(x_in[:, h, 0:a, :], x[bass.ds(j * (TG * P), a * P), :].rearrange("(t p) d -> p t d", p=P)).then_inc(x_got[h], 16)
                    sp.dma_start(x_in[:, h, a, :], x[bass.ds(j * (TG * P) + a * P, P), :]).then_inc(x_got[h], 16)
                for t in range(TG):
                    if not (first and h == 0):
                        sp.wait_ge(half_made, TG * (j - 1) + t + 1)
                    sp.dma_start(a_in[:, t, :, :], acc_dram[:, bass.ds(j * (TG * P) + t * P, P), :].rearrange("k p d -> p k d")).then_inc(a_got[t], 16)

            def x1_store(j, h):
                sp.wait_ge(x1_made, TG * (j + 1))
                sp.dma_start(x1_dram[bass.ds(j * (TG * P), TG * P), :].rearrange("(t p) d -> p t d", p=P), x1[:, h, :, :]).then_inc(x1_out[h], 16)

            node_load(0, 0, True, False)
            node_load(1, 1, True, False)

            def node_pair(i, tail):
                for h in range(2):
                    x1_store(2 * i + h, h)
                    node_load(2 * i + h + 2, h, False, tail and h == 1)

            with sp.Fori(0, NG // 2 - 2) as i:
                node_pair(i, False)
            node_pair(NG // 2 - 2, True)
            x1_store(NG - 2, 0)
            x1_store(NG - 1, 1)
            for s in range(2):
                sp.wait_ge(x1_out[s], 16 * (NG // 2))
                sp.wait_ge(h_out[s], 16 * TG * (NG // 2))

            def w1_load(e, split):
                if split is not None:
                    sp.wait_ge(w_split, split)
                sp.dma_start(w1_in_sb, w1[bass.ds(e, 1), :, :].rearrange("e (k p) n -> p (e k) n", p=P)).then_inc(w1_in, 16)

            def w2_load(e, split):
                if split is not None:
                    sp.wait_ge(w_split, split)
                sp.dma_start(w2_in_sb, w2[bass.ds(e, 1), :, :].rearrange("e (k p) n -> p (e k) n", p=P)).then_inc(w2_in, 16)

            def tokens_load(e, b, first):
                s = b % 2
                if not (first and b < 2):
                    sp.wait_ge(tok_turned, e * XB + b - 1)
                sp.dma_start(tok[:, s, :, :], buf_dram[bass.ds(e * C + b * (TB * P), TB * P), :].rearrange("(t p) d -> p t d", p=P)).then_inc(tok_in[s], 16)

            def expert_loads(e, first, last):
                tokens_load(e, 0, first)
                if not last:
                    w1_load(e + 1, XB * e + XB // 2)
                tokens_load(e, 1, first)
                tokens_load(e, 2, first)
                if not last:
                    w2_load(e + 1, XB * (e + 1))
                for b in range(3, XB):
                    tokens_load(e, b, first)

            w1_load(0, None)
            w2_load(0, None)
            expert_loads(0, True, False)
            with sp.Fori(1, NX - 1) as e:
                expert_loads(e, False, False)
            expert_loads(NX - 1, False, True)
            tokens_load(NX, 0, False)

            for s in range(2):
                sp.wait_ge(y_out[s], 16 * TB * (NX * XB // 2))
            sp.wait_ge(tok_copied, NX * XB + 1)
            def x1_load(j, h, first):
                if not first:
                    sp.wait_ge(o_made, j - 1)
                sp.dma_start(x1b[:, h, :, :], x1_dram[bass.ds(j * (TG * P), TG * P), :].rearrange("(t p) d -> p t d", p=P)).then_inc(x1_in[h], 16)

            def out_store(j, h, tail):
                sp.wait_ge(o_made, j + 1)
                if tail:
                    sp.dma_start(out[(NT - TG) * P:(NT - 1) * P, :].rearrange("(t p) d -> p t d", p=P), yp[:, h, 0:TG - 1, :]).then_inc(o_out[h], 16)
                    sp.dma_start(out[(NT - 1) * P:N, :], yp[0:NREST, h, TG - 1, :]).then_inc(o_out[h], 16)
                else:
                    a = TG - 1
                    sp.dma_start(out[bass.ds(j * (TG * P), a * P), :].rearrange("(t p) d -> p t d", p=P), yp[:, h, 0:a, :]).then_inc(o_out[h], 16)
                    sp.dma_start(out[bass.ds(j * (TG * P) + a * P, P), :], yp[:, h, a, :]).then_inc(o_out[h], 16)

            x1_load(0, 0, True)
            x1_load(1, 1, True)
            with sp.Fori(0, NG // 2 - 1) as i:
                for h in range(2):
                    out_store(2 * i + h, h, False)
                    x1_load(2 * i + h + 2, h, False)
            out_store(NG - 2, 0, False)
            out_store(NG - 1, 1, True)
            for s in range(2):
                sp.wait_ge(o_out[s], 32 * (NG // 2))

        @block.gpsimd
        def _(pool):
            pool.memset(ident[:, :], 0.0).then_inc(pool_step, 1)
            pool.memset(identb[:, :], 0.0).then_inc(pool_step, 1)
            pool.memset(earlier[:, :], 1.0).then_inc(pool_step, 1)
            pool.memset(upto[:, :], 1.0).then_inc(pool_step, 1)
            pool.memset(row0[:, :], 0.0).then_inc(pool_step, 1)
            pool.memset(valid[:, :], 1.0).then_inc(pool_step, 1)
            pool.memset(onesb[:, :], 1.0).then_inc(const_made, 1)
            pool.memset(onesf[:, :], 1.0).then_inc(const_made, 1)
            pool.memset(eps_t[:, :], EPS).then_inc(const_made, 1)
            pool.iota(iota_i[:, :], pattern=[[1, P]], base=0, channel_multiplier=0).then_inc(const_made, 1)
            pool.iota(part_i[:, :], pattern=[[0, 1]], base=0, channel_multiplier=1).then_inc(const_made, 1)
            for e in range(NX):
                last = pool.memset(falling[:, e:e + 1], float(NX - e))
            last.then_inc(const_made, 1)
            pool.wait_ge(pool_step, 6)
            for t in (ident, identb):
                pool.affine_select(out=t[:, :], in_=t[:, :], compare_op=ALU.not_equal, fill=1.0, base=0,
                                   pattern=[[1, P]], channel_multiplier=-1).then_inc(const_made, 1)
            pool.affine_select(out=earlier[:, :], in_=earlier[:, :], compare_op=ALU.is_gt, fill=0.0, base=0,
                               pattern=[[-1, P]], channel_multiplier=1).then_inc(const_made, 1)
            pool.affine_select(out=upto[:, :], in_=upto[:, :], compare_op=ALU.is_ge, fill=0.0, base=0,
                               pattern=[[1, P]], channel_multiplier=-1).then_inc(const_made, 1)
            pool.memset(row0[0:1, :], 1.0).then_inc(const_made, 1)
            pool.affine_select(out=valid[:, NT - 1:NT], in_=valid[:, NT - 1:NT], compare_op=ALU.is_ge, fill=0.0,
                               base=NREST - 1, pattern=[[0, 1]], channel_multiplier=-1).then_inc(const_made, 1)
            pool.memset(ecols[:, NCH:NCP, :], 0.0).then_inc(const_made, 1)

            def ln_scale(j, h, stored):
                pool.wait_ge(ln_xn, j + 1)
                if stored is not None:
                    pool.wait_ge(ln_out[h], stored)
                pool.tensor_tensor(ln_s[:, h, :, :], ln_n[:, h, :, :],
                                   neg_diag[:, :].unsqueeze(1).to_broadcast([P, TG, D]), ALU.mult).then_inc(ln_xs, 1)

            pool.wait_ge(prep, 4)
            for h in range(2):
                ln_scale(h, h, None)
            with pool.Fori(1, NG // 2) as i:
                for h in range(2):
                    ln_scale(2 * i + h, h, 32 * i)

            pool.wait_ge(acc_zero, 16 * ((COPIES - 1) * (AR // P // ZR) + (AR // P - NT)))
            for s in range(2):
                pool.wait_ge(ln_out[s], 32 * (NG // 2))
            pool.wait_ge(flag_ok, 1)
            flag = pool.value_load(flag_i[0:1, 0:1], min_val=0, max_val=P)
            with pool.If(flag == 0):
                def scatter_group(s, par, first):
                    pool.wait_ge(idx_made, s + 1)
                    for c in range(GC):
                        if c % 2 == 0:
                            pool.wait_ge(r_copied, 2 * s + c // 2 + 1)
                        if not first:
                            pool.wait_ge(acc_add[c], 16 * s)
                        pool.sem_inc(pool_passed, 1)
                        pool.indirect_dma_start(
                            out=acc_flat, out_offset=bass.IndirectOffsetOnAxis(ap=idx_a[:, par, c:c + 1], axis=0),
                            in_=rows[:, par, c, :], in_offset=None, compute_op=ALU.add).then_inc(acc_add[c], 16)

                for g in range(4):
                    scatter_group(g, g % 2, g == 0)
                with pool.Fori(1, NGR // 4) as i:
                    for g in range(4):
                        scatter_group(4 * i + g, g % 2, False)
                for c in range(COPIES):
                    pool.wait_ge(acc_add[c], 16 * NGR)
            with pool.Else():
                def general_group(s, first):
                    pool.wait_ge(gen_staged, s + 1)
                    if not first:
                        pool.wait_ge(gen_r, s)
                    pool.sem_inc(pool_passed, 1)
                    for c in range(GC):
                        pool.indirect_dma_start(
                            out=gathered[:, c, :], out_offset=None, in_=xs_dram[:, :],
                            in_offset=bass.IndirectOffsetOnAxis(ap=stage_d[:, c:c + 1], axis=0)).then_inc(gen_in[c], 16)
                    pool.wait_ge(gen_idx, s + 1)
                    pool.wait_ge(gen_rc, s + 1)
                    pool.sem_inc(pool_passed, 1)
                    for c in range(GC):
                        pool.indirect_dma_start(
                            out=acc_flat, out_offset=bass.IndirectOffsetOnAxis(ap=idx_a[:, 0, c:c + 1], axis=0),
                            in_=rows[:, 0, c, :], in_offset=None, compute_op=ALU.add).then_inc(gen_add[c], 16)
                    for c in range(COPIES):
                        pool.wait_ge(gen_add[c], 16 * (s + 1))
                general_group(0, True)
                with pool.Fori(1, NGR) as s:
                    general_group(s, False)
            pool.sem_inc(scattered, 1)

            pool.wait_ge(late_in, 16 * 5)

            def add_bias(j, h, got):
                pool.wait_ge(x_got[h], got)
                pool.tensor_tensor(x_in[:, h, :, :], x_in[:, h, :, :],
                                   bias_t[:, :].unsqueeze(1).to_broadcast([P, TG, D]), ALU.add).then_inc(xb_made, 1)

            def send_tokens(j, h):
                pool.wait_ge(slot_made, j + 1)
                pool.wait_ge(buf_zero, 16 * BZ)
                pool.sem_inc(pool_passed, 1)
                for t in range(TG):
                    pool.indirect_dma_start(
                        out=buf_dram[:, :], out_offset=bass.IndirectOffsetOnAxis(ap=scat_i[:, h, t:t + 1], axis=0),
                        in_=hn[:, h, t, :], in_offset=None).then_inc(h_out[h], 16)

            add_bias(0, 0, 32)
            add_bias(1, 1, 32)
            with pool.Fori(0, NG // 2 - 1) as i:
                for h in range(2):
                    add_bias(2 * i + h + 2, h, 32 * (i + 2))
                    send_tokens(2 * i + h, h)
            send_tokens(NG - 2, 0)
            send_tokens(NG - 1, 1)

            def y_store(e, b):
                s = b % 2
                pool.wait_ge(y_made, 2 * (e * XB + b + 1))
                for t in range(TB):
                    n = min(P, C - (b * TB + t) * P)
                    pool.dma_start(y_dram[bass.ds(e * C + (b * TB + t) * P, n), :], y_sb[0:n, s, t, :]).then_inc(y_out[s], 16)

            with pool.Fori(0, NX) as e:
                for b in range(XB):
                    y_store(e, b)

            for s in range(2):
                pool.wait_ge(y_out[s], 16 * TB * (NX * XB // 2))
            pool.wait_ge(tok_copied, NX * XB + 1)

            def gather_y(j, h, first):
                if not first:
                    pool.wait_ge(o_made, j - 1)
                pool.tensor_copy(gidx[:, h, 0:TG], gather_row[:, bass.ds(j * TG, TG)]).then_inc(gidx_made, 1)
                pool.wait_ge(gidx_made, j + 1)
                pool.sem_inc(pool_passed, 1)
                for t in range(TG):
                    pool.indirect_dma_start(
                        out=yg[:, h, t, :], out_offset=None, in_=y_dram[:, :],
                        in_offset=bass.IndirectOffsetOnAxis(ap=gidx[:, h, t:t + 1], axis=0)).then_inc(yg_in[h], 16)

            for h in range(2):
                gather_y(h, h, True)
            with pool.Fori(1, NG // 2) as i:
                for h in range(2):
                    gather_y(2 * i + h, h, False)

        @block.scalar
        def _(act):
            act.wait_ge(zeros_ok, 1)
            nz = AR // P // ZR
            for k in range(1, COPIES):
                v = acc_dram[k, :, :].rearrange("(p n) d -> p (n d)", p=P)
                for z in range(nz):
                    act.dma_start(v[:, z * ZR * D:(z + 1) * ZR * D], zeros[:, :]).then_inc(acc_zero, 16)
            for z in range(0, AR - NT * P, P):
                act.dma_start(acc_dram[0, NT * P + z:NT * P + z + P, :], zeros[:, 0:D]).then_inc(acc_zero, 16)

            for k in range(EQ):
                for a in range(3):
                    n = 3 * k + a
                    act.wait_ge(e_turned, n + 1)
                    q = bank(n % 4, 0, P)
                    act.copy(ecols[:, k:NCH:EQ, a], q).then_inc(e_col, 1)
            act.wait_ge(b1_turned, 1)
            act.copy(b1_t[:, :], bank(4, 0, NX * KF)).then_inc(b1_ok, 1)

            act.wait_ge(const_made, N_CONST)
            with act.Fori(0, NG // 2) as i:
                for h in range(2):
                    act.wait_ge(ln_mean, 2 * i + h + 1)
                    act.activation(ln_std[:, h, :], ln_mv[:, h, :, 1], ACT.Sqrt, bias=eps_t[:, 0:1]).then_inc(ln_sq, 1)

            act.wait_ge(flag_ok, 1)
            flag = act.value_load(flag_i[0:1, 0:1], min_val=0, max_val=P)
            act.wait_ge(ln_out[0], 32 * (NG // 2))
            act.wait_ge(ln_out[1], 32 * (NG // 2))
            with act.If(flag == 0):
                def stage(s, par):
                    act.copy(stage_s[:, par, :, :], esplit[:, bass.ds(s * GC, GC), :])
                    act.copy(stage_e[:, par, :, :], ecols[:, bass.ds(s * GC, GC), :]).then_inc(staged, 1)

                def copy_group(s, par, g, peeled):
                    if not (peeled and g == 0):
                        act.wait_ge(idx_made, s)
                    stage(s + 1, 1 - par)
                    for c in range(2):
                        act.wait_ge(g_made, 2 * s + c + 1)
                        if not (peeled and g < 2):
                            act.wait_ge(r_made, 2 * (s - 1))
                        act.copy(g_sb[:, par, 2 * c:2 * c + 2, :], bank(2 + c, 0, 2 * P).rearrange("p (a b) -> p a b", b=P)).then_inc(g_copied, 1)
                    for c in range(2):
                        act.wait_ge(r_made, 2 * s + c + 1)
                        if not (peeled and g < 2):
                            for k in (2 * c, 2 * c + 1):
                                act.wait_ge(acc_add[k], 16 * (s - 1))
                        act.copy(rows[:, par, 2 * c:2 * c + 2, :], bank(4 + 2 * par + c).rearrange("p (a b) -> p a b", b=D)).then_inc(r_copied, 1)

                stage(0, 0)
                for g in range(4):
                    copy_group(g, g % 2, g, True)
                with act.Fori(1, NGR // 4) as i:
                    for g in range(4):
                        copy_group(4 * i + g, g % 2, g, False)
            with act.Else():
                def general_copy(s, first):
                    if not first:
                        act.wait_ge(gen_idx, s)
                        act.wait_ge(gen_r, s)
                    act.copy(stage_s[:, 0, :, :], esplit[:, bass.ds(s * GC, GC), :])
                    act.copy(stage_e[:, 0, :, :], ecols[:, bass.ds(s * GC, GC), :])
                    act.copy(stage_d[:, :], dcols[:, bass.ds(s * GC, GC)]).then_inc(gen_staged, 1)
                    act.wait_ge(gen_r, s + 1)
                    if not first:
                        for c in range(COPIES):
                            act.wait_ge(gen_add[c], 16 * s)
                    for c in range(2):
                        last = act.copy(rows[:, 0, 2 * c:2 * c + 2, :], bank(4 + c).rearrange("p (a b) -> p a b", b=D))
                    last.then_inc(gen_rc, 1)
                general_copy(0, True)
                with act.Fori(1, NGR) as s:
                    general_copy(s, False)

            act.wait_ge(scattered, 1)

            def copy_e4(j, t, peeled):
                act.wait_ge(e4_turned, TG * j + t + 1)
                if not (peeled and t < 2):
                    act.wait_ge(w_made, TG * j + t - 1)
                act.copy(e4t[:, t % 2, :, :], bank(4 + t % 2, 0, D).rearrange("p (a b) -> p a b", b=P)).then_inc(e4_copied, 1)

            def copy_h(j, t, peeled):
                act.wait_ge(h_turned, TG * j + t + 1)
                if not (peeled and t < 2):
                    act.wait_ge(lg_made, TG * j + t - 1)
                act.copy(hnt[:, t % 2, :, :], bank(5 - t % 2, 0, D).rearrange("p (a b) -> p a b", b=P)).then_inc(h_copied, 1)

            def node_group(j, first, last):
                act.wait_ge(mv_made, j + 1)
                act.activation(std3, mv3[:, :, 1], ACT.Sqrt, bias=eps_t[:, 0:1]).then_inc(std_made, 1)
                for t in range(TG):
                    copy_h(j, t, first)
                act.wait_ge(route, NR * j + 3)
                act.activation(pr, t56, ACT.Exp).then_inc(exp_made, 1)
                if not last:
                    for t in range(TG):
                        copy_e4(j + 1, t, False)

            for t in range(TG):
                copy_e4(0, t, True)
            node_group(0, True, False)
            with act.Fori(1, NG - 1) as j:
                node_group(j, False, False)
            node_group(NG - 1, False, True)

            for s in range(2):
                act.wait_ge(h_out[s], 16 * TG * (NG // 2))

            def turn_copy(n, first):
                act.wait_ge(tok_turned, n + 1)
                if not first:
                    act.wait_ge(tok_split, n)
                for k in range(KD):
                    last = act.copy(tokT[:, k, :], bank(k))
                last.then_inc(tok_copied, 1)

            def expert_block(e, b, first):
                n = e * XB + b
                cols = min(TB * P, C - b * TB * P)
                for m in range(KF):
                    act.wait_ge(m1_made, KF * n + m + 1)
                    if not (first and b == 0 and m < 2):
                        act.wait_ge(hid_split, KF * n + m - 1)
                    act.sem_inc(act_passed, 1)
                    act.activation(hid[:, m % 2, 0:cols], bank(2 + m % 4, 0, cols), ACT.Relu, bias=b1_t[:, bass.ds(e * KF + m, 1)]).then_inc(hid_made, 1)
                turn_copy(n + 1, False)

            turn_copy(0, True)
            for b in range(XB):
                expert_block(0, b, True)
            with act.Fori(1, NX) as e:
                for b in range(XB):
                    expert_block(e, b, False)

        @block.tensor
        def _(pe):
            pe.wait_ge(const_made, N_CONST)
            pe.wait_ge(e_float, 5)
            pe.wait_ge(edges_in, 16 * 9)
            for k in range(EQ):
                for a, t in enumerate((e_src, e_w, e_dst)):
                    n = 3 * k + a
                    if n >= 4:
                        pe.wait_ge(e_col, n - 3)
                    pe.transpose(bank(n % 4, 0, P), t[:, k * P:(k + 1) * P], ident[:, :]).then_inc(e_turned, 1)
            pe.wait_ge(consts_in, 32)
            pe.transpose(bank(4, 0, NX * KF), b1_rows[:, :], ident[0:NX * KF, 0:NX * KF]).then_inc(b1_turned, 1)
            pe.wait_ge(e_col, 3 * EQ)
            pe.matmul(bank(0, 0, NB), row0[:, :], ecols[:, 0:NCH:BC, 2], start=True, stop=True).then_inc(base_bc, 1)
            pe.wait_ge(prep, 11)
            pe.matmul(bank(1, 0, 1), onesf[:, :], spread[:, 3:4], start=True, stop=True).then_inc(flag_sum, 1)

            pe.wait_ge(flag_ok, 1)
            flag = pe.value_load(flag_i[0:1, 0:1], min_val=0, max_val=P)
            with pe.If(flag == 0):
                def broadcast_src(par, sem_, b0):
                    for c in range(GC):
                        for k in range(2):
                            mm = pe.matmul(bank(b0 + par, c * P, (c + 1) * P), stage_s[:, par, c, k:k + 1].to_broadcast([P, P]),
                                           identb[:, :], start=(k == 0), stop=(k == 1))
                    mm.then_inc(sem_, 1)

                def product_group(s, par, g, fills, peeled):
                    for c in range(GC):
                        pe.wait_ge(oh_made, GC * s + c + 1)
                        if c % 2 == 0 and not (peeled and g == 0):
                            pe.wait_ge(g_copied, 2 * (s - 1) + c // 2 + 1)
                        mm = pe.matmul(bank(2 + c // 2, (c % 2) * P, (c % 2 + 1) * P), is_node[:, par, c, :], same_w[:, par, c, :], start=True, stop=True)
                        if c % 2:
                            mm.then_inc(g_made, 1)
                    pe.wait_ge(staged, s + 2)
                    if not (peeled and g == 0):
                        pe.wait_ge(idx_made, s)
                    broadcast_src(1 - par, bc_made, 0)
                    if g % 2 == 0:
                        pe.wait_ge(win_in[g // 2], 16 * fills)
                    for c in range(GC):
                        if c % 2 == 0:
                            pe.wait_ge(g_copied, 2 * s + c // 2 + 1)
                            if not (peeled and g < 2):
                                pe.wait_ge(r_copied, 2 * (s - 2) + c // 2 + 1)
                        mm = pe.matmul(bank(4 + 2 * par + c // 2, (c % 2) * D, (c % 2 + 1) * D), g_sb[:, par, c, :], window[:, g // 2, :], start=True, stop=True)
                        if c % 2:
                            mm.then_inc(r_made, 1)

                pe.wait_ge(staged, 1)
                broadcast_src(0, bc_made, 0)
                for g in range(4):
                    product_group(g, g % 2, g, 1, True)
                with pe.Fori(1, NGR // 4) as i:
                    for g in range(4):
                        product_group(4 * i + g, g % 2, g, i + 1, False)
            with pe.Else():
                def general_products(s, first):
                    pe.wait_ge(gen_staged, s + 1)
                    if not first:
                        pe.wait_ge(gen_idx, s)
                    for c in range(GC):
                        for k in range(2):
                            mm = pe.matmul(bank(0, c * P, (c + 1) * P), stage_s[:, 0, c, k:k + 1].to_broadcast([P, P]),
                                           identb[:, :], start=(k == 0), stop=(k == 1))
                    mm.then_inc(gen_bc, 1)
                    pe.wait_ge(gen_same, s + 1)
                    if not first:
                        pe.wait_ge(gen_rc, s)
                    for c in range(GC):
                        pe.wait_ge(gen_in[c], 16 * (s + 1))
                        mm = pe.matmul(bank(4 + c // 2, (c % 2) * D, (c % 2 + 1) * D), same_w[:, 0, c, :], gathered[:, c, :], start=True, stop=True)
                    mm.then_inc(gen_r, 1)
                general_products(0, True)
                with pe.Fori(1, NGR) as s:
                    general_products(s, False)

            pe.wait_ge(late_in, 16 * 5)

            def o_bank(t):
                return bank(t // 2, (t % 2) * D, (t % 2 + 1) * D)

            def turn_and_multiply(j, peeled):
                for t in range(TG + 1):
                    if t < TG:
                        pe.wait_ge(e4_made, TG * j + t + 1)
                        if t >= 2:
                            pe.wait_ge(e4_copied, TG * j + t - 1)
                        elif not peeled:
                            pe.wait_ge(h_copied, TG * (j - 1) + TG - 1 + t)
                        for k in range(KD):
                            mm = pe.transpose(bank(4 + t % 2, k * P, (k + 1) * P), e4[:, t, k * P:(k + 1) * P], ident[:, :])
                        mm.then_inc(e4_turned, 1)
                    if t >= 1:
                        u = t - 1
                        pe.wait_ge(e4_copied, TG * j + u + 1)
                        if u == 0 and not peeled:
                            pe.wait_ge(x1_made, TG * j)
                        for k in range(KD):
                            mm = pe.matmul(o_bank(u), e4t[:, u % 2, k, :], w_sb[:, k, :], start=(k == 0), stop=(k == KD - 1))
                        mm.then_inc(w_made, 1)

            def turn_and_gate(j, h, first):
                for t in range(TG + 1):
                    if t < TG:
                        pe.wait_ge(h_made, TG * j + t + 1)
                        if t >= 2:
                            pe.wait_ge(h_copied, TG * j + t - 1)
                        else:
                            pe.wait_ge(e4_copied, TG * j + TG - 1 + t)
                        for k in range(KD):
                            mm = pe.transpose(bank(5 - t % 2, k * P, (k + 1) * P), hn[:, h, t, k * P:(k + 1) * P], ident[:, :])
                        mm.then_inc(h_turned, 1)
                    if t >= 1:
                        u = t - 1
                        pe.wait_ge(h_copied, TG * j + u + 1)
                        if u == 0 and not first:
                            pe.wait_ge(route, NR * (j - 1) + 1)
                        for k in range(KD):
                            mm = pe.matmul(bank(6, u * NX, (u + 1) * NX), hnt[:, u % 2, k, :], gate_sb[:, k, :], start=(k == 0), stop=(k == KD - 1))
                        mm.then_inc(lg_made, 1)

            def rank_products(j, first):
                pe.wait_ge(route, NR * j + 12)
                if not first:
                    pe.wait_ge(route, NR * j)
                r_out = bank(7, 0, TG * NX)
                pe.matmul(r_out, onesb[:, :], seenb.unsqueeze(1).to_broadcast([P, TG, NX]), start=True, stop=True)
                for t in range(TG - 1):
                    pe.matmul(bank(7, (t + 1) * NX, TG * NX).rearrange("p (a b) -> p a b", b=NX), onesb[:, :],
                              ohb[:, t:t + 1, :].to_broadcast([P, TG - 1 - t, NX]), start=False, stop=True, skip_group_check=True)
                pe.matmul(r_out, upto[:, :], ohb[:, :, :].rearrange("p a b -> p (a b)"),
                          start=False, stop=True, skip_group_check=True).then_inc(rank_made, 1)

            turn_and_multiply(0, True)
            turn_and_gate(0, 0, True)
            turn_and_multiply(1, False)
            rank_products(0, True)
            with pe.Fori(0, NG // 2 - 1) as i:
                for h in (1, 0):
                    j = 2 * i + 2 - h
                    turn_and_gate(j, h, False)
                    turn_and_multiply(j + 1, False)
                    rank_products(j, False)
            turn_and_gate(NG - 1, 1, False)
            rank_products(NG - 1, False)

            def turn_tokens(n, s, first):
                if not first:
                    pe.wait_ge(tok_copied, n)
                for k in range(KD):
                    for t in range(TB):
                        mm = pe.transpose(bank(k, t * P, (t + 1) * P), tok[:, s, t, k * P:(k + 1) * P], ident[:, :])
                mm.then_inc(tok_turned, 1)

            def expert_products(e, s_e, b, first):
                n = e * XB + b
                cols = min(TB * P, C - b * TB * P)
                pe.wait_ge(tok_split, n + 1)
                for m in range(KF):
                    if not (first and b == 0 and m < 4):
                        pe.wait_ge(hid_made, KF * n + m - 3)
                    for k in range(KD):
                        for i, (w, tk) in enumerate(((w1_hi, tok_hi), (w1_hi, tok_lo), (w1_lo, tok_hi))):
                            mm = pe.matmul(bank(2 + m % 4, 0, cols), w[:, s_e, k, m * P:(m + 1) * P], tk[:, k, 0:cols],
                                           start=(k + i == 0), stop=(k == KD - 1 and i == 2))
                    mm.then_inc(m1_made, 1)

            def expert_out(e, s_e, b, first):
                n = e * XB + b
                cols = min(TB * P, C - b * TB * P)
                for t in range(TB):
                    w = min(P, cols - t * P)
                    if t % 2 == 0 and not (first and b == 0):
                        pe.wait_ge(y_made, 2 * n - 1 + t // 2)
                    for m in range(KF):
                        if t == 0:
                            pe.wait_ge(hid_split, KF * n + m + 1)
                        for i, (hd, wt) in enumerate(((hid_hi, w2_hi), (hid_hi, w2_lo), (hid_lo, w2_hi))):
                            mm = pe.matmul(bank(6 + t // 2, (t % 2) * D, (t % 2 + 1) * D)[0:w, :], hd[:, m, t * P:t * P + w], wt[:, s_e, m, :],
                                           start=(m + i == 0), stop=(m == KF - 1 and i == 2))
                    if t % 2:
                        mm.then_inc(m2_made, 1)

            pe.wait_ge(tok_in[0], 16)
            turn_tokens(0, 0, True)

            def expert(e, s_e, toks, first):
                pe.wait_ge(w_split, XB * (e + 1))
                for b in range(XB):
                    expert_products(e, s_e, b, first)
                    pe.wait_ge(tok_in[(b + 1) % 2], 16 * (toks + (b + 1) // 2 + 1))
                    turn_tokens(e * XB + b + 1, (b + 1) % 2, False)
                    expert_out(e, s_e, b, first)

            expert(0, 0, 0, True)
            expert(1, 1, XB // 2, False)
            with pe.Fori(1, NX // 2) as i:
                for s_e in range(2):
                    expert(2 * i + s_e, s_e, (2 * i + s_e) * (XB // 2), False)
            pe.wait_ge(check_step, 1 + 2 * TB * NX * XB + 3)
            pe.wait_ge(tok_copied, NX * XB + 1)
            pe.matmul(bank(0, 0, 1), onesf[:, :], zero_part[:, :], start=True, stop=True).then_inc(fine_sum, 1)

        @block.vector
        def _(dve):
            dve.memset(e_src_i[96:P, :], PAD_NODE).then_inc(e_float, 1)
            dve.memset(e_dst_i[96:P, :], N - 1).then_inc(e_float, 1)
            dve.memset(e_w[96:P, :], 0.0).then_inc(e_float, 1)
            dve.memset(zeros[:, :], 0.0).then_inc(zeros_ok, 1)
            dve.memset(esplit[:, NCH:NCP, :], 0.0)
            dve.wait_ge(edges_in, 16 * 9)
            dve.tensor_copy(e_src, e_src_i).then_inc(e_float, 1)
            dve.tensor_copy(e_dst, e_dst_i).then_inc(e_float, 1)
            dve.wait_ge(const_made, N_CONST)
            dve.tensor_copy(iota_f[:, :], iota_i[:, :]).then_inc(prep, 1)
            dve.tensor_scalar(acc_dump[:, :], part_i[:, :], float(DUMP), None, ALU.add).then_inc(prep, 1)
            for n in range(2 * TG):
                last = dve.tensor_scalar(buf_dump[:, n:n + 1], part_i[:, :], float(BDUMP + n * P), None, ALU.add)
            last.then_inc(prep, 1)
            for c in range(COPIES):
                dve.tensor_scalar(acc_dump4[:, c:c + 1], part_i[:, :], float(DUMP + c * AR), None, ALU.add)
            dve.wait_ge(consts_in, 32)
            dve.tensor_scalar(neg_diag[:, :], neg_diag[:, :], -1.0, -1.0, ALU.mult, ALU.add).then_inc(prep, 1)
            dve.wait_ge(e_col, 3 * EQ)
            dve.tensor_copy(src_i, ecols[:, 0:NCH, 0]).then_inc(prep, 1)
            dve.tensor_copy(dcols[:, 0:NCH], ecols[:, 0:NCH, 2])
            dve.memset(dcols[:, NCH:NCP], 0)
            dve.wait_ge(prep, 5)
            dve.tensor_scalar(src_part, src_i, ~127, None, ALU.bitwise_and).then_inc(prep, 1)
            dve.tensor_scalar(src_i, src_i, 127, None, ALU.bitwise_and).then_inc(prep, 1)
            dve.wait_ge(prep, 7)
            dve.tensor_copy(esplit[:, 0:NCH, 0], src_part)
            dve.tensor_copy(esplit[:, 0:NCH, 1], src_i)
            dve.wait_ge(base_bc, 1)
            dve.tensor_scalar(base_f[:, :], bank(0, 0, NB), float(N - P), None, ALU.min).then_inc(prep, 1)
            dve.wait_ge(prep, 8)
            dve.tensor_copy(base_i[:, :], base_f[:, :])
            rel = ecols[:, 0:NCH, 2].rearrange("p (b c) -> p b c", c=BC)
            dve.tensor_tensor(rel, rel, base_f[:, :].unsqueeze(2).to_broadcast([P, NB, BC]), ALU.subtract).then_inc(prep, 1)
            dve.wait_ge(prep, 9)
            dve.tensor_reduce(spread[:, 0:1], ecols[:, 0:NCH, 2], AX_X, ALU.max)
            dve.tensor_reduce(spread[:, 1:2], ecols[:, 0:NCH, 2], AX_X, ALU.min).then_inc(prep, 1)
            dve.wait_ge(prep, 10)
            dve.tensor_scalar(spread[:, 2:3], spread[:, 0:1], float(P - 1), None, ALU.is_gt).then_inc(base_out, 1)
            dve.wait_ge(base_out, 1)
            dve.scalar_tensor_tensor(out=spread[:, 3:4], in0=spread[:, 1:2], scalar=0.0, in1=spread[:, 2:3], op0=ALU.is_lt, op1=ALU.max).then_inc(prep, 1)
            dve.wait_ge(flag_sum, 1)
            dve.tensor_copy(flag_i[:, :], bank(1, 0, 1)).then_inc(flag_ok, 1)

            def ln_group(j, h, peeled):
                dve.wait_ge(ln_in[h], 32 * (j // 2 + 1) if peeled else 32 * (lni[0] + 1))
                for t in range(TG):
                    last = dve.bn_stats(ln_stat[:, h, t, :], ln_x[:, h, t, :])
                last.then_inc(ln_step, 1)
                dve.wait_ge(ln_step, 2 * j + 1)
                dve.sem_inc(dve_passed, 1)
                for t in range(TG):
                    last = dve.bn_aggr(ln_mv[:, h, t, :], ln_stat[:, h, t, :])
                last.then_inc(ln_mean, 1)
                dve.wait_ge(ln_sq, j + 1)
                dve.reciprocal(ln_rstd[:, h, :], ln_std[:, h, :]).then_inc(ln_step, 1)
                dve.wait_ge(ln_step, 2 * j + 2)
                if not peeled:
                    dve.wait_ge(ln_out[h], 32 * lni[0])
                for t in range(TG):
                    last = dve.tensor_scalar(ln_n[:, h, t, :], ln_x[:, h, t, :], ln_mv[:, h, t, 0:1], ln_rstd[:, h, t:t + 1], ALU.subtract, ALU.mult)
                last.then_inc(ln_xn, 1)

            lni = [None]
            for h in range(2):
                ln_group(h, h, True)
            with dve.Fori(1, NG // 2) as i:
                lni[0] = i
                for h in range(2):
                    ln_group(2 * i + h, h, False)

            flag = dve.value_load(flag_i[0:1, 0:1], min_val=0, max_val=P)
            dve.wait_ge(ln_out[0], 32 * (NG // 2))
            dve.wait_ge(ln_out[1], 32 * (NG // 2))
            with dve.If(flag == 0):
                def match_group(s, par, g, peeled):
                    dve.wait_ge(bc_made, s + 1)
                    if not (peeled and g < 2):
                        dve.wait_ge(g_made, 2 * (s - 1))
                    for c in range(GC):
                        srcs = bank(par, c * P, (c + 1) * P)
                        dve.tensor_scalar(same_w[:, par, c, :], srcs, stage_e[:, par, c, 0:1], stage_e[:, par, c, 1:2], ALU.is_equal, ALU.mult)
                        dve.tensor_scalar(is_node[:, par, c, :], iota_f[:, :], stage_e[:, par, c, 2:3], None, ALU.is_equal).then_inc(oh_made, 1)
                    for c in range(GC):
                        last = dve.scalar_tensor_tensor(out=picked[:, par, c, :], in0=bank(par, c * P, (c + 1) * P), scalar=stage_e[:, par, c, 0:1],
                                                        in1=earlier[:, :], op0=ALU.is_equal, op1=ALU.mult, accum_out=sooner[:, par, c:c + 1])
                    dve.tensor_scalar(offs[:, par, :], stage_e[:, par, :, 0], acc_dump[:, 0:1], None, ALU.subtract).then_inc(idx_step, 1)
                    dve.wait_ge(idx_step, 2 * s + 1)
                    dve.scalar_tensor_tensor(out=idx_f[:, par, :], in0=sooner[:, par, :], scalar=0.0, in1=offs[:, par, :], op0=ALU.is_equal, op1=ALU.mult).then_inc(idx_step, 1)
                    dve.wait_ge(idx_step, 2 * s + 2)
                    if not (peeled and g < 2):
                        for c in range(COPIES):
                            dve.wait_ge(acc_add[c], 16 * (s - 1))
                    dve.tensor_tensor(idx_a[:, par, :], idx_f[:, par, :], acc_dump4[:, :], ALU.add).then_inc(idx_made, 1)

                for g in range(4):
                    match_group(g, g % 2, g, True)
                with dve.Fori(1, NGR // 4) as i:
                    for g in range(4):
                        match_group(4 * i + g, g % 2, g, False)
            with dve.Else():
                def general_match(s, first):
                    dve.wait_ge(gen_bc, s + 1)
                    if not first:
                        dve.wait_ge(gen_r, s)
                        for c in range(COPIES):
                            dve.wait_ge(gen_add[c], 16 * s)
                    for c in range(GC):
                        last = dve.tensor_scalar(same_w[:, 0, c, :], bank(0, c * P, (c + 1) * P), stage_e[:, 0, c, 0:1], stage_e[:, 0, c, 1:2], ALU.is_equal, ALU.mult)
                    last.then_inc(gen_same, 1)
                    for c in range(GC):
                        dve.scalar_tensor_tensor(out=picked[:, 0, c, :], in0=bank(0, c * P, (c + 1) * P), scalar=stage_e[:, 0, c, 0:1],
                                                 in1=earlier[:, :], op0=ALU.is_equal, op1=ALU.mult, accum_out=sooner[:, 0, c:c + 1])
                    dve.tensor_scalar(offs[:, 0, :], stage_e[:, 0, :, 0], acc_dump[:, 0:1], None, ALU.subtract).then_inc(gen_step, 1)
                    dve.wait_ge(gen_step, 2 * s + 1)
                    dve.scalar_tensor_tensor(out=idx_f[:, 0, :], in0=sooner[:, 0, :], scalar=0.0, in1=offs[:, 0, :], op0=ALU.is_equal, op1=ALU.mult).then_inc(gen_step, 1)
                    dve.wait_ge(gen_step, 2 * s + 2)
                    dve.tensor_tensor(idx_a[:, 0, :], idx_f[:, 0, :], acc_dump4[:, :], ALU.add).then_inc(gen_idx, 1)
                general_match(0, True)
                with dve.Fori(1, NGR) as s:
                    general_match(s, False)

            dve.wait_ge(scattered, 1)
            dve.wait_ge(late_in, 16 * 5)
            dve.memset(seen, 0.0)
            dve.memset(seenb, 0.0)

            def sum_half(t, fills):
                dve.wait_ge(a_got[t], 16 * fills)
                dve.tensor_tensor(half[:, t, :, :], a_in[:, t, 0:2, :], a_in[:, t, 2:4, :], ALU.add).then_inc(half_made, 1)

            def sum_rest(j, t):
                dve.wait_ge(half_made, TG * j + t + 1)
                dve.tensor_tensor(e4[:, t, :], half[:, t, 0, :], half[:, t, 1, :], ALU.add).then_inc(e4_made, 1)

            def step(ins, j, n):
                ins.then_inc(route, 1)
                dve.wait_ge(route, NR * j + n)

            def over_experts(v):
                return v.unsqueeze(2).to_broadcast([P, TG, NX])

            def over_tiles(v):
                return v.unsqueeze(1).to_broadcast([P, TG, NX])

            mx, sm, rc, prb, top, pos, kept, base, rowf, under, k2, sidx = c7

            def route_logits(j):
                dve.wait_ge(lg_made, TG * (j + 1))
                step(dve.tensor_tensor(lg, bank(6, 0, TG * NX).rearrange("p (a b) -> p a b", b=NX), over_tiles(gateb_t[:, :]), ALU.add), j, 1)
                step(dve.tensor_reduce(mx, lg, AX_X, ALU.max), j, 2)
                step(dve.tensor_tensor(t56, lg, over_experts(mx), ALU.subtract), j, 3)

            def route_choice(j):
                dve.wait_ge(exp_made, j + 1)
                step(dve.tensor_reduce(sm, pr, AX_X, ALU.add), j, 4)
                step(dve.reciprocal(rc, sm), j, 5)
                step(dve.tensor_tensor(pr, pr, over_experts(rc), ALU.mult), j, 6)
                step(dve.tensor_reduce(prb, pr, AX_X, ALU.max), j, 7)
                step(dve.tensor_tensor(t56, pr, over_experts(prb), ALU.is_equal), j, 8)
                step(dve.tensor_tensor(t56, t56, over_tiles(falling[:, :]), ALU.mult), j, 9)
                step(dve.tensor_reduce(top, t56, AX_X, ALU.max), j, 10)
                step(dve.tensor_tensor(oh, over_experts(top), over_tiles(falling[:, :]), ALU.is_equal), j, 11)
                step(dve.tensor_tensor(ohb, oh, over_experts(valid[:, bass.ds(j * TG, TG)]), ALU.mult), j, 12)

            def route_rows(j, h):
                dve.wait_ge(rank_made, j + 1)
                step(dve.tensor_tensor(t56, bank(7, 0, TG * NX).rearrange("p (a b) -> p a b", b=NX), ohb, ALU.mult), j, 13)
                step(dve.tensor_reduce(pos, t56, AX_X, ALU.add), j, 14)
                step(dve.tensor_reduce(new8, ohb.rearrange("p a b -> p b a"), AX_X, ALU.add), j, 15)
                dve.tensor_scalar(base, top, -float(C), float(NX * C - 1), ALU.mult, ALU.add)
                dve.tensor_scalar(under, pos, float(C), None, ALU.is_le)
                step(dve.tensor_scalar(rowf, pos, float(C), None, ALU.min), j, 16)
                dve.scalar_tensor_tensor(out=kept, in0=pos, scalar=0.0, in1=under, op0=ALU.is_gt, op1=ALU.mult)
                step(dve.tensor_tensor(rowf, rowf, base, ALU.add), j, 17)
                dve.tensor_tensor(y_scale[:, bass.ds(j * TG, TG)], prb, kept, ALU.mult)
                dve.tensor_scalar(gather_row[:, bass.ds(j * TG, TG)], rowf, 0.0, None, ALU.max)
                step(dve.tensor_tensor(k2, rowf, buf_dump[:, h * TG:(h + 1) * TG], ALU.subtract), j, 18)
                step(dve.tensor_tensor(sidx, k2, kept, ALU.mult), j, 19)
                dve.tensor_tensor(scat_i[:, h, 0:TG], sidx, buf_dump[:, h * TG:(h + 1) * TG], ALU.add).then_inc(slot_made, 1)
                step(dve.tensor_tensor(seen, seen, new8, ALU.add), j, 20)
                step(dve.tensor_copy(seenb, seen), j, 21)

            def node_group(j, h, fills, first, last_group):
                dve.wait_ge(xb_made, j + 1)
                if fills is not None:
                    dve.wait_ge(x1_out[h], 16 * fills)
                for t in range(TG + 1):
                    if t < TG:
                        dve.wait_ge(w_made, TG * j + min(TG, t - t % 2 + 2))
                        dve.tensor_tensor(x1[:, h, t, :], bank(t // 2, (t % 2) * D, (t % 2 + 1) * D), x_in[:, h, t, :], ALU.add).then_inc(x1_made, 1)
                    if t >= 1:
                        dve.wait_ge(x1_made, TG * j + t)
                        last = dve.bn_stats(st3[:, t - 1, :], x1[:, h, t - 1, :])
                last.then_inc(stat_made, 1)
                dve.wait_ge(stat_made, j + 1)
                dve.sem_inc(dve_passed, 1)
                for t in range(TG):
                    last = dve.bn_aggr(mv3[:, t, :], st3[:, t, :])
                last.then_inc(mv_made, 1)
                if not first:
                    route_rows(j - 1, 1 - h)
                dve.wait_ge(std_made, j + 1)
                dve.reciprocal(rstd3, std3).then_inc(rstd_made, 1)
                dve.wait_ge(rstd_made, j + 1)
                if fills is not None:
                    dve.wait_ge(h_out[h], 16 * TG * fills)
                for t in range(TG):
                    dve.tensor_scalar(hn[:, h, t, :], x1[:, h, t, :], mv3[:, t, 0:1], rstd3[:, t:t + 1], ALU.subtract, ALU.mult).then_inc(h_made, 1)
                if not last_group:
                    sum_half(0, j + 2)
                    for t in range(TG):
                        if t + 1 < TG:
                            sum_half(t + 1, j + 2)
                        sum_rest(j + 1, t)
                route_logits(j)
                route_choice(j)

            sum_half(0, 1)
            for t in range(TG):
                if t + 1 < TG:
                    sum_half(t + 1, 1)
                sum_rest(0, t)
            node_group(0, 0, None, True, False)
            node_group(1, 1, None, False, False)
            with dve.Fori(1, NG // 2 - 1) as i:
                for h in range(2):
                    node_group(2 * i + h, h, i, False, False)
            for h in range(2):
                node_group(NG - 2 + h, h, NG // 2 - 1, False, h == 1)
            route_rows(NG - 1, 1)

            dve.memset(zero_sum[:, :], 0.0).then_inc(check_step, 1)
            dve.wait_ge(check_step, 1)

            def check(v, junk, w, k):
                dve.tensor_scalar(junk, v, 0.0, None, ALU.mult, ALU.add, accum_out=zero_part[0:w, :]).then_inc(check_step, 1)
                dve.wait_ge(check_step, k + 1)
                dve.tensor_tensor(zero_sum[0:w, :], zero_sum[0:w, :], zero_part[0:w, :], ALU.add).then_inc(check_step, 1)
                dve.wait_ge(check_step, k + 2)

            def split_weights(e, s, b):
                if b < 2:
                    dve.wait_ge(w1_in, 16 * (e + 1))
                    n = KD // 2
                    whole, hi, lo = (t[:, b * n:(b + 1) * n, :] for t in (w1_in_sb, w1_hi[:, s, :, :], w1_lo[:, s, :, :]))
                else:
                    dve.wait_ge(w2_in, 16 * (e + 1))
                    n = KF // 2
                    whole, hi, lo = (t[:, (b - 2) * n:(b - 1) * n, :] for t in (w2_in_sb, w2_hi[:, s, :, :], w2_lo[:, s, :, :]))
                dve.tensor_copy(hi, whole).then_inc(w_hi_made, 1)
                dve.wait_ge(w_hi_made, XB * e + b + 1)
                dve.tensor_tensor(lo, whole, hi.bitcast(F32), ALU.subtract).then_inc(w_split, 1)

            def split_tokens(n, first):
                dve.wait_ge(tok_copied, n + 1)
                if not first:
                    dve.wait_ge(m1_made, KF * n)
                dve.tensor_copy(tok_hi[:, :, :], tokT).then_inc(tok_hi_made, 1)
                dve.wait_ge(tok_hi_made, n + 1)
                dve.tensor_tensor(tok_lo[:, :, :], tokT, tok_hi[:, :, :].bitcast(F32), ALU.subtract).then_inc(tok_split, 1)

            def expert_sum(e, b, s_e, first, last_expert):
                n = e * XB + b
                s = b % 2
                cols = min(TB * P, C - b * TB * P)
                for m in range(KF):
                    dve.wait_ge(hid_made, KF * n + m + 1)
                    if m == 0 and not (first and b == 0):
                        dve.wait_ge(m2_made, 2 * n)
                    dve.tensor_copy(hid_hi[:, m, 0:cols], hid[:, m % 2, 0:cols]).then_inc(hid_hi_made, 1)
                    dve.wait_ge(hid_hi_made, KF * n + m + 1)
                    dve.tensor_tensor(hid_lo[:, m, 0:cols], hid[:, m % 2, 0:cols], hid_hi[:, m, 0:cols].bitcast(F32), ALU.subtract).then_inc(hid_split, 1)
                split_tokens(n + 1, False)
                if not (first and b < 2):
                    dve.wait_ge(y_out[s], 16 * TB * (e * (XB // 2) + b // 2))
                for t in range(0, TB, 2):
                    dve.wait_ge(m2_made, 2 * n + t // 2 + 1)
                    for u in range(t, t + 2):
                        w = min(P, C - (b * TB + u) * P)
                        last = dve.tensor_tensor(y_sb[0:w, s, u, :], bank(6 + t // 2, (u - t) * D, (u - t + 1) * D)[0:w, :],
                                                 b2_t[0:w, bass.ds(e, 1), :].rearrange("p a d -> p (a d)"), ALU.add)
                    last.then_inc(y_made, 1)
                    dve.wait_ge(y_made, 2 * n + t // 2 + 1)
                    for u in range(t, t + 2):
                        w = min(P, C - (b * TB + u) * P)
                        check(y_sb[0:w, s, u, :], y_zero[0:w, :], w, 1 + 2 * (TB * n + u))
                    if t == 0 and not last_expert:
                        if b == 0 and not first:
                            dve.wait_ge(m2_made, 2 * XB * e)
                        split_weights(e + 1, 1 - s_e, b)

            for b in range(XB):
                split_weights(0, 0, b)
            split_tokens(0, True)

            def expert_blocks(e, s_e, first, last_expert):
                for b in range(XB):
                    expert_sum(e, b, s_e, first, last_expert)

            expert_blocks(0, 0, True, False)
            expert_blocks(1, 1, False, False)
            with dve.Fori(1, NX // 2 - 1) as i:
                for s_e in range(2):
                    expert_blocks(2 * i + s_e, s_e, False, False)
            expert_blocks(NX - 2, 0, False, False)
            expert_blocks(NX - 1, 1, False, True)
            k = 1 + 2 * TB * NX * XB
            check(y_scale[:, :], y_zero[:, 0:NT], P, k)
            dve.tensor_scalar(zero_part[:, :], zero_sum[:, :], 0.0, None, ALU.is_equal).then_inc(check_step, 1)
            dve.wait_ge(fine_sum, 1)
            dve.tensor_copy(fine_i[:, :], bank(0, 0, 1)).then_inc(check_step, 1)
            dve.wait_ge(check_step, k + 4)

            dve.wait_ge(tok_copied, NX * XB + 1)
            dve.wait_ge(m2_made, 2 * NX * XB)
            dve.memset(big4, 10000.0).then_inc(lim_made, 1)
            dve.memset(neg4, -10000.0).then_inc(lim_made, 1)
            dve.wait_ge(lim_made, 2)

            fine = dve.value_load(fine_i[0:1, 0:1], min_val=0, max_val=P)
            with dve.If(fine == P):
                def add_finite(j, h, fills, first):
                    dve.wait_ge(yg_in[h], 16 * TG * fills)
                    dve.wait_ge(x1_in[h], 16 * fills)
                    if not first:
                        dve.wait_ge(o_out[h], 32 * (fills - 1))
                    for t in range(TG):
                        last = dve.scalar_tensor_tensor(out=yp[:, h, t, :], in0=yg[:, h, t, :], scalar=y_scale[:, bass.ds(j * TG + t, 1)],
                                                        in1=x1b[:, h, t, :], op0=ALU.mult, op1=ALU.add)
                    last.then_inc(o_made, 1)

                for h in range(2):
                    add_finite(h, h, 1, True)
                with dve.Fori(1, NG // 2) as i:
                    for h in range(2):
                        add_finite(2 * i + h, h, i + 1, False)
            with dve.Else():
                def add_any(j, h, fills, first):
                    f0 = NP_FIN * j
                    dve.wait_ge(yg_in[h], 16 * TG * fills)
                    if not first:
                        dve.wait_ge(o_out[h], 32 * (fills - 1))
                    for t in range(TG):
                        sc = y_scale[:, bass.ds(j * TG + t, 1)]
                        dve.tensor_scalar(yp[:, h, t, :], yg[:, h, t, :], sc, 0.0, ALU.mult, ALU.max)
                        last = dve.tensor_scalar(yn[:, h, t, :], yg[:, h, t, :], sc, 0.0, ALU.mult, ALU.min)
                    last.then_inc(fin_step, 1)
                    dve.wait_ge(fin_step, f0 + 1)
                    flat_p = yp[:, h, :, :].rearrange("p a b -> p (a b)")
                    flat_n = yn[:, h, :, :].rearrange("p a b -> p (a b)")
                    flat_m = over.rearrange("p a b -> p (a b)")
                    dve.tensor_scalar(flat_m, flat_p, HUGE, None, ALU.is_gt).then_inc(fin_step, 1)
                    dve.wait_ge(fin_step, f0 + 2)
                    dve.sem_inc(dve_passed, 1)
                    dve.copy_predicated(flat_p, flat_m, big4).then_inc(fin_step, 1)
                    dve.wait_ge(fin_step, f0 + 3)
                    dve.tensor_scalar(flat_m, flat_n, -HUGE, None, ALU.is_lt).then_inc(fin_step, 1)
                    dve.wait_ge(fin_step, f0 + 4)
                    dve.sem_inc(dve_passed, 1)
                    dve.copy_predicated(flat_n, flat_m, neg4).then_inc(fin_step, 1)
                    dve.wait_ge(fin_step, f0 + 5)
                    dve.tensor_tensor(flat_p, flat_p, flat_n, ALU.add).then_inc(fin_step, 1)
                    dve.wait_ge(fin_step, f0 + 6)
                    dve.wait_ge(x1_in[h], 16 * fills)
                    dve.tensor_tensor(flat_p, flat_p, x1b[:, h, :, :].rearrange("p a b -> p (a b)"), ALU.add).then_inc(o_made, 1)

                for h in range(2):
                    add_any(h, h, 1, True)
                with dve.Fori(1, NG // 2) as i:
                    for h in range(2):
                        add_any(2 * i + h, h, i + 1, False)


_INS = ['x', 'src', 'dst', 'edge_weight', 'L0_gnn_weight', 'L0_gnn_learnable_diag', 'L0_gnn_bias',
        'L0_ffn_gate_w', 'L0_ffn_gate_b', 'L0_ffn_w1', 'L0_ffn_b1', 'L0_ffn_w2', 'L0_ffn_b2']
_OUTS = [((12500, 256), 'float32')]


def kernel(**inputs):
    import numpy as _np
    import concourse.bacc as _bacc
    from concourse import mybir as _mybir
    from concourse.bass_utils import run_bass_kernel_spmd as _run

    nc = _bacc.Bacc("TRN2", target_bir_lowering=False, num_devices=1)
    arrays, args = {}, []
    for name in _INS:
        a = _np.ascontiguousarray(inputs[name])
        arrays[f"in_{name}_dram"] = a
        args.append(nc.dram_tensor(f"in_{name}_dram", a.shape, _mybir.dt.from_np(a.dtype), kind="ExternalInput").ap())
    for i, (shape, dtype) in enumerate(_OUTS):
        dt = _mybir.dt.from_np(_np.dtype(dtype))
        args.append(nc.dram_tensor(f"out_{i}_dram", shape, dt, kind="ExternalOutput").ap())
    gnn_moe_layer(nc, *args)
    r = _run(nc, [arrays], core_ids=[0])
    got = tuple(r.results[0][f"out_{i}_dram"] for i in range(len(_OUTS)))
    return got[0]
```

```python
from contextlib import ExitStack

import concourse.bass as bass
from concourse import mybir

ALU = mybir.AluOpType
ACT = mybir.ActivationFunctionType
AX_X = mybir.AxisListType.X
F32 = mybir.dt.float32
BF16 = mybir.dt.bfloat16
F32R = mybir.dt.float32r
I32 = mybir.dt.int32
U32 = mybir.dt.uint32

P = 128
EPS = 1e-5
COPIES = 4
GC = 4
BC = 8
TG = 7
HUGE = 3.4028234663852886e38


def gnn_moe_layer(nc, x, src, dst, edge_weight, gnn_w, gnn_diag, gnn_bias, gate_w, gate_b,
                  w1, b1, w2, b2, out):
    N, D = x.shape
    E = src.shape[0]
    NX, _, F = w1.shape
    C = max(1, -(-5 * N // (4 * NX)))
    KD = D // P
    KF = F // P

    EQ = -(-E // (P * P))
    EP = EQ * P
    NCH = P * EQ
    NGR = NCH // GC
    NB = NCH // BC
    assert NCH % (2 * BC) == 0
    EFULL = E // EP
    EREST = E - EFULL * EP
    assert 96 <= EFULL == P - 1 and EREST > 0

    NT = -(-N // P)
    NREST = N - (NT - 1) * P
    NG = NT // TG
    assert NG * TG == NT and NG % 2 == 0
    PAD_NODE = N
    DUMP = N + 1
    AR = (NT + 1) * P
    ZR = 11
    assert AR // P % ZR == 0 and DUMP + P <= AR

    TB = 4
    XT = -(-C // P)
    XB = -(-XT // TB)
    assert XT == XB * TB and XB == 4 and NG == 2 * (NX - 1) and NX % 2 == 0 and KD == 2
    HW = D + 2
    NOWHERE = 1 << 20
    BDUMP = NX * C
    ZB = 2
    BZ = -(-(NX * C + max(TB, 2 * TG) * P) // (P * ZB))
    BR = BZ * P * ZB
    assert BZ < NB // 2 and ZB * HW <= ZR * D

    acc_dram = nc.dram_tensor("acc_dram", (COPIES, AR, D), F32)
    acc_flat = acc_dram[:, :, :].rearrange("k r d -> (k r) d")
    xs_dram = nc.dram_tensor("xs_dram", (NT * P, D), F32)
    x1_dram = nc.dram_tensor("x1_dram", (NT * P, D), F32)
    buf_dram = nc.dram_tensor("buf_dram", (BR, HW), F32)
    y_dram = nc.dram_tensor("y_dram", (NX * C, D), F32)

    with ExitStack() as ctx:
        def sb(name, shape, dt=F32):
            return ctx.enter_context(nc.sbuf_tensor(name, shape, dt))

        def sem(name):
            return ctx.enter_context(nc.semaphore(name))

        ident = sb("ident", [P, P])
        identb = sb("identb", [P, P], BF16)
        earlier = sb("earlier", [P, P])
        upto = sb("upto", [P, P], BF16)
        onesb = sb("onesb", [P, P], BF16)
        onesf = sb("onesf", [P, P])
        row0 = sb("row0", [P, P])
        iota_i = sb("iota_i", [P, P], I32)
        iota_f = sb("iota_f", [P, P])
        part_i = sb("part_i", [P, 1], I32)
        acc_dump = sb("acc_dump", [P, 1])
        acc_dump4 = sb("acc_dump4", [P, COPIES])
        buf_dump = sb("buf_dump", [P, 2 * TG])
        falling = sb("falling", [P, NX])
        node_i = sb("node_i", [P, NT], I32)
        node1 = sb("node1", [P, NT])
        node0 = sb("node0", [P, NT])
        valid = sb("valid", [P, NT])
        eps_t = sb("eps_t", [P, 1])
        neg_diag = sb("neg_diag", [P, D])
        bias_t = sb("bias_t", [P, D])
        gateb_t = sb("gateb_t", [P, NX])
        w_sb = sb("w_sb", [P, KD, D])
        gate_sb = sb("gate_sb", [P, KD, NX])
        b1_rows = sb("b1_rows", [NX * KF, P])
        b1_t = sb("b1_t", [P, NX * KF])
        b2_t = sb("b2_t", [P, NX, D])
        alone = sb("alone", [P, NT], I32)
        gather_row = sb("gather_row", [P, NT], I32)
        y_scale = sb("y_scale", [P, NT])

        zero_sum = sb("zero_sum", [P, 1])
        zero_part = sb("zero_part", [P, 1])
        y_zero = sb("y_zero", [P, D])
        fine_i = sb("fine_i", [P, 1], I32)

        base_f = sb("base_f", [P, NB])
        base_i = sb("base_i", [P, NB], I32)
        spread = sb("spread", [P, 4])
        flag_i = sb("flag_i", [P, 1], I32)

        REGION = 45600
        region_at = -(-nc.sbuf_base // 32) * 32
        big = sb("big", [P, REGION])
        assert region_at + 4 * REGION <= nc.sbuf_base

        def region(start=0):
            at = [start]

            def take(shape, dt=F32, name=None):
                n = 1
                for s in shape:
                    n *= s
                n = n * (2 if dt == BF16 else 4) // 4
                at[0] += n
                assert at[0] <= REGION
                if dt == F32R:
                    at_byte = region_at + 4 * (at[0] - n)
                    return nc.alloc_sbuf_tensor_at(name, [P] + shape, F32R, offset=at_byte)
                v = big[:, at[0] - n:at[0]]
                if dt != F32:
                    v = v.bitcast(dt)
                if len(shape) == 1:
                    return v
                names = "abcd"[:len(shape)]
                return v.rearrange(f"p ({' '.join(names)}) -> p {' '.join(names)}",
                                   **dict(zip(names[1:], shape[1:])))
            return take, lambda: -(-at[0] // 8) * 8

        NCP = NCH + GC
        r, r_end = region()
        ecols = r([NCP, 3])
        esplit = r([NCP, 2], BF16)
        dcols = r([NCP], I32)
        zeros = r([ZR * D])
        held = NCP * 5 + ZR * D
        r, r_end = region(held)
        e_src_i, e_dst_i, e_w = r([EP], I32), r([EP], I32), r([EP])
        e_src, e_dst = r([EP]), r([EP])
        src_i, src_part = r([NCH], I32), r([NCH], I32)
        ln_x, ln_n, ln_s = r([2, TG, D]), r([2, TG, D]), r([2, TG, D])
        ln_stat, ln_mv, ln_std, ln_rstd = r([2, TG, 6]), r([2, TG, 2]), r([2, TG]), r([2, TG])
        r, r_end = region(held)
        stage_e, stage_s, stage_d = r([2, GC, 3]), r([2, GC, 2], BF16), r([GC], I32)
        same_w, is_node, g_sb = r([2, GC, P]), r([2, GC, P]), r([2, GC, P])
        rows, window = r([2, GC, D]), r([2, D])
        picked, sooner, offs, idx_f = r([2, GC, P]), r([2, GC]), r([2, GC]), r([2, GC])
        idx_a = r([2, GC], I32)
        gathered = r([GC, D])
        r, r_end = region()
        a_in, half, e4 = r([TG, COPIES, D]), r([TG, 2, D]), r([TG, D])
        x_in, x1 = r([2, TG, D]), r([2, TG, D])
        hn = r([2, TG, HW])
        e4t, hnt = r([2, KD, P]), r([2, KD, P])
        st3, mv3, std3, rstd3, shift3 = r([TG, 6]), r([TG, 2]), r([TG]), r([TG]), r([TG])
        lg, pr, oh, t56 = r([TG, NX]), r([TG, NX]), r([TG, NX]), r([TG, NX])
        ohb = r([TG, NX], BF16)
        seen, seenb, new8 = r([NX]), r([NX], BF16), r([NX])
        c7 = [r([TG]) for _ in range(12)]
        scat_i = r([2, TG + 1], I32)
        NODES_END = r_end()
        r, r_end = region()
        tok, tokT = r([2, TB, HW]), r([KD, TB * P])
        tok_hi, tok_lo = r([KD, TB * P], F32R, "tok_hi"), r([KD, TB * P], F32R, "tok_lo")
        hid = r([2, TB * P])
        hid_hi, hid_lo = r([KF, TB * P], F32R, "hid_hi"), r([KF, TB * P], F32R, "hid_lo")
        y_sb, o_sb = r([2, TB, D]), r([2, TB, D])
        meta, meta_i, meta_w = r([TB]), r([2, TB], I32), r([2, TB])
        x1_rows, alone_i = r([2, TG, D]), r([2, TG + 1], I32)
        assert r_end() <= NODES_END
        r, r_end = region(NODES_END)
        w1_in_sb, w2_in_sb = r([KD, F]), r([KF, D])
        w1_hi, w1_lo = r([2, KD, F], F32R, "w1_hi"), r([2, KD, F], F32R, "w1_lo")
        w2_hi, w2_lo = r([2, KF, D], F32R, "w2_hi"), r([2, KF, D], F32R, "w2_lo")
        r, r_end = region()
        yg, x1b = r([2, TG, D]), r([2, TG, D])
        yp, yn = r([2, TG, D]), r([2, TG, D])
        over, big4, neg4 = r([TG, D], U32), r([TG * D]), r([TG * D])
        gidx = r([2, TG + 1], I32)

        ps = ctx.enter_context(nc.psum_tensor("ps", [P, 8 * 512], F32))

        def bank(n, lo=0, hi=512):
            return ps[:, n * 512 + lo:n * 512 + hi]

        edges_in, consts_in, late_in, const_made = sem("edges_in"), sem("consts_in"), sem("late_in"), sem("const_made")
        pool_step = sem("pool_step")
        e_float, e_turned, e_col = sem("e_float"), sem("e_turned"), sem("e_col")
        prep, base_bc, base_out, flag_sum, flag_ok = sem("prep"), sem("base_bc"), sem("base_out"), sem("flag_sum"), sem("flag_ok")
        b1_turned, b1_ok = sem("b1_turned"), sem("b1_ok")
        zeros_ok, acc_zero, buf_zero = sem("zeros_ok"), sem("acc_zero"), sem("buf_zero")
        ln_in = [sem(f"ln_in{i}") for i in range(2)]
        ln_step, ln_sq, ln_xn, ln_xs = sem("ln_step"), sem("ln_sq"), sem("ln_xn"), sem("ln_xs")
        ln_mean = sem("ln_mean")
        ln_out = [sem(f"ln_out{i}") for i in range(2)]
        staged, bc_made, oh_made, g_made, g_copied = sem("staged"), sem("bc_made"), sem("oh_made"), sem("g_made"), sem("g_copied")
        r_made, r_copied, idx_step, idx_made = sem("r_made"), sem("r_copied"), sem("idx_step"), sem("idx_made")
        win_in = [sem(f"win_in{i}") for i in range(2)]
        acc_add = [sem(f"acc_add{i}") for i in range(COPIES)]
        gen_add = [sem(f"gen_add{i}") for i in range(COPIES)]
        gen_in = [sem(f"gen_in{i}") for i in range(GC)]
        gen_staged, gen_bc, gen_same, gen_idx, gen_step, gen_r, gen_rc = (
            sem(n) for n in ("gen_staged", "gen_bc", "gen_same", "gen_idx", "gen_step", "gen_r", "gen_rc"))
        scattered = sem("scattered")
        a_got = [sem(f"a_got{i}") for i in range(TG)]
        x_got = [sem(f"x_got{i}") for i in range(2)]
        half_made, e4_made, e4_turned, e4_copied, w_made = sem("half_made"), sem("e4_made"), sem("e4_turned"), sem("e4_copied"), sem("w_made")
        xb_made, x1_made, stat_made, mv_made, std_made, rstd_made = (
            sem(n) for n in ("xb_made", "x1_made", "stat_made", "mv_made", "std_made", "rstd_made"))
        shift_made, h_made, h_turned, h_copied, lg_made = sem("shift_made"), sem("h_made"), sem("h_turned"), sem("h_copied"), sem("lg_made")
        x1_out = [sem(f"x1_out{i}") for i in range(2)]
        route, exp_made, rank_made, slot_made = sem("route"), sem("exp_made"), sem("rank_made"), sem("slot_made")
        h_out = [sem(f"h_out{i}") for i in range(2)]
        w1_in, w2_in, w_hi_made, w_split = sem("w1_in"), sem("w2_in"), sem("w_hi_made"), sem("w_split")
        tok_hi_made, tok_split, hid_hi_made, hid_split = (
            sem(n) for n in ("tok_hi_made", "tok_split", "hid_hi_made", "hid_split"))
        tok_in = [sem(f"tok_in{i}") for i in range(2)]
        tok_turned, tok_copied, m1_made, hid_made, m2_made, y_made = (
            sem(n) for n in ("tok_turned", "tok_copied", "m1_made", "hid_made", "m2_made", "y_made"))
        y_out = [sem(f"y_out{i}") for i in range(2)]
        meta_step, meta_made, o_clear, o_made = sem("meta_step"), sem("meta_made"), sem("o_clear"), sem("o_made")
        o_in = [sem(f"o_in{i}") for i in range(2)]
        x1_rows_in = [sem(f"x1_rows_in{i}") for i in range(2)]
        alone_made = sem("alone_made")
        alone_out = [sem(f"alone_out{i}") for i in range(2)]
        o_out = [sem(f"o_out{i}") for i in range(2)]
        gidx_made, check_step, fine_sum = sem("gidx_made"), sem("check_step"), sem("fine_sum")
        yg_in = [sem(f"yg_in{i}") for i in range(2)]
        x1_in = [sem(f"x1_in{i}") for i in range(2)]
        lim_made, fin_step, fin_made, y_in_dram = sem("lim_made"), sem("fin_step"), sem("fin_made"), sem("y_in_dram")
        fin_out = [sem(f"fin_out{i}") for i in range(2)]

        NR = 21
        N_CONST = 14
        NP_FIN = 6
        CHECKS = 1 + 2 * TB * NX * XB + 4

        pool_passed, act_passed, dve_passed = sem("pool_passed"), sem("act_passed"), sem("dve_passed")

        block = ctx.enter_context(nc.Block())

        @block.sync
        def _(sp):
            def edge_load(dst_t, src_d):
                v = src_d[0:EFULL * EP].rearrange("(q n) -> q n", n=EP)
                cut = EFULL // 16 * 16
                sp.dma_start(dst_t[0:cut, :], v[0:cut, :]).then_inc(edges_in, 16)
                sp.dma_start(dst_t[cut:EFULL, :], v[cut:EFULL, :]).then_inc(edges_in, 16)
                sp.dma_start(dst_t[EFULL:P, 0:EREST], src_d[EFULL * EP:E].rearrange("(q n) -> q n", q=1)).then_inc(edges_in, 16)

            sp.wait_ge(e_float, 3)
            edge_load(e_src_i, src)
            edge_load(e_dst_i, dst)
            edge_load(e_w, edge_weight)
            sp.dma_start(neg_diag[:, :], gnn_diag.rearrange("(q n) -> q n", q=1).to_broadcast([P, D])).then_inc(consts_in, 16)
            sp.dma_start(b1_rows[:, :], b1.rearrange("e (m p) -> (e m) p", p=P)).then_inc(consts_in, 16)

            def ln_load(j, slot, tail):
                if tail:
                    sp.dma_start(ln_x[:, slot, 0:TG - 1, :], x[(NT - TG) * P:(NT - 1) * P, :].rearrange("(t p) d -> p t d", p=P)).then_inc(ln_in[slot], 16)
                    sp.dma_start(ln_x[0:NREST, slot, TG - 1, :], x[(NT - 1) * P:N, :]).then_inc(ln_in[slot], 16)
                else:
                    a = TG - 1
                    sp.dma_start(ln_x[:, slot, 0:a, :], x[bass.ds(j * (TG * P), a * P), :].rearrange("(t p) d -> p t d", p=P)).then_inc(ln_in[slot], 16)
                    sp.dma_start(ln_x[:, slot, a, :], x[bass.ds(j * (TG * P) + a * P, P), :]).then_inc(ln_in[slot], 16)

            def ln_store(j, slot):
                sp.wait_ge(ln_xn, j + 1)
                sp.dma_start(acc_dram[0, bass.ds(j * (TG * P), TG * P), :].rearrange("(t p) d -> p t d", p=P), ln_n[:, slot, :, :]).then_inc(ln_out[slot], 16)
                sp.wait_ge(ln_xs, j + 1)
                sp.dma_start(xs_dram[bass.ds(j * (TG * P), TG * P), :].rearrange("(t p) d -> p t d", p=P), ln_s[:, slot, :, :]).then_inc(ln_out[slot], 16)

            ln_load(0, 0, False)
            ln_load(1, 1, False)

            def ln_pair(i, tail):
                for h in range(2):
                    sp.wait_ge(ln_xn, 2 * i + h + 1)
                    ln_load(2 * i + h + 2, h, tail and h == 1)
                    ln_store(2 * i + h, h)

            with sp.Fori(0, NG // 2 - 2) as i:
                ln_pair(i, False)
            ln_pair(NG // 2 - 2, True)
            ln_store(NG - 2, 0)
            ln_store(NG - 1, 1)
            sp.dma_start(bias_t[:, :], gnn_bias.rearrange("(q n) -> q n", q=1).to_broadcast([P, D])).then_inc(late_in, 16)
            sp.dma_start(gateb_t[:, :], gate_b.rearrange("(q n) -> q n", q=1).to_broadcast([P, NX])).then_inc(late_in, 16)
            sp.dma_start(w_sb[:, :, :], gnn_w.rearrange("(k p) n -> p k n", p=P)).then_inc(late_in, 16)
            sp.dma_start(gate_sb[:, :, :], gate_w.rearrange("(k p) n -> p k n", p=P)).then_inc(late_in, 16)
            sp.dma_start(b2_t[:, :, :], b2.rearrange("(q e) n -> q e n", q=1).to_broadcast([P, NX, D])).then_inc(late_in, 16)
            for s in range(2):
                sp.wait_ge(ln_out[s], 32 * (NG // 2))

            sp.wait_ge(flag_ok, 1)
            flag = sp.value_load(flag_i[0:1, 0:1], min_val=0, max_val=P)
            buf_rows = buf_dram[:, :].rearrange("(z p n) d -> z p (n d)", p=P, n=ZB)
            with sp.If(flag == 0):
                def window_load(b, slot, first):
                    if not first:
                        sp.wait_ge(r_made, 4 * (b - 1))
                    base = sp.value_load(base_i[0:1, bass.ds(b, 1)], min_val=0, max_val=N - P)
                    sp.dma_start(window[:, slot, :], xs_dram[bass.ds(base, P), :]).then_inc(win_in[slot], 16)

                for h in range(2):
                    window_load(h, h, True)
                with sp.Fori(1, 1 + BZ) as i:
                    sp.dma_start(buf_rows[bass.ds(i - 1, 1), :, :].rearrange("z p n -> p (z n)"), zeros[:, 0:ZB * HW]).then_inc(buf_zero, 16)
                    for h in range(2):
                        window_load(2 * i + h, h, False)
                with sp.Fori(1 + BZ, NB // 2) as i:
                    for h in range(2):
                        window_load(2 * i + h, h, False)
            with sp.Else():
                with sp.Fori(0, BZ) as z:
                    sp.dma_start(buf_rows[bass.ds(z, 1), :, :].rearrange("z p n -> p (z n)"), zeros[:, 0:ZB * HW]).then_inc(buf_zero, 16)

            sp.wait_ge(scattered, 1)
            def w1_load(e, split):
                if split is not None:
                    sp.wait_ge(w_split, split)
                sp.dma_start(w1_in_sb, w1[bass.ds(e, 1), :, :].rearrange("e (k p) n -> p (e k) n", p=P)).then_inc(w1_in, 16)

            def w2_load(e, split):
                if split is not None:
                    sp.wait_ge(w_split, split)
                sp.dma_start(w2_in_sb, w2[bass.ds(e, 1), :, :].rearrange("e (k p) n -> p (e k) n", p=P)).then_inc(w2_in, 16)

            def sums_load(j, first):
                for t in range(TG):
                    if not first:
                        sp.wait_ge(half_made, TG * (j - 1) + t + 1)
                    sp.dma_start(a_in[:, t, :, :], acc_dram[:, bass.ds(j * (TG * P) + t * P, P), :].rearrange("k p d -> p k d")).then_inc(a_got[t], 16)

            def x_load(j, h, first, tail):
                if not first:
                    sp.wait_ge(x1_made, TG * (j - 1))
                if tail:
                    sp.dma_start(x_in[:, h, 0:TG - 1, :], x[(NT - TG) * P:(NT - 1) * P, :].rearrange("(t p) d -> p t d", p=P)).then_inc(x_got[h], 16)
                    sp.dma_start(x_in[0:NREST, h, TG - 1, :], x[(NT - 1) * P:N, :]).then_inc(x_got[h], 16)
                else:
                    a = TG - 1
                    sp.dma_start(x_in[:, h, 0:a, :], x[bass.ds(j * (TG * P), a * P), :].rearrange("(t p) d -> p t d", p=P)).then_inc(x_got[h], 16)
                    sp.dma_start(x_in[:, h, a, :], x[bass.ds(j * (TG * P) + a * P, P), :]).then_inc(x_got[h], 16)

            def rows_store(dst, j, rows, tail, sem_):
                a = TG - 1
                if tail:
                    sp.dma_start(dst[(NT - TG) * P:(NT - 1) * P, :].rearrange("(t p) d -> p t d", p=P), rows[:, 0:a, :]).then_inc(sem_, 16)
                    sp.dma_start(dst[(NT - 1) * P:N, :], rows[0:NREST, a, :]).then_inc(sem_, 16)
                else:
                    sp.dma_start(dst[bass.ds(j * (TG * P), a * P), :].rearrange("(t p) d -> p t d", p=P), rows[:, 0:a, :]).then_inc(sem_, 16)
                    sp.dma_start(dst[bass.ds(j * (TG * P) + a * P, P), :], rows[:, a, :]).then_inc(sem_, 16)

            def x1_store(j, h):
                sp.wait_ge(x1_made, TG * (j + 1))
                sp.dma_start(x1_dram[bass.ds(j * (TG * P), TG * P), :].rearrange("(t p) d -> p t d", p=P), x1[:, h, :, :]).then_inc(x1_out[h], 16)

            sums_load(0, True)
            x_load(0, 0, True, False)
            x_load(1, 1, True, False)
            sums_load(1, False)

            def node_pair(i, tail):
                for h in range(2):
                    sums_load(2 * i + h + 2, False)
                    x1_store(2 * i + h, h)
                    x_load(2 * i + h + 2, h, False, tail and h == 1)

            with sp.Fori(0, NG // 2 - 2) as i:
                node_pair(i, False)
            node_pair(NG // 2 - 2, True)
            w1_load(0, None)
            w2_load(0, None)
            x1_store(NG - 2, 0)
            x1_store(NG - 1, 1)
            for s in range(2):
                sp.wait_ge(x1_out[s], 16 * (NG // 2))
                sp.wait_ge(h_out[s], 16 * TG * (NG // 2))

            def tokens_load(e, b, first):
                s = b % 2
                if not (first and b < 2):
                    sp.wait_ge(tok_turned, e * XB + b - 1)
                    sp.wait_ge(meta_made, e * XB + b - 1)
                sp.dma_start(tok[:, s, :, :], buf_dram[bass.ds(e * C + b * (TB * P), TB * P), :].rearrange("(t p) d -> p t d", p=P)).then_inc(tok_in[s], 16)

            def y_store(e, b):
                s = b % 2
                sp.wait_ge(y_made, 2 * (e * XB + b + 1))
                a = (TB - 1) * P
                n = min(P, C - b * (TB * P) - a)
                sp.dma_start(y_dram[bass.ds(e * C + b * (TB * P), a), :].rearrange("(t p) d -> p t d", p=P), y_sb[:, s, 0:TB - 1, :]).then_inc(y_out[s], 16)
                sp.dma_start(y_dram[bass.ds(e * C + b * (TB * P) + a, n), :], y_sb[0:n, s, TB - 1, :]).then_inc(y_out[s], 16)

            def x1_rows_load(e, s):
                sp.wait_ge(alone_out[s], 16 * TG * (e - 1))
                sp.dma_start(x1_rows[:, s, :, :], x1_dram[bass.ds((2 * (e - 1) + s) * (TG * P), TG * P), :].rearrange("(t p) d -> p t d", p=P)).then_inc(x1_rows_in[s], 16)

            def expert_loads(e, first, second, last):
                for b in range(XB):
                    tokens_load(e, b, first)
                    if first and b < 2:
                        sp.dma_start(x1_rows[:, b, :, :], x1_dram[b * (TG * P):(b + 1) * (TG * P), :].rearrange("(t p) d -> p t d", p=P)).then_inc(x1_rows_in[b], 16)
                    if not first and not second and b % 2 == 0:
                        x1_rows_load(e, b // 2)
                    if b == XB - 1:
                        y_store(e, 0)
                    elif not first:
                        y_store(e - 1, b + 1)
                    if b == 0 and not last:
                        w1_load(e + 1, XB * e + XB // 2)
                    if b == 2 and not last:
                        w2_load(e + 1, XB * (e + 1))

            expert_loads(0, True, False, False)
            expert_loads(1, False, True, False)
            with sp.Fori(2, NX - 1) as e:
                expert_loads(e, False, False, False)
            expert_loads(NX - 1, False, False, True)
            tokens_load(NX, 0, False)

            for b in range(1, XB):
                y_store(NX - 1, b)

            sp.wait_ge(check_step, CHECKS)
            fine = sp.value_load(fine_i[0:1, 0:1], min_val=0, max_val=P)
            for s in range(2):
                sp.wait_ge(o_out[s], 16 * TB * (NX * XB // 2))
            with sp.If(fine < P):
                sp.wait_ge(y_in_dram, 1)

                def x1_load(j, h, first):
                    if not first:
                        sp.wait_ge(fin_made, j - 1)
                    sp.dma_start(x1b[:, h, :, :], x1_dram[bass.ds(j * (TG * P), TG * P), :].rearrange("(t p) d -> p t d", p=P)).then_inc(x1_in[h], 16)

                def out_store(j, h, tail):
                    sp.wait_ge(fin_made, j + 1)
                    rows_store(out, j, yp[:, h, :, :], tail, fin_out[h])

                x1_load(0, 0, True)
                x1_load(1, 1, True)
                with sp.Fori(0, NG // 2 - 1) as i:
                    for h in range(2):
                        out_store(2 * i + h, h, False)
                        x1_load(2 * i + h + 2, h, False)
                out_store(NG - 2, 0, False)
                out_store(NG - 1, 1, True)
                for s in range(2):
                    sp.wait_ge(fin_out[s], 32 * (NG // 2))

        @block.gpsimd
        def _(pool):
            pool.memset(ident[:, :], 0.0).then_inc(pool_step, 1)
            pool.memset(identb[:, :], 0.0).then_inc(pool_step, 1)
            pool.memset(earlier[:, :], 1.0).then_inc(pool_step, 1)
            pool.memset(upto[:, :], 1.0).then_inc(pool_step, 1)
            pool.memset(row0[:, :], 0.0).then_inc(pool_step, 1)
            pool.memset(valid[:, :], 1.0).then_inc(pool_step, 1)
            pool.memset(onesb[:, :], 1.0).then_inc(const_made, 1)
            pool.memset(onesf[:, :], 1.0).then_inc(const_made, 1)
            pool.memset(eps_t[:, :], EPS).then_inc(const_made, 1)
            pool.iota(iota_i[:, :], pattern=[[1, P]], base=0, channel_multiplier=0).then_inc(const_made, 1)
            pool.iota(node_i[:, :], pattern=[[P, NT]], base=1, channel_multiplier=1).then_inc(const_made, 1)
            pool.iota(part_i[:, :], pattern=[[0, 1]], base=0, channel_multiplier=1).then_inc(const_made, 1)
            for e in range(NX):
                last = pool.memset(falling[:, e:e + 1], float(NX - e))
            last.then_inc(const_made, 1)
            pool.wait_ge(pool_step, 6)
            for t in (ident, identb):
                pool.affine_select(out=t[:, :], in_=t[:, :], compare_op=ALU.not_equal, fill=1.0, base=0,
                                   pattern=[[1, P]], channel_multiplier=-1).then_inc(const_made, 1)
            pool.affine_select(out=earlier[:, :], in_=earlier[:, :], compare_op=ALU.is_gt, fill=0.0, base=0,
                               pattern=[[-1, P]], channel_multiplier=1).then_inc(const_made, 1)
            pool.affine_select(out=upto[:, :], in_=upto[:, :], compare_op=ALU.is_ge, fill=0.0, base=0,
                               pattern=[[1, P]], channel_multiplier=-1).then_inc(const_made, 1)
            pool.memset(row0[0:1, :], 1.0).then_inc(const_made, 1)
            pool.affine_select(out=valid[:, NT - 1:NT], in_=valid[:, NT - 1:NT], compare_op=ALU.is_ge, fill=0.0,
                               base=NREST - 1, pattern=[[0, 1]], channel_multiplier=-1).then_inc(const_made, 1)
            pool.memset(ecols[:, NCH:NCP, :], 0.0).then_inc(const_made, 1)

            def ln_scale(j, h, stored):
                pool.wait_ge(ln_xn, j + 1)
                if stored is not None:
                    pool.wait_ge(ln_out[h], stored)
                pool.tensor_tensor(ln_s[:, h, :, :], ln_n[:, h, :, :],
                                   neg_diag[:, :].unsqueeze(1).to_broadcast([P, TG, D]), ALU.mult).then_inc(ln_xs, 1)

            pool.wait_ge(prep, 4)
            for h in range(2):
                ln_scale(h, h, None)
            with pool.Fori(1, NG // 2) as i:
                for h in range(2):
                    ln_scale(2 * i + h, h, 32 * i)

            pool.wait_ge(acc_zero, 16 * ((COPIES - 1) * (AR // P // ZR) + (AR // P - NT)))
            for s in range(2):
                pool.wait_ge(ln_out[s], 32 * (NG // 2))
            pool.wait_ge(flag_ok, 1)
            flag = pool.value_load(flag_i[0:1, 0:1], min_val=0, max_val=P)
            with pool.If(flag == 0):
                def scatter_group(s, par, first):
                    pool.wait_ge(idx_made, s + 1)
                    for c in range(GC):
                        if c % 2 == 0:
                            pool.wait_ge(r_copied, 2 * s + c // 2 + 1)
                        if not first:
                            pool.wait_ge(acc_add[c], 16 * s)
                        pool.sem_inc(pool_passed, 1)
                        pool.indirect_dma_start(
                            out=acc_flat, out_offset=bass.IndirectOffsetOnAxis(ap=idx_a[:, par, c:c + 1], axis=0),
                            in_=rows[:, par, c, :], in_offset=None, compute_op=ALU.add).then_inc(acc_add[c], 16)

                for g in range(4):
                    scatter_group(g, g % 2, g == 0)
                with pool.Fori(1, NGR // 4) as i:
                    for g in range(4):
                        scatter_group(4 * i + g, g % 2, False)
                for c in range(COPIES):
                    pool.wait_ge(acc_add[c], 16 * NGR)
            with pool.Else():
                def general_group(s, first):
                    pool.wait_ge(gen_staged, s + 1)
                    if not first:
                        pool.wait_ge(gen_r, s)
                    pool.sem_inc(pool_passed, 1)
                    for c in range(GC):
                        pool.indirect_dma_start(
                            out=gathered[:, c, :], out_offset=None, in_=xs_dram[:, :],
                            in_offset=bass.IndirectOffsetOnAxis(ap=stage_d[:, c:c + 1], axis=0)).then_inc(gen_in[c], 16)
                    pool.wait_ge(gen_idx, s + 1)
                    pool.wait_ge(gen_rc, s + 1)
                    pool.sem_inc(pool_passed, 1)
                    for c in range(GC):
                        pool.indirect_dma_start(
                            out=acc_flat, out_offset=bass.IndirectOffsetOnAxis(ap=idx_a[:, 0, c:c + 1], axis=0),
                            in_=rows[:, 0, c, :], in_offset=None, compute_op=ALU.add).then_inc(gen_add[c], 16)
                    for c in range(COPIES):
                        pool.wait_ge(gen_add[c], 16 * (s + 1))
                general_group(0, True)
                with pool.Fori(1, NGR) as s:
                    general_group(s, False)
            pool.sem_inc(scattered, 1)

            pool.wait_ge(late_in, 16 * 5)

            def add_bias(j, h, got):
                pool.wait_ge(x_got[h], got)
                pool.tensor_tensor(x_in[:, h, :, :], x_in[:, h, :, :],
                                   bias_t[:, :].unsqueeze(1).to_broadcast([P, TG, D]), ALU.add).then_inc(xb_made, 1)

            def send_tokens(j, h):
                pool.wait_ge(slot_made, j + 1)
                pool.wait_ge(buf_zero, 16 * BZ)
                pool.sem_inc(pool_passed, 1)
                for t in range(TG):
                    pool.indirect_dma_start(
                        out=buf_dram[:, :], out_offset=bass.IndirectOffsetOnAxis(ap=scat_i[:, h, t:t + 1], axis=0),
                        in_=hn[:, h, t, :], in_offset=None).then_inc(h_out[h], 16)

            add_bias(0, 0, 32)
            add_bias(1, 1, 32)
            with pool.Fori(0, NG // 2 - 1) as i:
                for h in range(2):
                    add_bias(2 * i + h + 2, h, 32 * (i + 2))
                    send_tokens(2 * i + h, h)
            send_tokens(NG - 2, 0)
            send_tokens(NG - 1, 1)

            for s in range(2):
                pool.wait_ge(x1_out[s], 16 * (NG // 2))
            pool.wait_ge(o_clear, 1)

            def tile_rows(b, t):
                return min(P, C - (b * TB + t) * P)

            def x1_gather(e, b, first):
                n = e * XB + b
                s = b % 2
                pool.wait_ge(meta_made, n + 1)
                if not (first and b < 2):
                    pool.wait_ge(o_out[s], 16 * TB * (e * (XB // 2) + b // 2))
                pool.sem_inc(pool_passed, 1)
                for t in range(TB):
                    w = tile_rows(b, t)
                    pool.indirect_dma_start(
                        out=o_sb[0:w, s, t, :], out_offset=None, in_=x1_dram[:, :],
                        in_offset=bass.IndirectOffsetOnAxis(ap=meta_i[0:w, s, t:t + 1], axis=0),
                        bounds_check=N - 1, oob_is_err=False).then_inc(o_in[s], 16)

            def out_scatter(e, b):
                n = e * XB + b
                s = b % 2
                pool.wait_ge(o_made, n + 1)
                pool.sem_inc(pool_passed, 1)
                for t in range(TB):
                    w = tile_rows(b, t)
                    pool.indirect_dma_start(
                        out=out, out_offset=bass.IndirectOffsetOnAxis(ap=meta_i[0:w, s, t:t + 1], axis=0),
                        in_=o_sb[0:w, s, t, :], in_offset=None,
                        bounds_check=N - 1, oob_is_err=False).then_inc(o_out[s], 16)

            def alone_scatter(e, s):
                pool.wait_ge(x1_rows_in[s], 16 * e)
                pool.tensor_copy(alone_i[:, s, 0:TG], alone[:, bass.ds((2 * (e - 1) + s) * TG, TG)]).then_inc(alone_made, 1)
                pool.wait_ge(alone_made, 2 * (e - 1) + s + 1)
                pool.sem_inc(pool_passed, 1)
                for t in range(TG):
                    pool.indirect_dma_start(
                        out=out, out_offset=bass.IndirectOffsetOnAxis(ap=alone_i[:, s, t:t + 1], axis=0),
                        in_=x1_rows[:, s, t, :], in_offset=None,
                        bounds_check=N - 1, oob_is_err=False).then_inc(alone_out[s], 16)

            x1_gather(0, 0, True)
            for b in range(1, XB):
                x1_gather(0, b, True)
                out_scatter(0, b - 1)
            with pool.Fori(1, NX) as e:
                for b in range(XB):
                    x1_gather(e, b, False)
                    if b == 0:
                        out_scatter(e - 1, XB - 1)
                    else:
                        out_scatter(e, b - 1)
                    if b % 2:
                        alone_scatter(e, b // 2)
            out_scatter(NX - 1, XB - 1)
            for s in range(2):
                pool.wait_ge(o_out[s], 16 * TB * (NX * XB // 2))
                pool.wait_ge(y_out[s], 32 * (NX * XB // 2))
                pool.wait_ge(alone_out[s], 16 * TG * (NG // 2))
            pool.sem_inc(y_in_dram, 1)

            pool.wait_ge(check_step, CHECKS)
            fine = pool.value_load(fine_i[0:1, 0:1], min_val=0, max_val=P)
            with pool.If(fine < P):
                def gather_y(j, h, first):
                    if not first:
                        pool.wait_ge(fin_made, j - 1)
                    pool.tensor_copy(gidx[:, h, 0:TG], gather_row[:, bass.ds(j * TG, TG)]).then_inc(gidx_made, 1)
                    pool.wait_ge(gidx_made, j + 1)
                    pool.sem_inc(pool_passed, 1)
                    for t in range(TG):
                        pool.indirect_dma_start(
                            out=yg[:, h, t, :], out_offset=None, in_=y_dram[:, :],
                            in_offset=bass.IndirectOffsetOnAxis(ap=gidx[:, h, t:t + 1], axis=0)).then_inc(yg_in[h], 16)

                for h in range(2):
                    gather_y(h, h, True)
                with pool.Fori(1, NG // 2) as i:
                    for h in range(2):
                        gather_y(2 * i + h, h, False)

        @block.scalar
        def _(act):
            act.wait_ge(zeros_ok, 1)
            nz = AR // P // ZR
            for k in range(1, COPIES):
                v = acc_dram[k, :, :].rearrange("(p n) d -> p (n d)", p=P)
                for z in range(nz):
                    act.dma_start(v[:, z * ZR * D:(z + 1) * ZR * D], zeros).then_inc(acc_zero, 16)
            for z in range(0, AR - NT * P, P):
                act.dma_start(acc_dram[0, NT * P + z:NT * P + z + P, :], zeros[:, 0:D]).then_inc(acc_zero, 16)

            for k in range(EQ):
                for a in range(3):
                    n = 3 * k + a
                    act.wait_ge(e_turned, n + 1)
                    q = bank(n % 4, 0, P)
                    act.copy(ecols[:, k:NCH:EQ, a], q).then_inc(e_col, 1)
            act.wait_ge(b1_turned, 1)
            act.copy(b1_t[:, :], bank(4, 0, NX * KF)).then_inc(b1_ok, 1)

            act.wait_ge(const_made, N_CONST)
            with act.Fori(0, NG // 2) as i:
                for h in range(2):
                    act.wait_ge(ln_mean, 2 * i + h + 1)
                    act.activation(ln_std[:, h, :], ln_mv[:, h, :, 1], ACT.Sqrt, bias=eps_t[:, 0:1]).then_inc(ln_sq, 1)

            act.wait_ge(flag_ok, 1)
            flag = act.value_load(flag_i[0:1, 0:1], min_val=0, max_val=P)
            act.wait_ge(ln_out[0], 32 * (NG // 2))
            act.wait_ge(ln_out[1], 32 * (NG // 2))
            with act.If(flag == 0):
                def stage(s, par):
                    act.copy(stage_s[:, par, :, :], esplit[:, bass.ds(s * GC, GC), :])
                    act.copy(stage_e[:, par, :, :], ecols[:, bass.ds(s * GC, GC), :]).then_inc(staged, 1)

                def copy_group(s, par, g, peeled):
                    if not (peeled and g == 0):
                        act.wait_ge(idx_made, s)
                    stage(s + 1, 1 - par)
                    for c in range(2):
                        act.wait_ge(g_made, 2 * s + c + 1)
                        if not (peeled and g < 2):
                            act.wait_ge(r_made, 2 * (s - 1))
                        act.copy(g_sb[:, par, 2 * c:2 * c + 2, :], bank(2 + c, 0, 2 * P).rearrange("p (a b) -> p a b", b=P)).then_inc(g_copied, 1)
                    for c in range(2):
                        act.wait_ge(r_made, 2 * s + c + 1)
                        if not (peeled and g < 2):
                            for k in (2 * c, 2 * c + 1):
                                act.wait_ge(acc_add[k], 16 * (s - 1))
                        act.copy(rows[:, par, 2 * c:2 * c + 2, :], bank(4 + 2 * par + c).rearrange("p (a b) -> p a b", b=D)).then_inc(r_copied, 1)

                stage(0, 0)
                for g in range(4):
                    copy_group(g, g % 2, g, True)
                with act.Fori(1, NGR // 4) as i:
                    for g in range(4):
                        copy_group(4 * i + g, g % 2, g, False)
            with act.Else():
                def general_copy(s, first):
                    if not first:
                        act.wait_ge(gen_idx, s)
                        act.wait_ge(gen_r, s)
                    act.copy(stage_s[:, 0, :, :], esplit[:, bass.ds(s * GC, GC), :])
                    act.copy(stage_e[:, 0, :, :], ecols[:, bass.ds(s * GC, GC), :])
                    act.copy(stage_d[:, :], dcols[:, bass.ds(s * GC, GC)]).then_inc(gen_staged, 1)
                    act.wait_ge(gen_r, s + 1)
                    if not first:
                        for c in range(COPIES):
                            act.wait_ge(gen_add[c], 16 * s)
                    for c in range(2):
                        last = act.copy(rows[:, 0, 2 * c:2 * c + 2, :], bank(4 + c).rearrange("p (a b) -> p a b", b=D))
                    last.then_inc(gen_rc, 1)
                general_copy(0, True)
                with act.Fori(1, NGR) as s:
                    general_copy(s, False)

            act.wait_ge(scattered, 1)

            def copy_e4(j, t, peeled):
                act.wait_ge(e4_turned, TG * j + t + 1)
                if not (peeled and t < 2):
                    act.wait_ge(w_made, TG * j + t - 1)
                act.copy(e4t[:, t % 2, :, :], bank(4 + t % 2, 0, D).rearrange("p (a b) -> p a b", b=P)).then_inc(e4_copied, 1)

            def copy_h(j, t, peeled):
                act.wait_ge(h_turned, TG * j + t + 1)
                if not (peeled and t < 2):
                    act.wait_ge(lg_made, TG * j + t - 1)
                act.copy(hnt[:, t % 2, :, :], bank(5 - t % 2, 0, D).rearrange("p (a b) -> p a b", b=P)).then_inc(h_copied, 1)

            def root(j):
                act.wait_ge(mv_made, j + 1)
                act.activation(std3, mv3[:, :, 1], ACT.Sqrt, bias=eps_t[:, 0:1]).then_inc(std_made, 1)

            def exponentials(j):
                act.wait_ge(route, NR * j + 3)
                act.activation(pr, t56, ACT.Exp).then_inc(exp_made, 1)

            for t in range(TG):
                copy_e4(0, t, True)

            def make_h(j, h, fills, t0, t1):
                if t0 == 0:
                    act.wait_ge(shift_made, j + 1)
                    if fills is not None:
                        act.wait_ge(h_out[h], 16 * TG * fills)
                    act.sem_inc(act_passed, 1)
                for t in range(t0, t1):
                    act.activation(hn[:, h, t, 0:D], x1[:, h, t, :], ACT.Identity, bias=shift3[:, t:t + 1], scale=rstd3[:, t:t + 1]).then_inc(h_made, 1)

            def turned_group(j, h, fills, first):
                for t in range(TG):
                    copy_e4(j, t, False)
                    if t == 1:
                        root(j - 1)
                    if t >= 3:
                        make_h(j - 1, h, fills, max(0, 2 * t - 7), 2 * t - 5)
                for t in range(TG):
                    copy_h(j - 1, t, first)
                exponentials(j - 1)

            turned_group(1, 0, None, True)
            turned_group(2, 1, None, False)
            with act.Fori(1, NG // 2 - 1) as i:
                for h in range(2):
                    turned_group(2 * i + h + 1, h, i, False)
            turned_group(NG - 1, 0, NG // 2 - 1, False)
            root(NG - 1)
            make_h(NG - 1, 1, NG // 2 - 1, 0, TG)
            for t in range(TG):
                copy_h(NG - 1, t, False)
            exponentials(NG - 1)

            act.wait_ge(b1_ok, 1)
            for s in range(2):
                act.wait_ge(h_out[s], 16 * TG * (NG // 2))

            def turn_copy(n, first):
                act.wait_ge(tok_turned, n + 1)
                if not first:
                    act.wait_ge(tok_split, n)
                for k in range(KD):
                    last = act.copy(tokT[:, k, :], bank(k))
                last.then_inc(tok_copied, 1)

            def expert_block(e, b, first):
                n = e * XB + b
                cols = min(TB * P, C - b * TB * P)
                for m in range(KF):
                    act.wait_ge(m1_made, KF * n + m + 1)
                    if not (first and b == 0 and m < 2):
                        act.wait_ge(hid_split, KF * n + m - 1)
                    act.sem_inc(act_passed, 1)
                    act.activation(hid[:, m % 2, 0:cols], bank(2 + m % 4, 0, cols), ACT.Relu, bias=b1_t[:, bass.ds(e * KF + m, 1)]).then_inc(hid_made, 1)
                turn_copy(n + 1, False)

            turn_copy(0, True)
            for b in range(XB):
                expert_block(0, b, True)
            with act.Fori(1, NX) as e:
                for b in range(XB):
                    expert_block(e, b, False)

        @block.tensor
        def _(pe):
            pe.wait_ge(const_made, N_CONST)
            pe.wait_ge(e_float, 5)
            pe.wait_ge(edges_in, 16 * 9)
            for k in range(EQ):
                for a, t in enumerate((e_src, e_w, e_dst)):
                    n = 3 * k + a
                    if n >= 4:
                        pe.wait_ge(e_col, n - 3)
                    pe.transpose(bank(n % 4, 0, P), t[:, k * P:(k + 1) * P], ident[:, :]).then_inc(e_turned, 1)
            pe.wait_ge(consts_in, 32)
            pe.transpose(bank(4, 0, NX * KF), b1_rows[:, :], ident[0:NX * KF, 0:NX * KF]).then_inc(b1_turned, 1)
            pe.wait_ge(e_col, 3 * EQ)
            pe.matmul(bank(0, 0, NB), row0[:, :], ecols[:, 0:NCH:BC, 2], start=True, stop=True).then_inc(base_bc, 1)
            pe.wait_ge(prep, 11)
            pe.matmul(bank(1, 0, 1), onesf[:, :], spread[:, 3:4], start=True, stop=True).then_inc(flag_sum, 1)

            pe.wait_ge(flag_ok, 1)
            flag = pe.value_load(flag_i[0:1, 0:1], min_val=0, max_val=P)
            with pe.If(flag == 0):
                def broadcast_src(par, sem_, b0):
                    for c in range(GC):
                        for k in range(2):
                            mm = pe.matmul(bank(b0 + par, c * P, (c + 1) * P), stage_s[:, par, c, k:k + 1].to_broadcast([P, P]),
                                           identb[:, :], start=(k == 0), stop=(k == 1))
                    mm.then_inc(sem_, 1)

                def product_group(s, par, g, fills, peeled):
                    for c in range(GC):
                        pe.wait_ge(oh_made, GC * s + c + 1)
                        if c % 2 == 0 and not (peeled and g == 0):
                            pe.wait_ge(g_copied, 2 * (s - 1) + c // 2 + 1)
                        mm = pe.matmul(bank(2 + c // 2, (c % 2) * P, (c % 2 + 1) * P), is_node[:, par, c, :], same_w[:, par, c, :], start=True, stop=True)
                        if c % 2:
                            mm.then_inc(g_made, 1)
                    pe.wait_ge(staged, s + 2)
                    if not (peeled and g == 0):
                        pe.wait_ge(idx_made, s)
                    broadcast_src(1 - par, bc_made, 0)
                    if g % 2 == 0:
                        pe.wait_ge(win_in[g // 2], 16 * fills)
                    for c in range(GC):
                        if c % 2 == 0:
                            pe.wait_ge(g_copied, 2 * s + c // 2 + 1)
                            if not (peeled and g < 2):
                                pe.wait_ge(r_copied, 2 * (s - 2) + c // 2 + 1)
                        mm = pe.matmul(bank(4 + 2 * par + c // 2, (c % 2) * D, (c % 2 + 1) * D), g_sb[:, par, c, :], window[:, g // 2, :], start=True, stop=True)
                        if c % 2:
                            mm.then_inc(r_made, 1)

                pe.wait_ge(staged, 1)
                broadcast_src(0, bc_made, 0)
                for g in range(4):
                    product_group(g, g % 2, g, 1, True)
                with pe.Fori(1, NGR // 4) as i:
                    for g in range(4):
                        product_group(4 * i + g, g % 2, g, i + 1, False)
            with pe.Else():
                def general_products(s, first):
                    pe.wait_ge(gen_staged, s + 1)
                    if not first:
                        pe.wait_ge(gen_idx, s)
                    for c in range(GC):
                        for k in range(2):
                            mm = pe.matmul(bank(0, c * P, (c + 1) * P), stage_s[:, 0, c, k:k + 1].to_broadcast([P, P]),
                                           identb[:, :], start=(k == 0), stop=(k == 1))
                    mm.then_inc(gen_bc, 1)
                    pe.wait_ge(gen_same, s + 1)
                    if not first:
                        pe.wait_ge(gen_rc, s)
                    for c in range(GC):
                        pe.wait_ge(gen_in[c], 16 * (s + 1))
                        mm = pe.matmul(bank(4 + c // 2, (c % 2) * D, (c % 2 + 1) * D), same_w[:, 0, c, :], gathered[:, c, :], start=True, stop=True)
                    mm.then_inc(gen_r, 1)
                general_products(0, True)
                with pe.Fori(1, NGR) as s:
                    general_products(s, False)

            pe.wait_ge(late_in, 16 * 5)

            def o_bank(t):
                return bank(t // 2, (t % 2) * D, (t % 2 + 1) * D)

            def turn_and_multiply(j, order, rank):
                for t in range(TG + 1):
                    if t < TG:
                        pe.wait_ge(e4_made, TG * j + t + 1)
                        if t >= 2:
                            pe.wait_ge(e4_copied, TG * j + t - 1)
                        elif order == 1:
                            pe.wait_ge(e4_copied, TG)
                        elif order == 2:
                            pe.wait_ge(h_copied, TG * (j - 2) + TG - 1 + t)
                        for k in range(KD):
                            mm = pe.transpose(bank(4 + t % 2, k * P, (k + 1) * P), e4[:, t, k * P:(k + 1) * P], ident[:, :])
                        mm.then_inc(e4_turned, 1)
                    if t >= 1:
                        u = t - 1
                        pe.wait_ge(e4_copied, TG * j + u + 1)
                        if u == 0 and order > 0:
                            pe.wait_ge(x1_made, TG * j)
                        for k in range(KD):
                            mm = pe.matmul(o_bank(u), e4t[:, u % 2, k, :], w_sb[:, k, :], start=(k == 0), stop=(k == KD - 1))
                        mm.then_inc(w_made, 1)
                    if t == 2 and rank is not None:
                        rank_products(*rank)

            def turn_and_gate(j, h, first, last):
                for t in range(TG + 1):
                    if t < TG:
                        pe.wait_ge(h_made, TG * j + t + 1)
                        if t >= 2:
                            pe.wait_ge(h_copied, TG * j + t - 1)
                        elif last:
                            pe.wait_ge(h_copied, TG * j)
                        else:
                            pe.wait_ge(e4_copied, TG * (j + 1) + TG - 1 + t)
                        for k in range(KD):
                            mm = pe.transpose(bank(5 - t % 2, k * P, (k + 1) * P), hn[:, h, t, k * P:(k + 1) * P], ident[:, :])
                        mm.then_inc(h_turned, 1)
                    if t >= 1:
                        u = t - 1
                        pe.wait_ge(h_copied, TG * j + u + 1)
                        if u == 0 and not first:
                            pe.wait_ge(route, NR * (j - 1) + 1)
                        for k in range(KD):
                            mm = pe.matmul(bank(6, u * NX, (u + 1) * NX), hnt[:, u % 2, k, :], gate_sb[:, k, :], start=(k == 0), stop=(k == KD - 1))
                        mm.then_inc(lg_made, 1)

            def rank_products(j, first):
                pe.wait_ge(route, NR * j + 12)
                if not first:
                    pe.wait_ge(route, NR * j)
                r_out = bank(7, 0, TG * NX)
                pe.matmul(r_out, onesb[:, :], seenb.unsqueeze(1).to_broadcast([P, TG, NX]), start=True, stop=True)
                for t in range(TG - 1):
                    pe.matmul(bank(7, (t + 1) * NX, TG * NX).rearrange("p (a b) -> p a b", b=NX), onesb[:, :],
                              ohb[:, t:t + 1, :].to_broadcast([P, TG - 1 - t, NX]), start=False, stop=True, skip_group_check=True)
                pe.matmul(r_out, upto[:, :], ohb[:, :, :].rearrange("p a b -> p (a b)"),
                          start=False, stop=True, skip_group_check=True).then_inc(rank_made, 1)

            turn_and_multiply(0, 0, None)
            turn_and_multiply(1, 1, None)
            turn_and_gate(0, 0, True, False)
            turn_and_multiply(2, 2, (0, True))
            turn_and_gate(1, 1, False, False)
            with pe.Fori(1, NG // 2 - 1) as i:
                for h in range(2):
                    j = 2 * i + h
                    turn_and_multiply(j + 1, 2, (j - 1, False))
                    turn_and_gate(j, h, False, False)
            turn_and_multiply(NG - 1, 2, (NG - 3, False))
            turn_and_gate(NG - 2, 0, False, False)
            rank_products(NG - 2, False)
            turn_and_gate(NG - 1, 1, False, True)
            rank_products(NG - 1, False)

            def turn_tokens(n, s, first):
                if not first:
                    pe.wait_ge(tok_copied, n)
                for k in range(KD):
                    for t in range(TB):
                        mm = pe.transpose(bank(k, t * P, (t + 1) * P), tok[:, s, t, k * P:(k + 1) * P], ident[:, :])
                mm.then_inc(tok_turned, 1)

            def expert_products(e, s_e, b, first):
                n = e * XB + b
                cols = min(TB * P, C - b * TB * P)
                pe.wait_ge(tok_split, n + 1)
                for m in range(KF):
                    if not (first and b == 0 and m < 4):
                        pe.wait_ge(hid_made, KF * n + m - 3)
                    for k in range(KD):
                        for i, (w, tk) in enumerate(((w1_hi, tok_hi), (w1_hi, tok_lo), (w1_lo, tok_hi))):
                            mm = pe.matmul(bank(2 + m % 4, 0, cols), w[:, s_e, k, m * P:(m + 1) * P], tk[:, k, 0:cols],
                                           start=(k + i == 0), stop=(k == KD - 1 and i == 2))
                    mm.then_inc(m1_made, 1)

            def expert_out(e, s_e, b, first):
                n = e * XB + b
                cols = min(TB * P, C - b * TB * P)
                for t in range(TB):
                    w = min(P, cols - t * P)
                    if t % 2 == 0 and not (first and b == 0):
                        pe.wait_ge(y_made, 2 * n - 1 + t // 2)
                    for m in range(KF):
                        if t == 0:
                            pe.wait_ge(hid_split, KF * n + m + 1)
                        for i, (hd, wt) in enumerate(((hid_hi, w2_hi), (hid_hi, w2_lo), (hid_lo, w2_hi))):
                            mm = pe.matmul(bank(6 + t // 2, (t % 2) * D, (t % 2 + 1) * D)[0:w, :], hd[:, m, t * P:t * P + w], wt[:, s_e, m, :],
                                           start=(m + i == 0), stop=(m == KF - 1 and i == 2))
                    if t % 2:
                        mm.then_inc(m2_made, 1)

            pe.wait_ge(tok_in[0], 16)
            turn_tokens(0, 0, True)

            def expert(e, s_e, toks, first):
                pe.wait_ge(w_split, XB * (e + 1))
                for b in range(XB):
                    expert_products(e, s_e, b, first)
                    pe.wait_ge(tok_in[(b + 1) % 2], 16 * (toks + (b + 1) // 2 + 1))
                    turn_tokens(e * XB + b + 1, (b + 1) % 2, False)
                    expert_out(e, s_e, b, first)

            expert(0, 0, 0, True)
            expert(1, 1, XB // 2, False)
            with pe.Fori(1, NX // 2) as i:
                for s_e in range(2):
                    expert(2 * i + s_e, s_e, (2 * i + s_e) * (XB // 2), False)
            pe.wait_ge(check_step, 1 + 2 * TB * NX * XB + 3)
            pe.wait_ge(tok_copied, NX * XB + 1)
            pe.matmul(bank(0, 0, 1), onesf[:, :], zero_part[:, :], start=True, stop=True).then_inc(fine_sum, 1)

        @block.vector
        def _(dve):
            dve.memset(e_src_i[96:P, :], PAD_NODE).then_inc(e_float, 1)
            dve.memset(e_dst_i[96:P, :], N - 1).then_inc(e_float, 1)
            dve.memset(e_w[96:P, :], 0.0).then_inc(e_float, 1)
            dve.memset(zeros, 0.0).then_inc(zeros_ok, 1)
            dve.memset(esplit[:, NCH:NCP, :], 0.0)
            dve.wait_ge(edges_in, 16 * 9)
            dve.tensor_copy(e_src, e_src_i).then_inc(e_float, 1)
            dve.tensor_copy(e_dst, e_dst_i).then_inc(e_float, 1)
            dve.wait_ge(const_made, N_CONST)
            dve.tensor_copy(iota_f[:, :], iota_i[:, :]).then_inc(prep, 1)
            dve.tensor_scalar(acc_dump[:, :], part_i[:, :], float(DUMP), None, ALU.add).then_inc(prep, 1)
            for n in range(2 * TG):
                last = dve.tensor_scalar(buf_dump[:, n:n + 1], part_i[:, :], float(BDUMP + n * P), None, ALU.add)
            last.then_inc(prep, 1)
            dve.tensor_copy(node1[:, :], node_i[:, :])
            dve.tensor_scalar(node0[:, :], node_i[:, :], -1.0, None, ALU.add)
            for c in range(COPIES):
                dve.tensor_scalar(acc_dump4[:, c:c + 1], part_i[:, :], float(DUMP + c * AR), None, ALU.add)
            dve.wait_ge(consts_in, 32)
            dve.tensor_scalar(neg_diag[:, :], neg_diag[:, :], -1.0, -1.0, ALU.mult, ALU.add).then_inc(prep, 1)
            dve.wait_ge(e_col, 3 * EQ)
            dve.tensor_copy(src_i, ecols[:, 0:NCH, 0]).then_inc(prep, 1)
            dve.tensor_copy(dcols[:, 0:NCH], ecols[:, 0:NCH, 2])
            dve.memset(dcols[:, NCH:NCP], 0)
            dve.wait_ge(prep, 5)
            dve.tensor_scalar(src_part, src_i, ~127, None, ALU.bitwise_and).then_inc(prep, 1)
            dve.tensor_scalar(src_i, src_i, 127, None, ALU.bitwise_and).then_inc(prep, 1)
            dve.wait_ge(prep, 7)
            dve.tensor_copy(esplit[:, 0:NCH, 0], src_part)
            dve.tensor_copy(esplit[:, 0:NCH, 1], src_i)
            dve.wait_ge(base_bc, 1)
            dve.tensor_scalar(base_f[:, :], bank(0, 0, NB), float(N - P), None, ALU.min).then_inc(prep, 1)
            dve.wait_ge(prep, 8)
            dve.tensor_copy(base_i[:, :], base_f[:, :])
            rel = ecols[:, 0:NCH, 2].rearrange("p (b c) -> p b c", c=BC)
            dve.tensor_tensor(rel, rel, base_f[:, :].unsqueeze(2).to_broadcast([P, NB, BC]), ALU.subtract).then_inc(prep, 1)
            dve.wait_ge(prep, 9)
            dve.tensor_reduce(spread[:, 0:1], ecols[:, 0:NCH, 2], AX_X, ALU.max)
            dve.tensor_reduce(spread[:, 1:2], ecols[:, 0:NCH, 2], AX_X, ALU.min).then_inc(prep, 1)
            dve.wait_ge(prep, 10)
            dve.tensor_scalar(spread[:, 2:3], spread[:, 0:1], float(P - 1), None, ALU.is_gt).then_inc(base_out, 1)
            dve.wait_ge(base_out, 1)
            dve.scalar_tensor_tensor(out=spread[:, 3:4], in0=spread[:, 1:2], scalar=0.0, in1=spread[:, 2:3], op0=ALU.is_lt, op1=ALU.max).then_inc(prep, 1)
            dve.wait_ge(flag_sum, 1)
            dve.tensor_copy(flag_i[:, :], bank(1, 0, 1)).then_inc(flag_ok, 1)

            def ln_group(j, h, fills):
                dve.wait_ge(ln_in[h], 32 if fills is None else 32 * (fills + 1))
                for t in range(TG):
                    last = dve.bn_stats(ln_stat[:, h, t, :], ln_x[:, h, t, :])
                last.then_inc(ln_step, 1)
                dve.wait_ge(ln_step, 2 * j + 1)
                dve.sem_inc(dve_passed, 1)
                for t in range(TG):
                    last = dve.bn_aggr(ln_mv[:, h, t, :], ln_stat[:, h, t, :])
                last.then_inc(ln_mean, 1)
                dve.wait_ge(ln_sq, j + 1)
                dve.reciprocal(ln_rstd[:, h, :], ln_std[:, h, :]).then_inc(ln_step, 1)
                dve.wait_ge(ln_step, 2 * j + 2)
                if fills is not None:
                    dve.wait_ge(ln_out[h], 32 * fills)
                for t in range(TG):
                    last = dve.tensor_scalar(ln_n[:, h, t, :], ln_x[:, h, t, :], ln_mv[:, h, t, 0:1], ln_rstd[:, h, t:t + 1], ALU.subtract, ALU.mult)
                last.then_inc(ln_xn, 1)

            for h in range(2):
                ln_group(h, h, None)
            with dve.Fori(1, NG // 2) as i:
                for h in range(2):
                    ln_group(2 * i + h, h, i)

            flag = dve.value_load(flag_i[0:1, 0:1], min_val=0, max_val=P)
            dve.wait_ge(ln_out[0], 32 * (NG // 2))
            dve.wait_ge(ln_out[1], 32 * (NG // 2))
            with dve.If(flag == 0):
                def match_group(s, par, g, peeled):
                    dve.wait_ge(bc_made, s + 1)
                    if not (peeled and g < 2):
                        dve.wait_ge(g_made, 2 * (s - 1))
                    for c in range(GC):
                        srcs = bank(par, c * P, (c + 1) * P)
                        dve.tensor_scalar(same_w[:, par, c, :], srcs, stage_e[:, par, c, 0:1], stage_e[:, par, c, 1:2], ALU.is_equal, ALU.mult)
                        dve.tensor_scalar(is_node[:, par, c, :], iota_f[:, :], stage_e[:, par, c, 2:3], None, ALU.is_equal).then_inc(oh_made, 1)
                    for c in range(GC):
                        last = dve.scalar_tensor_tensor(out=picked[:, par, c, :], in0=bank(par, c * P, (c + 1) * P), scalar=stage_e[:, par, c, 0:1],
                                                        in1=earlier[:, :], op0=ALU.is_equal, op1=ALU.mult, accum_out=sooner[:, par, c:c + 1])
                    dve.tensor_scalar(offs[:, par, :], stage_e[:, par, :, 0], acc_dump[:, 0:1], None, ALU.subtract).then_inc(idx_step, 1)
                    dve.wait_ge(idx_step, 2 * s + 1)
                    dve.scalar_tensor_tensor(out=idx_f[:, par, :], in0=sooner[:, par, :], scalar=0.0, in1=offs[:, par, :], op0=ALU.is_equal, op1=ALU.mult).then_inc(idx_step, 1)
                    dve.wait_ge(idx_step, 2 * s + 2)
                    if not (peeled and g < 2):
                        for c in range(COPIES):
                            dve.wait_ge(acc_add[c], 16 * (s - 1))
                    dve.tensor_tensor(idx_a[:, par, :], idx_f[:, par, :], acc_dump4[:, :], ALU.add).then_inc(idx_made, 1)

                for g in range(4):
                    match_group(g, g % 2, g, True)
                with dve.Fori(1, NGR // 4) as i:
                    for g in range(4):
                        match_group(4 * i + g, g % 2, g, False)
            with dve.Else():
                def general_match(s, first):
                    dve.wait_ge(gen_bc, s + 1)
                    if not first:
                        dve.wait_ge(gen_r, s)
                        for c in range(COPIES):
                            dve.wait_ge(gen_add[c], 16 * s)
                    for c in range(GC):
                        last = dve.tensor_scalar(same_w[:, 0, c, :], bank(0, c * P, (c + 1) * P), stage_e[:, 0, c, 0:1], stage_e[:, 0, c, 1:2], ALU.is_equal, ALU.mult)
                    last.then_inc(gen_same, 1)
                    for c in range(GC):
                        dve.scalar_tensor_tensor(out=picked[:, 0, c, :], in0=bank(0, c * P, (c + 1) * P), scalar=stage_e[:, 0, c, 0:1],
                                                 in1=earlier[:, :], op0=ALU.is_equal, op1=ALU.mult, accum_out=sooner[:, 0, c:c + 1])
                    dve.tensor_scalar(offs[:, 0, :], stage_e[:, 0, :, 0], acc_dump[:, 0:1], None, ALU.subtract).then_inc(gen_step, 1)
                    dve.wait_ge(gen_step, 2 * s + 1)
                    dve.scalar_tensor_tensor(out=idx_f[:, 0, :], in0=sooner[:, 0, :], scalar=0.0, in1=offs[:, 0, :], op0=ALU.is_equal, op1=ALU.mult).then_inc(gen_step, 1)
                    dve.wait_ge(gen_step, 2 * s + 2)
                    dve.tensor_tensor(idx_a[:, 0, :], idx_f[:, 0, :], acc_dump4[:, :], ALU.add).then_inc(gen_idx, 1)
                general_match(0, True)
                with dve.Fori(1, NGR) as s:
                    general_match(s, False)

            dve.wait_ge(scattered, 1)
            dve.wait_ge(late_in, 16 * 5)
            dve.memset(seen, 0.0)
            dve.memset(seenb, 0.0)

            def sum_half(t, fills):
                dve.wait_ge(a_got[t], 16 * fills)
                dve.tensor_tensor(half[:, t, :, :], a_in[:, t, 0:2, :], a_in[:, t, 2:4, :], ALU.add).then_inc(half_made, 1)

            def sum_rest(j, t):
                dve.wait_ge(half_made, TG * j + t + 1)
                dve.tensor_tensor(e4[:, t, :], half[:, t, 0, :], half[:, t, 1, :], ALU.add).then_inc(e4_made, 1)

            def step(ins, j, n):
                ins.then_inc(route, 1)
                dve.wait_ge(route, NR * j + n)

            def over_experts(v):
                return v.unsqueeze(2).to_broadcast([P, TG, NX])

            def over_tiles(v):
                return v.unsqueeze(1).to_broadcast([P, TG, NX])

            mx, sm, rc, prb, top, pos, kept, base, rowf, under, k2, sidx = c7

            def route_logits(j):
                dve.wait_ge(lg_made, TG * (j + 1))
                step(dve.tensor_tensor(lg, bank(6, 0, TG * NX).rearrange("p (a b) -> p a b", b=NX), over_tiles(gateb_t[:, :]), ALU.add), j, 1)
                step(dve.tensor_reduce(mx, lg, AX_X, ALU.max), j, 2)
                step(dve.tensor_tensor(t56, lg, over_experts(mx), ALU.subtract), j, 3)

            def route_choice(j):
                dve.wait_ge(exp_made, j + 1)
                step(dve.tensor_reduce(sm, pr, AX_X, ALU.add), j, 4)
                step(dve.reciprocal(rc, sm), j, 5)
                step(dve.tensor_tensor(pr, pr, over_experts(rc), ALU.mult), j, 6)
                step(dve.tensor_reduce(prb, pr, AX_X, ALU.max), j, 7)
                step(dve.tensor_tensor(t56, pr, over_experts(prb), ALU.is_equal), j, 8)
                step(dve.tensor_tensor(t56, t56, over_tiles(falling[:, :]), ALU.mult), j, 9)
                step(dve.tensor_reduce(top, t56, AX_X, ALU.max), j, 10)
                step(dve.tensor_tensor(oh, over_experts(top), over_tiles(falling[:, :]), ALU.is_equal), j, 11)
                step(dve.tensor_tensor(ohb, oh, over_experts(valid[:, bass.ds(j * TG, TG)]), ALU.mult), j, 12)

            def route_rows(j, h):
                dve.wait_ge(rank_made, j + 1)
                step(dve.tensor_tensor(t56, bank(7, 0, TG * NX).rearrange("p (a b) -> p a b", b=NX), ohb, ALU.mult), j, 13)
                step(dve.tensor_reduce(pos, t56, AX_X, ALU.add), j, 14)
                step(dve.tensor_reduce(new8, ohb.rearrange("p a b -> p b a"), AX_X, ALU.add), j, 15)
                dve.tensor_scalar(base, top, -float(C), float(NX * C - 1), ALU.mult, ALU.add)
                dve.tensor_scalar(under, pos, float(C), None, ALU.is_le)
                step(dve.tensor_scalar(rowf, pos, float(C), None, ALU.min), j, 16)
                dve.scalar_tensor_tensor(out=kept, in0=pos, scalar=0.0, in1=under, op0=ALU.is_gt, op1=ALU.mult)
                step(dve.tensor_tensor(rowf, rowf, base, ALU.add), j, 17)
                dve.tensor_tensor(y_scale[:, bass.ds(j * TG, TG)], prb, kept, ALU.mult)
                dve.tensor_scalar(gather_row[:, bass.ds(j * TG, TG)], rowf, 0.0, None, ALU.max)
                dve.tensor_copy(hn[:, h, :, D], node1[:, bass.ds(j * TG, TG)])
                dve.tensor_copy(hn[:, h, :, D + 1], prb)
                dve.scalar_tensor_tensor(out=alone[:, bass.ds(j * TG, TG)], in0=kept, scalar=float(NOWHERE), in1=node0[:, bass.ds(j * TG, TG)],
                                         op0=ALU.mult, op1=ALU.add)
                step(dve.tensor_tensor(k2, rowf, buf_dump[:, h * TG:(h + 1) * TG], ALU.subtract), j, 18)
                step(dve.tensor_tensor(sidx, k2, kept, ALU.mult), j, 19)
                dve.tensor_tensor(scat_i[:, h, 0:TG], sidx, buf_dump[:, h * TG:(h + 1) * TG], ALU.add).then_inc(slot_made, 1)
                step(dve.tensor_tensor(seen, seen, new8, ALU.add), j, 20)
                step(dve.tensor_copy(seenb, seen), j, 21)

            def add_x(j, h, fills, first, next_sums):
                dve.wait_ge(xb_made, j + 1)
                if fills is not None:
                    dve.wait_ge(x1_out[h], 16 * fills)
                if next_sums:
                    sum_half(0, j + 2)
                for t in range(TG + 1):
                    if t < TG:
                        dve.wait_ge(w_made, TG * j + min(TG, t - t % 2 + 2))
                        dve.tensor_tensor(x1[:, h, t, :], bank(t // 2, (t % 2) * D, (t % 2 + 1) * D), x_in[:, h, t, :], ALU.add).then_inc(x1_made, 1)
                    if t >= 1:
                        dve.wait_ge(x1_made, TG * j + t)
                        last = dve.bn_stats(st3[:, t - 1, :], x1[:, h, t - 1, :])
                    if next_sums and t < TG:
                        if t + 1 < TG:
                            sum_half(t + 1, j + 2)
                        sum_rest(j + 1, t)
                    if t == TG - 2 and not first:
                        route_logits(j - 1)
                last.then_inc(stat_made, 1)
                dve.wait_ge(stat_made, j + 1)
                dve.sem_inc(dve_passed, 1)
                for t in range(TG):
                    last = dve.bn_aggr(mv3[:, t, :], st3[:, t, :])
                last.then_inc(mv_made, 1)

            def norm_factors(j):
                dve.wait_ge(std_made, j + 1)
                dve.reciprocal(rstd3, std3).then_inc(rstd_made, 1)
                dve.wait_ge(rstd_made, j + 1)
                dve.scalar_tensor_tensor(out=shift3, in0=mv3[:, :, 0], scalar=-1.0, in1=rstd3, op0=ALU.mult, op1=ALU.mult).then_inc(shift_made, 1)

            def node_group(j, h, fills, last_group):
                add_x(j, h, fills, False, not last_group)
                route_choice(j - 1)
                norm_factors(j)
                route_rows(j - 1, 1 - h)

            def split_weights(e, s, b):
                if b < 2:
                    dve.wait_ge(w1_in, 16 * (e + 1))
                    n = KD // 2
                    whole, hi, lo = (t[:, b * n:(b + 1) * n, :] for t in (w1_in_sb, w1_hi[:, s, :, :], w1_lo[:, s, :, :]))
                else:
                    dve.wait_ge(w2_in, 16 * (e + 1))
                    n = KF // 2
                    whole, hi, lo = (t[:, (b - 2) * n:(b - 1) * n, :] for t in (w2_in_sb, w2_hi[:, s, :, :], w2_lo[:, s, :, :]))
                dve.tensor_copy(hi, whole).then_inc(w_hi_made, 1)
                dve.wait_ge(w_hi_made, XB * e + b + 1)
                dve.tensor_tensor(lo, whole, hi.bitcast(F32), ALU.subtract).then_inc(w_split, 1)

            for t in range(TG):
                sum_half(t, 1)
                if t >= 1:
                    sum_rest(0, t - 1)
            sum_rest(0, TG - 1)
            add_x(0, 0, None, True, True)
            norm_factors(0)
            add_x(1, 1, None, False, True)
            route_choice(0)
            norm_factors(1)
            route_rows(0, 0)
            with dve.Fori(1, NG // 2 - 1) as i:
                for h in range(2):
                    node_group(2 * i + h, h, i, False)
            for h in range(2):
                node_group(NG - 2 + h, h, NG // 2 - 1, h == 1)
            route_logits(NG - 1)
            route_choice(NG - 1)
            route_rows(NG - 1, 1)
            for b in range(XB):
                split_weights(0, 0, b)

            dve.memset(zero_sum[:, :], 0.0).then_inc(check_step, 1)
            dve.wait_ge(check_step, 1)

            def check(v, junk, w, k):
                dve.tensor_scalar(junk, v, 0.0, None, ALU.mult, ALU.add, accum_out=zero_part[0:w, :]).then_inc(check_step, 1)
                dve.wait_ge(check_step, k + 1)
                dve.tensor_tensor(zero_sum[0:w, :], zero_sum[0:w, :], zero_part[0:w, :], ALU.add).then_inc(check_step, 1)
                dve.wait_ge(check_step, k + 2)

            def split_tokens(n, first):
                dve.wait_ge(tok_copied, n + 1)
                if not first:
                    dve.wait_ge(m1_made, KF * n)
                dve.tensor_copy(tok_hi[:, :, :], tokT).then_inc(tok_hi_made, 1)
                dve.wait_ge(tok_hi_made, n + 1)
                dve.tensor_tensor(tok_lo[:, :, :], tokT, tok_hi[:, :, :].bitcast(F32), ALU.subtract).then_inc(tok_split, 1)

            def note_tokens(n, s):
                dve.tensor_scalar(meta, tok[:, s, :, D], 0.0, float(NOWHERE), ALU.is_equal, ALU.mult).then_inc(meta_step, 1)
                dve.tensor_copy(meta_w[:, s, :], tok[:, s, :, D + 1])
                dve.wait_ge(meta_step, n + 1)
                dve.scalar_tensor_tensor(out=meta_i[:, s, :], in0=meta, scalar=-1.0, in1=tok[:, s, :, D], op0=ALU.add, op1=ALU.add).then_inc(meta_made, 1)

            def expert_sum(e, b, s_e, first, last_expert):
                n = e * XB + b
                s = b % 2
                cols = min(TB * P, C - b * TB * P)
                for m in range(KF):
                    dve.wait_ge(hid_made, KF * n + m + 1)
                    if m == 0 and not (first and b == 0):
                        dve.wait_ge(m2_made, 2 * n)
                    dve.tensor_copy(hid_hi[:, m, 0:cols], hid[:, m % 2, 0:cols]).then_inc(hid_hi_made, 1)
                    dve.wait_ge(hid_hi_made, KF * n + m + 1)
                    dve.tensor_tensor(hid_lo[:, m, 0:cols], hid[:, m % 2, 0:cols], hid_hi[:, m, 0:cols].bitcast(F32), ALU.subtract).then_inc(hid_split, 1)
                split_tokens(n + 1, False)
                if not (first and b == 0):
                    turns = e * (XB // 2) + (b + 1) // 2
                    dve.wait_ge(o_out[1 - s], 16 * TB * turns)
                note_tokens(n + 1, 1 - s)
                if not (first and b < 2):
                    dve.wait_ge(y_out[s], 32 * (e * (XB // 2) + b // 2))
                for t in range(0, TB, 2):
                    dve.wait_ge(m2_made, 2 * n + t // 2 + 1)
                    for u in range(t, t + 2):
                        w = min(P, C - (b * TB + u) * P)
                        last = dve.tensor_tensor(y_sb[0:w, s, u, :], bank(6 + t // 2, (u - t) * D, (u - t + 1) * D)[0:w, :],
                                                 b2_t[0:w, bass.ds(e, 1), :].rearrange("p a d -> p (a d)"), ALU.add)
                    last.then_inc(y_made, 1)
                    dve.wait_ge(y_made, 2 * n + t // 2 + 1)
                    for u in range(t, t + 2):
                        w = min(P, C - (b * TB + u) * P)
                        check(y_sb[0:w, s, u, :], y_zero[0:w, :], w, 1 + 2 * (TB * n + u))
                    if t == 0:
                        dve.wait_ge(o_in[s], 16 * TB * (e * (XB // 2) + b // 2 + 1))
                    for u in range(t, t + 2):
                        w = min(P, C - (b * TB + u) * P)
                        last = dve.scalar_tensor_tensor(out=o_sb[0:w, s, u, :], in0=y_sb[0:w, s, u, :], scalar=meta_w[0:w, s, u:u + 1],
                                                        in1=o_sb[0:w, s, u, :], op0=ALU.mult, op1=ALU.add)
                    if t == TB - 2:
                        last.then_inc(o_made, 1)
                    if t == 0 and not last_expert:
                        if b == 0 and not first:
                            dve.wait_ge(m2_made, 2 * XB * e)
                        split_weights(e + 1, 1 - s_e, b)

            for s in range(2):
                dve.wait_ge(x1_out[s], 16 * (NG // 2))
                dve.wait_ge(h_out[s], 16 * TG * (NG // 2))
            dve.memset(o_sb[:, :, :, :], 0.0).then_inc(o_clear, 1)
            split_tokens(0, True)
            note_tokens(0, 0)

            def expert_blocks(e, s_e, first, last_expert):
                for b in range(XB):
                    expert_sum(e, b, s_e, first, last_expert)

            expert_blocks(0, 0, True, False)
            expert_blocks(1, 1, False, False)
            with dve.Fori(1, NX // 2 - 1) as i:
                for s_e in range(2):
                    expert_blocks(2 * i + s_e, s_e, False, False)
            expert_blocks(NX - 2, 0, False, False)
            expert_blocks(NX - 1, 1, False, True)
            k = 1 + 2 * TB * NX * XB
            check(y_scale[:, :], y_zero[:, 0:NT], P, k)
            dve.tensor_scalar(zero_part[:, :], zero_sum[:, :], 0.0, None, ALU.is_equal).then_inc(check_step, 1)
            dve.wait_ge(fine_sum, 1)
            dve.tensor_copy(fine_i[:, :], bank(0, 0, 1)).then_inc(check_step, 1)
            dve.wait_ge(check_step, k + 4)

            fine = dve.value_load(fine_i[0:1, 0:1], min_val=0, max_val=P)
            with dve.If(fine < P):
                dve.wait_ge(y_in_dram, 1)
                dve.memset(big4, 10000.0).then_inc(lim_made, 1)
                dve.memset(neg4, -10000.0).then_inc(lim_made, 1)
                dve.wait_ge(lim_made, 2)

                def add_any(j, h, fills, first):
                    f0 = NP_FIN * j
                    dve.wait_ge(yg_in[h], 16 * TG * fills)
                    if not first:
                        dve.wait_ge(fin_out[h], 32 * (fills - 1))
                    for t in range(TG):
                        sc = y_scale[:, bass.ds(j * TG + t, 1)]
                        dve.tensor_scalar(yp[:, h, t, :], yg[:, h, t, :], sc, 0.0, ALU.mult, ALU.max)
                        last = dve.tensor_scalar(yn[:, h, t, :], yg[:, h, t, :], sc, 0.0, ALU.mult, ALU.min)
                    last.then_inc(fin_step, 1)
                    dve.wait_ge(fin_step, f0 + 1)
                    flat_p = yp[:, h, :, :].rearrange("p a b -> p (a b)")
                    flat_n = yn[:, h, :, :].rearrange("p a b -> p (a b)")
                    flat_m = over.rearrange("p a b -> p (a b)")
                    dve.tensor_scalar(flat_m, flat_p, HUGE, None, ALU.is_gt).then_inc(fin_step, 1)
                    dve.wait_ge(fin_step, f0 + 2)
                    dve.sem_inc(dve_passed, 1)
                    dve.copy_predicated(flat_p, flat_m, big4).then_inc(fin_step, 1)
                    dve.wait_ge(fin_step, f0 + 3)
                    dve.tensor_scalar(flat_m, flat_n, -HUGE, None, ALU.is_lt).then_inc(fin_step, 1)
                    dve.wait_ge(fin_step, f0 + 4)
                    dve.sem_inc(dve_passed, 1)
                    dve.copy_predicated(flat_n, flat_m, neg4).then_inc(fin_step, 1)
                    dve.wait_ge(fin_step, f0 + 5)
                    dve.tensor_tensor(flat_p, flat_p, flat_n, ALU.add).then_inc(fin_step, 1)
                    dve.wait_ge(fin_step, f0 + 6)
                    dve.wait_ge(x1_in[h], 16 * fills)
                    dve.tensor_tensor(flat_p, flat_p, x1b[:, h, :, :].rearrange("p a b -> p (a b)"), ALU.add).then_inc(fin_made, 1)

                for h in range(2):
                    add_any(h, h, 1, True)
                with dve.Fori(1, NG // 2) as i:
                    for h in range(2):
                        add_any(2 * i + h, h, i + 1, False)


_INS = ['x', 'src', 'dst', 'edge_weight', 'L0_gnn_weight', 'L0_gnn_learnable_diag', 'L0_gnn_bias',
        'L0_ffn_gate_w', 'L0_ffn_gate_b', 'L0_ffn_w1', 'L0_ffn_b1', 'L0_ffn_w2', 'L0_ffn_b2']
_OUTS = [((12500, 256), 'float32')]


def kernel(**inputs):
    import numpy as _np
    import concourse.bacc as _bacc
    from concourse import mybir as _mybir
    from concourse.bass_utils import run_bass_kernel_spmd as _run

    nc = _bacc.Bacc("TRN2", target_bir_lowering=False, num_devices=1)
    arrays, args = {}, []
    for name in _INS:
        a = _np.ascontiguousarray(inputs[name])
        arrays[f"in_{name}_dram"] = a
        args.append(nc.dram_tensor(f"in_{name}_dram", a.shape, _mybir.dt.from_np(a.dtype), kind="ExternalInput").ap())
    for i, (shape, dtype) in enumerate(_OUTS):
        dt = _mybir.dt.from_np(_np.dtype(dtype))
        args.append(nc.dram_tensor(f"out_{i}_dram", shape, dt, kind="ExternalOutput").ap())
    gnn_moe_layer(nc, *args)
    r = _run(nc, [arrays], core_ids=[0])
    got = tuple(r.results[0][f"out_{i}_dram"] for i in range(len(_OUTS)))
    return got[0]
```
